# Optimizing a Trainium2 kernel written in Bass

```python
import numpy as np
import jax
import jax.numpy as jnp

def _softmax(x, axis=-1):
    return jax.nn.softmax(x, axis=axis)

def _gelu(x):
    return jax.nn.gelu(x, approximate=True)

def _silu(x):
    return jax.nn.silu(x)

def _sigmoid(x):
    return jax.nn.sigmoid(x)

def _layernorm(x, axis=-1, eps=1e-05):
    m = jnp.mean(x, axis=axis, keepdims=True)
    v = jnp.var(x, axis=axis, keepdims=True)
    return (x - m) / jnp.sqrt(v + eps)

def _scatter_add(tgt, idx, src, axis=0):
    return tgt.at[idx].add(src)

def _segment_sum(src, seg, n):
    return jax.ops.segment_sum(src, seg, n)
kernel_name = 'mk_gnn_ffn_d2_gnn_r32_d94328'

def setup_inputs(seed: int=0):
    np.random.seed(seed)
    _w = jnp.asarray

    def _rec_inputs():
        import jax
        import jax.numpy as jnp
        _gk = jax.random.key(seed)
        x = -8.776e-05 + 1 * jax.random.normal(jax.random.fold_in(_gk, 1), (3125, 256), jnp.float32)
        _s = jax.random.randint(jax.random.fold_in(_gk, 2), (25000,), 0, 3125, jnp.int32)
        _d = jax.random.randint(jax.random.fold_in(_gk, 3), (25000,), 0, 3125, jnp.int32)
        _loop = jnp.arange(3125, dtype=jnp.int32)
        src = jnp.concatenate([_s, _d, _loop])
        dst = jnp.concatenate([_d, _s, _loop])
        _o = jnp.argsort(dst, stable=True)
        src = src[_o]
        dst = dst[_o]
        edge_attr_64 = 0.000279952 + 1.00013 * jax.random.normal(jax.random.fold_in(_gk, 11), (53125, 64), jnp.float32)
        return (x, src, dst, edge_attr_64)
    x, src, dst, edge_attr_64 = _rec_inputs()

    def _L0_gnn_setup():
        import jax, jax.numpy as jnp
        import numpy as np
        N, E, H, ED = (625, 10000, 256, 64)
        key = jax.random.key(seed)
        ks = jax.random.split(key, 12)

        def init_w(k, shape, fan_in):
            return (jax.random.normal(k, shape, jnp.float32) / np.sqrt(fan_in)).astype(jnp.float32)
        h = jax.random.normal(ks[0], (N, H), jnp.float32)
        edge_indices = jax.random.randint(ks[1], (2, E), 0, N, jnp.int32)
        edge_attr = jax.random.normal(ks[2], (E, ED), jnp.float32)
        din = 2 * H + ED
        W1 = init_w(ks[3], (H, din), din)
        b1 = jnp.zeros((H,), jnp.float32)
        W2 = init_w(ks[4], (H, H), H)
        b2 = jnp.zeros((H,), jnp.float32)
        W_ih = init_w(ks[5], (3 * H, H), H)
        b_ih = jnp.zeros((3 * H,), jnp.float32)
        W_hh = init_w(ks[6], (3 * H, H), H)
        b_hh = jnp.zeros((3 * H,), jnp.float32)
        return {'h': h, 'edge_indices': edge_indices, 'edge_attr': edge_attr, 'W1': W1, 'b1': b1, 'W2': W2, 'b2': b2, 'W_ih': W_ih, 'b_ih': b_ih, 'W_hh': W_hh, 'b_hh': b_hh}
    _L0_gnn_all = _L0_gnn_setup()
    _L0_gnn_in = {k: v for k, v in _L0_gnn_all.items() if k in ('W1', 'b1', 'W2', 'b2', 'W_ih', 'b_ih', 'W_hh', 'b_hh')}
    del _L0_gnn_all

    def _L0_ffn_setup():
        import jax, jax.numpy as jnp
        import numpy as np
        TOP_K = 2
        LN_EPS = 1e-05
        key = jax.random.key(seed)
        ks = jax.random.split(key, 8)
        B, S, D, E, H = (16, 1024, 256, 8, 1024)
        x = jax.random.normal(ks[0], (B, S, D), dtype=jnp.float32)
        Wr = jax.random.normal(ks[1], (D, E), dtype=jnp.float32) * 0.1
        br = jnp.zeros((E,), dtype=jnp.float32)
        ln_g = jnp.ones((E, D), dtype=jnp.float32)
        ln_b = jnp.zeros((E, D), dtype=jnp.float32)
        W1 = jax.random.normal(ks[2], (E, D, H), dtype=jnp.float32) * (1.0 / np.sqrt(D))
        b1 = jnp.zeros((E, H), dtype=jnp.float32)
        W2 = jax.random.normal(ks[3], (E, H, D), dtype=jnp.float32) * (1.0 / np.sqrt(H))
        b2 = jnp.zeros((E, D), dtype=jnp.float32)
        return {'x': x, 'Wr': Wr, 'br': br, 'ln_g': ln_g, 'ln_b': ln_b, 'W1': W1, 'b1': b1, 'W2': W2, 'b2': b2}
    _L0_ffn_all = _L0_ffn_setup()
    _L0_ffn_in = {k: v for k, v in _L0_ffn_all.items() if k in ('Wr', 'br', 'ln_g', 'ln_b', 'W1', 'b1', 'W2', 'b2')}
    del _L0_ffn_all

    def _L1_gnn_setup():
        import jax, jax.numpy as jnp
        import numpy as np
        N_NODES = 10000
        N_EDGES = 10000
        DIM = 256
        key = jax.random.key(seed)
        k = jax.random.split(key, 6)
        scale = 1.0 / np.sqrt(DIM)
        x = jax.random.normal(k[0], (N_NODES, DIM), dtype=jnp.float32)
        W = jax.random.normal(k[1], (DIM, DIM), dtype=jnp.float32) * scale
        a_src = jax.random.normal(k[2], (DIM,), dtype=jnp.float32) * scale
        a_dst = jax.random.normal(k[3], (DIM,), dtype=jnp.float32) * scale
        bias = jnp.zeros((DIM,), dtype=jnp.float32)
        edge_index = jax.random.randint(k[4], (2, N_EDGES), 0, N_NODES, dtype=jnp.int64)
        return {'x': x, 'W': W, 'a_src': a_src, 'a_dst': a_dst, 'bias': bias, 'edge_index': edge_index}
    _L1_gnn_all = _L1_gnn_setup()
    _L1_gnn_in = {k: v for k, v in _L1_gnn_all.items() if k in ('W', 'a_src', 'a_dst', 'bias')}
    del _L1_gnn_all

    def _L1_ffn_setup():
        import jax, jax.numpy as jnp
        import numpy as np
        B, A = (128, 8)
        IN, OUT = (256, 256)
        SH1, SH2 = (256, 128)
        EH1, EH2 = (128, 64)
        E, TOPK = (4, 2)

        def _shared_mlp(x, W1, b1, W2, b2, W3, b3):
            h = jax.nn.relu(x @ W1 + b1)
            h = jax.nn.relu(h @ W2 + b2)
            return h @ W3 + b3

        def _experts_mlp(x, eW1, eb1, eW2, eb2, eW3, eb3):
            h = jax.nn.relu(jnp.einsum('baf,efh->ebah', x, eW1) + eb1[:, None, None, :])
            h = jax.nn.relu(jnp.einsum('ebah,ehg->ebag', h, eW2) + eb2[:, None, None, :])
            o = jnp.einsum('ebag,ego->ebao', h, eW3) + eb3[:, None, None, :]
            return jnp.moveaxis(o, 0, -1)
        key = jax.random.key(seed)
        ks = jax.random.split(key, 16)
        s = 0.05
        return {'x': jax.random.normal(ks[0], (B, A, IN), jnp.float32), 'sW1': jax.random.normal(ks[1], (IN, SH1), jnp.float32) * s, 'sb1': jnp.zeros((SH1,), jnp.float32), 'sW2': jax.random.normal(ks[2], (SH1, SH2), jnp.float32) * s, 'sb2': jnp.zeros((SH2,), jnp.float32), 'sW3': jax.random.normal(ks[3], (SH2, OUT), jnp.float32) * s, 'sb3': jnp.zeros((OUT,), jnp.float32), 'eW1': jax.random.normal(ks[4], (E, IN, EH1), jnp.float32) * s, 'eb1': jnp.zeros((E, EH1), jnp.float32), 'eW2': jax.random.normal(ks[5], (E, EH1, EH2), jnp.float32) * s, 'eb2': jnp.zeros((E, EH2), jnp.float32), 'eW3': jax.random.normal(ks[6], (E, EH2, OUT), jnp.float32) * s, 'eb3': jnp.zeros((E, OUT), jnp.float32), 'gW': jax.random.normal(ks[7], (IN, E), jnp.float32) * s, 'gb': jnp.zeros((E,), jnp.float32)}
    _L1_ffn_all = _L1_ffn_setup()
    _L1_ffn_in = {k: v for k, v in _L1_ffn_all.items() if k in ('sW1', 'sb1', 'sW2', 'sb2', 'sW3', 'sb3', 'eW1', 'eb1', 'eW2', 'eb2', 'eW3', 'eb3', 'gW', 'gb')}
    del _L1_ffn_all
    return {'x': x, 'src': src, 'dst': dst, 'edge_attr_64': edge_attr_64, 'L0_gnn_W1': _L0_gnn_in['W1'], 'L0_gnn_b1': _L0_gnn_in['b1'], 'L0_gnn_W2': _L0_gnn_in['W2'], 'L0_gnn_b2': _L0_gnn_in['b2'], 'L0_gnn_W_ih': _L0_gnn_in['W_ih'], 'L0_gnn_b_ih': _L0_gnn_in['b_ih'], 'L0_gnn_W_hh': _L0_gnn_in['W_hh'], 'L0_gnn_b_hh': _L0_gnn_in['b_hh'], 'L0_ffn_Wr': _L0_ffn_in['Wr'], 'L0_ffn_br': _L0_ffn_in['br'], 'L0_ffn_ln_g': _L0_ffn_in['ln_g'], 'L0_ffn_ln_b': _L0_ffn_in['ln_b'], 'L0_ffn_W1': _L0_ffn_in['W1'], 'L0_ffn_b1': _L0_ffn_in['b1'], 'L0_ffn_W2': _L0_ffn_in['W2'], 'L0_ffn_b2': _L0_ffn_in['b2'], 'L1_gnn_W': _L1_gnn_in['W'], 'L1_gnn_a_src': _L1_gnn_in['a_src'], 'L1_gnn_a_dst': _L1_gnn_in['a_dst'], 'L1_gnn_bias': _L1_gnn_in['bias'], 'L1_ffn_sW1': _L1_ffn_in['sW1'], 'L1_ffn_sb1': _L1_ffn_in['sb1'], 'L1_ffn_sW2': _L1_ffn_in['sW2'], 'L1_ffn_sb2': _L1_ffn_in['sb2'], 'L1_ffn_sW3': _L1_ffn_in['sW3'], 'L1_ffn_sb3': _L1_ffn_in['sb3'], 'L1_ffn_eW1': _L1_ffn_in['eW1'], 'L1_ffn_eb1': _L1_ffn_in['eb1'], 'L1_ffn_eW2': _L1_ffn_in['eW2'], 'L1_ffn_eb2': _L1_ffn_in['eb2'], 'L1_ffn_eW3': _L1_ffn_in['eW3'], 'L1_ffn_eb3': _L1_ffn_in['eb3'], 'L1_ffn_gW': _L1_ffn_in['gW'], 'L1_ffn_gb': _L1_ffn_in['gb']}

def reference(x, src, dst, edge_attr_64, L0_gnn_W1, L0_gnn_b1, L0_gnn_W2, L0_gnn_b2, L0_gnn_W_ih, L0_gnn_b_ih, L0_gnn_W_hh, L0_gnn_b_hh, L0_ffn_Wr, L0_ffn_br, L0_ffn_ln_g, L0_ffn_ln_b, L0_ffn_W1, L0_ffn_b1, L0_ffn_W2, L0_ffn_b2, L1_gnn_W, L1_gnn_a_src, L1_gnn_a_dst, L1_gnn_bias, L1_ffn_sW1, L1_ffn_sb1, L1_ffn_sW2, L1_ffn_sb2, L1_ffn_sW3, L1_ffn_sb3, L1_ffn_eW1, L1_ffn_eb1, L1_ffn_eW2, L1_ffn_eb2, L1_ffn_eW3, L1_ffn_eb3, L1_ffn_gW, L1_ffn_gb):
    import jax
    import jax.numpy as jnp

    def _L0_gnn_ref(h, edge_indices, edge_attr, W1, b1, W2, b2, W_ih, b_ih, W_hh, b_hh):
        import jax, jax.numpy as jnp
        import numpy as np
        N, E, H, ED = (625, 10000, 256, 64)
        row, col = (edge_indices[0], edge_indices[1])
        edge_in = jnp.concatenate([h[row], h[col], edge_attr], axis=-1)
        msg = jax.nn.relu(edge_in @ W1.T + b1) @ W2.T + b2
        agg = jax.ops.segment_sum(msg, row, num_segments=h.shape[0])
        gx = agg @ W_ih.T + b_ih
        gh = h @ W_hh.T + b_hh
        xr, xz, xn = jnp.split(gx, 3, axis=-1)
        hr, hz, hn = jnp.split(gh, 3, axis=-1)
        r = jax.nn.sigmoid(xr + hr)
        z = jax.nn.sigmoid(xz + hz)
        n = jnp.tanh(xn + r * hn)
        h_new = (1.0 - z) * n + z * h
        return h_new

    def _L0_ffn_ref(x, Wr, br, ln_g, ln_b, W1, b1, W2, b2):
        import jax, jax.numpy as jnp
        import numpy as np
        TOP_K = 2
        LN_EPS = 1e-05
        B, S, D = x.shape
        N = B * S
        xt = x.reshape(N, D)
        logits = xt @ Wr + br
        probs = jax.nn.softmax(logits, axis=-1)
        top_p, top_idx = jax.lax.top_k(probs, TOP_K)
        weights = top_p / top_p.sum(axis=-1, keepdims=True)
        mu = xt.mean(axis=-1, keepdims=True)
        var = ((xt - mu) ** 2).mean(axis=-1, keepdims=True)
        xn = (xt - mu) * jax.lax.rsqrt(var + LN_EPS)
        xe = xn[None, :, :] * ln_g[:, None, :] + ln_b[:, None, :]
        h = jax.nn.gelu(jnp.einsum('end,edh->enh', xe, W1) + b1[:, None, :], approximate=False)
        y = jnp.einsum('enh,ehd->end', h, W2) + b2[:, None, :]
        y_tok = jnp.transpose(y, (1, 0, 2))
        sel = jnp.take_along_axis(y_tok, top_idx[:, :, None], axis=1)
        out = (weights[:, :, None] * sel).sum(axis=1)
        return out.reshape(B, S, D)

    def _L1_gnn_ref(x, W, a_src, a_dst, bias, edge_index):
        import jax, jax.numpy as jnp
        import numpy as np
        N_NODES = 10000
        N_EDGES = 10000
        DIM = 256
        N, D = x.shape
        loop = jnp.arange(N, dtype=edge_index.dtype)
        src = jnp.concatenate([edge_index[0], loop])
        dst = jnp.concatenate([edge_index[1], loop])
        h = x @ W.T
        alpha_s = h @ a_src
        alpha_d = h @ a_dst
        e = jax.nn.leaky_relu(alpha_s[src] + alpha_d[dst], negative_slope=0.2)
        m = jax.ops.segment_max(e, dst, num_segments=N)
        p = jnp.exp(e - m[dst])
        s = jax.ops.segment_sum(p, dst, num_segments=N)
        alpha = p / s[dst]
        out = jax.ops.segment_sum(h[src] * alpha[:, None], dst, num_segments=N)
        out = out + bias
        out = jax.nn.relu(out)
        return x + out

    def _L1_ffn_ref(x, sW1, sb1, sW2, sb2, sW3, sb3, eW1, eb1, eW2, eb2, eW3, eb3, gW, gb):
        import jax, jax.numpy as jnp
        import numpy as np
        B, A = (128, 8)
        IN, OUT = (256, 256)
        SH1, SH2 = (256, 128)
        EH1, EH2 = (128, 64)
        E, TOPK = (4, 2)

        def _shared_mlp(x, W1, b1, W2, b2, W3, b3):
            h = jax.nn.relu(x @ W1 + b1)
            h = jax.nn.relu(h @ W2 + b2)
            return h @ W3 + b3

        def _experts_mlp(x, eW1, eb1, eW2, eb2, eW3, eb3):
            h = jax.nn.relu(jnp.einsum('baf,efh->ebah', x, eW1) + eb1[:, None, None, :])
            h = jax.nn.relu(jnp.einsum('ebah,ehg->ebag', h, eW2) + eb2[:, None, None, :])
            o = jnp.einsum('ebag,ego->ebao', h, eW3) + eb3[:, None, None, :]
            return jnp.moveaxis(o, 0, -1)
        all_out = _experts_mlp(x, eW1, eb1, eW2, eb2, eW3, eb3)
        shared = _shared_mlp(x, sW1, sb1, sW2, sb2, sW3, sb3)
        gates = jax.nn.softmax(x @ gW + gb, axis=-1)
        topv, topi = jax.lax.top_k(gates, TOPK)
        topw = jax.nn.softmax(topv, axis=-1)
        sel = jnp.take_along_axis(all_out, topi[:, :, None, :], axis=-1)
        gated = jnp.sum(sel * topw[:, :, None, :], axis=-1)
        return shared + gated
    edge_index = jnp.stack([src, dst])
    x = x + _L0_gnn_ref(_layernorm(x, axis=-1), edge_index, edge_attr_64, L0_gnn_W1, L0_gnn_b1, L0_gnn_W2, L0_gnn_b2, L0_gnn_W_ih, L0_gnn_b_ih, L0_gnn_W_hh, L0_gnn_b_hh)
    x = x + _L0_ffn_ref(_layernorm(x, axis=-1)[None], L0_ffn_Wr, L0_ffn_br, L0_ffn_ln_g, L0_ffn_ln_b, L0_ffn_W1, L0_ffn_b1, L0_ffn_W2, L0_ffn_b2)[0]
    x = x + _L1_gnn_ref(_layernorm(x, axis=-1), L1_gnn_W, L1_gnn_a_src, L1_gnn_a_dst, L1_gnn_bias, edge_index)
    x = x + _L1_ffn_ref(_layernorm(x, axis=-1)[None], L1_ffn_sW1, L1_ffn_sb1, L1_ffn_sW2, L1_ffn_sb2, L1_ffn_sW3, L1_ffn_sb3, L1_ffn_eW1, L1_ffn_eb1, L1_ffn_eW2, L1_ffn_eb2, L1_ffn_eW3, L1_ffn_eb3, L1_ffn_gW, L1_ffn_gb)[0]
    return x

_drawn_inputs = setup_inputs


def setup_inputs(seed=0):
    import zlib

    import numpy as np

    out = dict(_drawn_inputs(seed))
    spreads = {'L0_gnn_b1': (0.0, 0.1),
     'L0_gnn_b2': (0.0, 0.1),
     'L0_gnn_b_ih': (0.0, 0.292),
     'L0_gnn_b_hh': (0.0, 0.379),
     'L0_ffn_br': (0.0, 0.1),
     'L0_ffn_ln_g': (1.0, 0.2),
     'L0_ffn_ln_b': (0.0, 0.1),
     'L0_ffn_b1': (0.0, 0.1),
     'L0_ffn_b2': (0.0, 0.1),
     'L1_gnn_bias': (0.0, 0.317),
     'L1_ffn_sb1': (0.0, 0.8),
     'L1_ffn_sb2': (0.0, 0.589),
     'L1_ffn_sb3': (0.0, 0.1),
     'L1_ffn_eb1': (0.0, 0.8),
     'L1_ffn_eb2': (0.0, 0.8),
     'L1_ffn_eb3': (0.0, 0.321),
     'L1_ffn_gb': (0.0, 0.8)}
    factors = {'L1_gnn_a_dst': 3.495, 'L1_ffn_eW1': 3.496, 'L1_ffn_eW2': 3.07}
    for name, (base, spread) in spreads.items():
        noise = np.random.default_rng([zlib.crc32(name.encode()), seed]).standard_normal(out[name].shape)
        drawn = base * np.exp(spread * noise) if base else spread * noise
        out[name] = jnp.asarray(drawn.astype(out[name].dtype))
    for name, factor in factors.items():
        out[name] = (out[name] * factor).astype(out[name].dtype)
    return out
```

```python
from contextlib import ExitStack

import concourse.bass as bass
from concourse import mybir

F32 = mybir.dt.float32
BF16 = mybir.dt.bfloat16
I32 = mybir.dt.int32
U32 = mybir.dt.uint32
ALU = mybir.AluOpType
ACT = mybir.ActivationFunctionType
AX_X = mybir.AxisListType.X

N, D = 3125, 256
E = 53125
EA = 64
T = 125
NT = N // T
EC = E // T
B = 128
G = 5
REC = EA + 2
EB = (E + (B - 1) * NT) // B
EB += -EB % 4
NEX, HID = 8, 1024
TOK2 = 2 * NT
MB = (2 * N + (B - 1) * NEX) // B
MB += MB % 2
EPS = 1e-5
BIG = 1e30
HC = D + 2


def pipelined(eng, n, stages, U=2):
    most = max(lag for lag, _ in stages)
    first, end = (most + 2 * U - 1) // U, n // U

    def peeled(s):
        for lag, fn in stages:
            if 0 <= s - lag < n:
                fn((s - lag) // U, (s - lag) % U)

    if end - first < 2:
        for s in range(n + most):
            peeled(s)
        return
    for s in range(U * first):
        peeled(s)
    with eng.Fori(first, end) as k:
        for par in range(U):
            for lag, fn in stages:
                fn(k + (par - lag) // U, (par - lag) % U)
    for s in range(U * end, n + most):
        peeled(s)


def after(eng, sem, count):
    if not isinstance(count, int) or count > 0:
        eng.wait_ge(sem, count)


def held(eng, *values):
    return [v if isinstance(v, int) else eng.snap(v) for v in values]


class Pool_:

    def __init__(self, nc, ctx):
        self.nc, self.ctx, self.sems = nc, ctx, []

    def sb(self, name, shape, dt=F32):
        return self.ctx.enter_context(self.nc.sbuf_tensor("sb_" + name, shape, dt))

    def ps(self, name, shape, dt=F32):
        return self.ctx.enter_context(self.nc.psum_tensor("ps_" + name, shape, dt))

    def sem(self, name):
        self.sems.append(self.ctx.enter_context(self.nc.semaphore(name)))
        return self.sems[-1]

    def block(self):
        def clear():
            for s in self.sems:
                self.nc.gpsimd.sem_clear(s)
        self.ctx.callback(clear)
        return self.ctx.enter_context(self.nc.Block())


def chained(eng, sem):
    count = [0]

    def link(ins):
        count[0] += 1
        ins.then_inc(sem, 1)
        eng.wait_ge(sem, count[0])
    return link


def setup_phase(nc, m):
    with ExitStack() as ctx:
        a = Pool_(nc, ctx)
        ramp_i = a.sb("ramp_i", [B, B], I32)
        part_i = a.sb("part_i", [B, 4], I32)
        ramped = a.sem("ramped")
        chain = a.sem("setup_chain")
        block = a.block()

        @block.gpsimd
        def _(pool):
            nc.gpsimd.iota(ramp_i[:, :], pattern=[[1, B]], base=0, channel_multiplier=0).then_inc(ramped, 1)
            nc.gpsimd.iota(part_i[:, :], pattern=[[B, 4]], base=0, channel_multiplier=1).then_inc(ramped, 1)

        @block.vector
        def _(dve):
            link = chained(dve, chain)
            dve.wait_ge(ramped, 2)
            link(nc.vector.tensor_copy(m.ramp[:, :], ramp_i[:, :]))
            link(nc.vector.tensor_copy(m.part[:, :], part_i[:, :]))
            link(nc.vector.tensor_scalar(m.ident[:, :], m.ramp[:, :], m.part[:, 0:1], None, ALU.is_equal))
            link(nc.vector.tensor_scalar(m.upper[:, :], m.ramp[:, :], m.part[:, 0:1], None, ALU.is_gt))
            nc.vector.memset(m.ones[:, :], 1.0).then_inc(m.go, 1)


def dispatch(nc, m, name, key, C, J, width, blocks, pos_i, local, bucket_dram, bucket_row, extra=None):
    with ExitStack() as ctx:
        a = Pool_(nc, ctx)
        ge = a.sb(name + "ge", [T, J + 1, C], BF16)
        oh = a.sb(name + "oh", [T, J, C], BF16)
        scan = a.sb(name + "scan", [T, J, C])
        cum = a.sb(name + "cum", [T, J + 1])
        count = a.sb(name + "count", [T, J])
        base = a.sb(name + "base", [T, J])
        posf = a.sb(name + "posf", [T, C])
        total = a.sb(name + "total", [B, J])
        total_i = a.sb(name + "total_i", [B, J], I32)
        nblk = a.sb(name + "nblk", [B, J])
        end = a.sb(name + "end", [B, J])
        one = a.sb(name + "one", [B, J])
        past = a.sb(name + "past", [B, 4, J])
        bkt = a.sb(name + "bkt", [B, 4])
        bkt_i = a.sb(name + "bkt_i", [B, 4], I32)
        p_before = a.ps(name + "p_before", [T, 512])
        p_total = a.ps(name + "p_total", [B, 512])
        counted = a.sem(name + "counted")
        summed = a.sem(name + "summed")
        bucketed = a.sem(name + "bucketed")
        stored = a.sem(name + "stored")
        chain = a.sem(name + "chain")
        block = a.block()

        @block.vector
        def _(dve):
            link = chained(dve, chain)
            for j in range(J + 1):
                last = nc.vector.tensor_scalar(ge[:, j, :], key, float(width * j), None, ALU.is_ge)
            link(last)
            nc.vector.memset(one[:, :], 1.0)
            link(nc.vector.memset(cum[:, 0:1], 0.0))
            link(nc.vector.tensor_tensor(oh[:, :, :], ge[:, 0:J, :], ge[:, 1:J + 1, :], ALU.subtract))
            flat = "p j c -> p (j c)"
            if local is not None:
                link(nc.vector.tensor_reduce(posf[:, :], ge[:, 1:J, :].rearrange("p j c -> p c j"), AX_X, ALU.add))
                link(nc.vector.scalar_tensor_tensor(out=local, in0=posf[:, :], scalar=-float(width), in1=key,
                                                    op0=ALU.mult, op1=ALU.add))
            link(nc.vector.memset(ge[:, 0:J, :].rearrange(flat), 1.0))
            link(nc.vector.tensor_tensor_scan(scan[:, :, :].rearrange(flat), ge[:, 0:J, :].rearrange(flat),
                                              oh[:, :, :].rearrange(flat), 0.0, ALU.mult, ALU.add))
            link(nc.vector.tensor_copy(cum[:, 1:J + 1], scan[:, :, C - 1]))
            nc.vector.tensor_tensor(count[:, :], cum[:, 1:J + 1], cum[:, 0:J], ALU.subtract).then_inc(counted, 1)
            dve.wait_ge(summed, 1)
            link(nc.vector.tensor_scalar(total_i[:, :], p_total[:, 0:J], float(B - 1), None, ALU.add))
            link(nc.vector.tensor_scalar(total_i[:, :], total_i[:, :], B.bit_length() - 1, None,
                                         ALU.arith_shift_right))
            link(nc.vector.tensor_copy(nblk[:, :], total_i[:, :]))
            link(nc.vector.tensor_tensor_scan(end[:, :], one[:, :], nblk[:, :], 0.0, ALU.mult, ALU.add))
            for i in range(4):
                last = nc.vector.tensor_scalar(past[:, i, :], end[:, :], m.part[:, i:i + 1], None, ALU.is_le)
            link(last)
            link(nc.vector.tensor_reduce(bkt[:, :], past[:, :, :], AX_X, ALU.add))
            nc.vector.tensor_scalar(bkt_i[:, :], bkt[:, :], float(J - 1), None, ALU.min).then_inc(bucketed, 1)
            link(nc.vector.tensor_tensor(total[:, :], end[:, :], nblk[:, :], ALU.subtract))
            link(nc.vector.scalar_tensor_tensor(out=base[:, :], in0=total[0:T, :], scalar=float(B),
                                                in1=cum[:, 0:J], op0=ALU.mult, op1=ALU.subtract))
            link(nc.vector.scalar_tensor_tensor(out=base[:, :], in0=base[:, :], scalar=-1.0,
                                                in1=p_before[:, 0:J], op0=ALU.add, op1=ALU.add))
            for j in range(J):
                last = nc.vector.scalar_tensor_tensor(out=scan[:, j, :], in0=scan[:, j, :],
                                                      scalar=base[:, j:j + 1], in1=oh[:, j, :],
                                                      op0=ALU.add, op1=ALU.mult)
            link(last)
            link(nc.vector.tensor_reduce(posf[:, :], scan[:, :, :].rearrange("p j c -> p c j"), AX_X, ALU.add))
            link(nc.vector.tensor_copy(pos_i, posf[:, :]))

        @block.tensor
        def _(pe):
            pe.wait_ge(counted, 1)
            nc.tensor.matmul(p_before[:, 0:J], m.upper[0:T, 0:T], count[:, :], start=True, stop=True)
            nc.tensor.matmul(p_total[:, 0:J], m.ones[0:T, 0:B], count[:, :], start=True, stop=True).then_inc(summed, 1)

        @block.sync
        def _(sp):
            sp.wait_ge(bucketed, 1)
            with nc.allow_non_contiguous_dma(reason="a few hundred block numbers"):
                sp.dma_start(bucket_dram.rearrange("(i p) -> p i", p=B), bkt_i[:, :]).then_inc(stored, 16)
            sp.wait_ge(stored, 16)
            sp.dma_start(bucket_row, bucket_dram.rearrange("(a n) -> a n", a=1)[:, 0:blocks]).then_inc(stored, 16)
            sp.wait_ge(stored, 32)

        if extra is not None:
            extra(block, a)


def load_keys(nc, m, src, dst):
    with ExitStack() as ctx:
        a = Pool_(nc, ctx)
        loaded = a.sem("keys_loaded")
        chain = a.sem("keys_chain")
        block = a.block()

        @block.sync
        def _(sp):
            sp.dma_start(m.src_i[:, :], src.rearrange("(p c) -> p c", p=T)).then_inc(loaded, 16)
            sp.dma_start(m.dst_i[:, :], dst.rearrange("(p c) -> p c", p=T)).then_inc(loaded, 16)

        @block.vector
        def _(dve):
            link = chained(dve, chain)
            dve.wait_ge(loaded, 32)
            link(nc.vector.tensor_copy(m.src_f[:, :], m.src_i[:, :]))
            link(nc.vector.tensor_copy(m.dst_f[:, :], m.dst_i[:, :]))


def fill_records(nc, m, name, recs, cols, key_col):
    per = recs.shape[0] // B
    some = 22
    with ExitStack() as ctx:
        a = Pool_(nc, ctx)
        blank = a.sb(name + "blank", [B, some, cols])
        cleared = a.sem(name + "cleared")
        filled = a.sem(name + "filled")
        block = a.block()
        view = recs.rearrange("(p r) c -> p r c", p=B)

        @block.vector
        def _(dve):
            nc.vector.memset(blank[:, :, :], 0.0).then_inc(cleared, 1)
            dve.wait_ge(cleared, 1)
            nc.vector.memset(blank[:, :, key_col:key_col + 1], -1.0).then_inc(cleared, 1)

        @block.sync
        def _(sp):
            sp.wait_ge(cleared, 2)
            with sp.Fori(0, per // some) as i:
                sp.dma_start(view[:, bass.ds(i * some, some), :], blank[:, :, :]).then_inc(filled, 16)
            sp.wait_ge(filled, 16 * (per // some))


def scatter_records(nc, m, name, recs, pos_i, local, other_i, attrs):
    W = recs.shape[1]
    groups = EC // G
    with ExitStack() as ctx:
        a = Pool_(nc, ctx)
        rec = [a.sb(f"{name}rec{b}", [T, G, W]) for b in range(2)]
        pos = [a.sb(f"{name}pos{b}", [T, G], I32) for b in range(2)]
        attr_in = [a.sem(f"{name}attr_in{b}") for b in range(2)]
        built = a.sem(name + "built")
        sent = m.indirect_sems(2)
        block = a.block()

        if attrs is not None:
            view = attrs.rearrange("(p c) a -> p c a", p=T)

            @block.sync
            def _(sp):
                def load(k, b):
                    after(sp, sent[b], 16 * G * k)
                    sp.dma_start(rec[b][:, :, 0:EA], view[:, bass.ds((2 * k + b) * G, G), :]).then_inc(attr_in[b], 16)
                pipelined(sp, groups, [(0, load)])

        @block.vector
        def _(dve):
            def build(k, b):
                c = bass.ds((2 * k + b) * G, G)
                after(dve, sent[b], 16 * G * k)
                nc.vector.tensor_copy(rec[b][:, :, W - 2], local[:, c])
                nc.vector.tensor_copy(rec[b][:, :, W - 1].bitcast(I32), other_i[:, c])
                nc.vector.tensor_copy(pos[b][:, :], pos_i[:, c]).then_inc(built, 1)
            pipelined(dve, groups, [(0, build)])

        @block.gpsimd
        def _(pool):
            def scatter(k, b):
                pool.wait_ge(built, 2 * k + b + 1)
                if attrs is not None:
                    pool.wait_ge(attr_in[b], 16 * (k + 1))
                pool.sem_inc(m.tick, 1)
                for g in range(G):
                    nc.gpsimd.indirect_dma_start(
                        out=recs, out_offset=bass.IndirectOffsetOnAxis(ap=pos[b][:, g:g + 1].bitcast(U32), axis=0),
                        in_=rec[b][:, g, :], in_offset=None).then_inc(sent[b], 16)
            pipelined(pool, groups, [(0, scatter)])
            for b in range(2):
                pool.wait_ge(sent[b], 16 * G * ((groups + 1 - b) // 2))


def ln_stats(nc, dve, link, act_sem, sqrt_sem, n, src, mv, stats, stat_sem, rstd):
    with dve.Fori(0, NT) as t:
        nc.vector.bn_stats(stats[:, bass.ds(t, 1), :].rearrange("p a s -> p (a s)"), src(t)).then_inc(stat_sem, 1)
    dve.wait_ge(stat_sem, 2 * NT * n + NT)
    for t in range(NT):
        last = nc.vector.bn_aggr(mv[:, t, :], stats[:, t, :])
    last.then_inc(stat_sem, NT)
    dve.wait_ge(stat_sem, 2 * NT * (n + 1))
    nc.vector.tensor_scalar(rstd[:, :], mv[:, :, 1], EPS, None, ALU.add).then_inc(act_sem, 1)
    dve.wait_ge(sqrt_sem, n + 1)
    link(nc.vector.reciprocal(rstd[:, :], rstd[:, :]))


def ln_root(nc, act, act_sem, sqrt_sem, n, rstd):
    act.wait_ge(act_sem, n + 1)
    nc.scalar.activation(rstd[:, :], rstd[:, :], ACT.Sqrt).then_inc(sqrt_sem, 1)


def tile_of(x, t):
    return x[:, bass.ds(t, 1), :].rearrange("p a d -> p (a d)")


def node_phase(nc, m, x, w1ab, b1, b_table):
    with ExitStack() as ctx:
        a = Pool_(nc, ctx)
        w = a.sb("w1ab", [B, 2, 2 * D])
        bias = a.sb("b1_all", [T, D])
        stats = a.sb("n_stats", [T, NT, 6])
        mv = a.sb("n_mv", [T, NT, 2])
        rstd = a.sb("n_rstd", [T, NT])
        rows = [a.sb(f"b_rows{b}", [T, D]) for b in range(2)]
        hT = [a.sb(f"n_hT{b}", [B, 2, T]) for b in range(2)]
        p_t = [a.ps(f"n_pt{b}", [B, 512]) for b in range(2)]
        p_ab = [a.ps(f"n_pab{b}", [T, 512]) for b in range(2)]
        x_in, w_in, stat, var_ok, rooted, chain = (a.sem("n_" + s) for s in ("x_in", "w_in", "stat", "var", "root", "ch"))
        hn = [a.sb(f"n_hn{b}", [T, D]) for b in range(2)]
        kept = a.sem("n_kept")
        normed, turned, copied, multiplied, split = (a.sem("n_" + s) for s in ("normed", "turned", "copied", "mul", "split"))
        stored = [a.sem(f"n_stored{b}") for b in range(2)]
        block = a.block()

        @block.sync
        def _(sp):
            sp.dma_start(m.x[:, :, :], x.rearrange("(t p) d -> p t d", p=T)).then_inc(x_in, 16)
            sp.dma_start(w[:, :, :], w1ab.rearrange("(k p) n -> p k n", p=B)).then_inc(w_in, 16)
            sp.dma_start(bias[:, :], b1.rearrange("(a d) -> a d", a=1).to_broadcast([T, D])).then_inc(w_in, 16)

            def store(k, b):
                t = 2 * k + b
                sp.wait_ge(split, t + 1)
                sp.dma_start(b_table[bass.ds(t * T, T), :], rows[b][:, :]).then_inc(stored[b], 16)
            pipelined(sp, NT, [(0, store)])
            for b in range(2):
                sp.wait_ge(stored[b], 16 * ((NT + 1 - b) // 2))

        @block.vector
        def _(dve):
            link = chained(dve, chain)
            dve.wait_ge(x_in, 16)
            ln_stats(nc, dve, link, var_ok, rooted, 0, lambda t: tile_of(m.x, t), mv, stats, stat, rstd)
            dve.wait_ge(w_in, 32)

            def norm(k, b):
                t = 2 * k + b
                after(dve, turned, t - 1)
                after(dve, kept, t - 1)
                nc.vector.tensor_scalar(hn[b][:, :], tile_of(m.x, t), mv[:, bass.ds(t, 1), 0],
                                        rstd[:, bass.ds(t, 1)], ALU.subtract, ALU.mult).then_inc(normed, 1)

            def spread(k, b):
                t = 2 * k + b
                dve.wait_ge(multiplied, t + 1)
                after(dve, stored[b], 16 * k)
                nc.vector.tensor_copy(tile_of(m.a, t), p_ab[b][:, 0:D])
                nc.vector.tensor_tensor(rows[b][:, :], p_ab[b][:, D:2 * D], bias[:, :], ALU.add).then_inc(split, 1)
            pipelined(dve, NT, [(0, norm), (2, spread)])

        @block.gpsimd
        def _(pool):
            def keep(k, b):
                pool.wait_ge(normed, 2 * k + b + 1)
                nc.gpsimd.tensor_copy(tile_of(m.hn, 2 * k + b), hn[b][:, :]).then_inc(kept, 1)
            pipelined(pool, NT, [(0, keep)])

        @block.scalar
        def _(act):
            ln_root(nc, act, var_ok, rooted, 0, rstd)

            def copy(k, b):
                t = 2 * k + b
                act.wait_ge(turned, t + 1)
                after(act, multiplied, t - 1)
                nc.scalar.copy(hT[b][:, :, :].rearrange("p k n -> p (k n)"), p_t[b][:, 0:2 * T]).then_inc(copied, 1)
            pipelined(act, NT, [(0, copy)])

        @block.tensor
        def _(pe):
            pe.wait_ge(w_in, 32)

            def turn(k, b):
                t = 2 * k + b
                pe.wait_ge(normed, t + 1)
                after(pe, copied, t - 1)
                for j in range(2):
                    last = nc.tensor.transpose(p_t[b][:, j * T:(j + 1) * T],
                                               hn[b][:, j * B:(j + 1) * B],
                                               m.ident[0:T, 0:T])
                last.then_inc(turned, 1)

            def multiply(k, b):
                t = 2 * k + b
                pe.wait_ge(copied, t + 1)
                after(pe, split, t - 1)
                for j in range(2):
                    last = nc.tensor.matmul(p_ab[b][:, :], hT[b][:, j, :], w[:, j, :], start=(j == 0), stop=(j == 1))
                last.then_inc(multiplied, 1)
            pipelined(pe, NT, [(0, turn), (1, multiply)])


def message_phase(nc, m, recs, b_table, w1c):
    with ExitStack() as ctx:
        a = Pool_(nc, ctx)
        w = a.sb("w1c", [EA, D])
        rec = [a.sb(f"m_rec{b}", [B, REC]) for b in range(4)]
        got = [a.sb(f"m_got{b}", [B, D]) for b in range(4)]
        oh = [a.sb(f"m_oh{b}", [B, T]) for b in range(4)]
        attrT = [a.sb(f"m_attrT{b}", [EA, B]) for b in range(4)]
        ohT = [a.sb(f"m_ohT{b}", [T, B]) for b in range(4)]
        msg = [a.sb(f"m_msg{b}", [B, D + 1]) for b in range(4)]
        p_t = [a.ps(f"m_pt{b}", [B, 512]) for b in range(2)]
        p_pre = [a.ps(f"m_pre{b}", [B, 512]) for b in range(2)]
        p_seg = [a.ps(f"m_seg{b}", [T, 512]) for b in range(2)]
        w_in = a.sem("m_w_in")
        rec_in = [a.sem(f"m_rec_in{b}") for b in range(4)]
        got_in = m.indirect_sems(4)
        marked, turned, copied, pre, added, relued, summed, taken, cleared = (
            a.sem("m_" + s) for s in ("marked", "turned", "copied", "pre", "added", "relued", "summed", "taken", "cleared"))
        block = a.block()

        @block.sync
        def _(sp):
            sp.dma_start(w[:, :], w1c).then_inc(w_in, 16)

            def load(k, b):
                q = 4 * k + b
                after(sp, got_in[b], 16 * k)
                sp.sem_inc(m.tick, 1)
                after(sp, turned, q - 3)
                sp.sem_inc(m.tick, 1)
                sp.dma_start(rec[b][:, :], recs[bass.ds(q * B, B), :]).then_inc(rec_in[b], 16)
            pipelined(sp, EB, [(0, load)], 4)

        @block.gpsimd
        def _(pool):
            def gather(k, b):
                q = 4 * k + b
                pool.wait_ge(rec_in[b], 16 * (k + 1))
                after(pool, added, q - 3)
                pool.sem_inc(m.tick, 1)
                nc.gpsimd.indirect_dma_start(
                    out=got[b][:, :], out_offset=None, in_=b_table,
                    in_offset=bass.IndirectOffsetOnAxis(ap=rec[b][:, EA + 1:EA + 2].bitcast(U32), axis=0)
                ).then_inc(got_in[b], 16)
            pipelined(pool, EB, [(0, gather)], 4)

        @block.vector
        def _(dve):
            for b in range(4):
                nc.vector.memset(msg[b][:, D:D + 1], 1.0)
            nc.vector.memset(m.acc[:, :, :], 0.0).then_inc(cleared, 1)
            dve.wait_ge(cleared, 1)

            def mark(k, b):
                q = 4 * k + b
                dve.wait_ge(rec_in[b], 16 * (k + 1))
                after(dve, summed, q - 3)
                nc.vector.tensor_scalar(oh[b][:, :], m.ramp[:, 0:T], rec[b][:, EA:EA + 1], None,
                                        ALU.is_equal).then_inc(marked, 1)

            def add(k, b):
                q = 4 * k + b
                dve.wait_ge(pre, q + 1)
                dve.wait_ge(got_in[b], 16 * (k + 1))
                after(dve, summed, q - 3)
                nc.vector.tensor_tensor(msg[b][:, 0:D], p_pre[b % 2][:, 0:D], got[b][:, :], ALU.add).then_inc(added, 1)

            def take(k, b):
                q = 4 * k + b
                t = dve.value_load(m.src_tile[0:1, bass.ds(q, 1)], min_val=0, max_val=NT - 1)
                dve.wait_ge(summed, q + 1)
                after(dve, taken, q)
                nc.vector.tensor_tensor(tile_of(m.acc, t), tile_of(m.acc, t), p_seg[b % 2][:, 0:D + 1],
                                        ALU.add).then_inc(taken, 1)
            pipelined(dve, EB, [(4, take), (2, add), (0, mark)], 4)

        @block.scalar
        def _(act):
            def copy(k, b):
                q = 4 * k + b
                act.wait_ge(turned, q + 1)
                after(act, pre, q - 3)
                nc.scalar.copy(attrT[b][:, :], p_t[b % 2][0:EA, 0:B])
                nc.scalar.copy(ohT[b][:, :], p_t[b % 2][0:T, B:2 * B]).then_inc(copied, 1)

            def relu(k, b):
                q = 4 * k + b
                act.wait_ge(added, q + 1)
                nc.scalar.activation(msg[b][:, 0:D], msg[b][:, 0:D], ACT.Relu).then_inc(relued, 1)
            pipelined(act, EB, [(1, copy), (2, relu)], 4)

        @block.tensor
        def _(pe):
            pe.wait_ge(w_in, 16)
            pe.wait_ge(cleared, 1)

            def turn(k, b):
                q = 4 * k + b
                pe.wait_ge(marked, q + 1)
                pe.wait_ge(rec_in[b], 16 * (k + 1))
                after(pe, copied, q - 1)
                nc.tensor.transpose(p_t[b % 2][0:REC, 0:B], rec[b][:, :], m.ident[:, :])
                nc.tensor.transpose(p_t[b % 2][0:T, B:2 * B], oh[b][:, :], m.ident[:, :]).then_inc(turned, 1)

            def sum_up(k, b):
                q = 4 * k + b
                t = pe.value_load(m.src_tile[0:1, bass.ds(q, 1)], min_val=0, max_val=NT - 1)
                pe.wait_ge(copied, q + 1)
                after(pe, added, q - 1)
                nc.tensor.matmul(p_pre[b % 2][:, 0:D], attrT[b][:, :], w[:, :], start=True, stop=False)
                nc.tensor.matmul(p_pre[b % 2][:, 0:D], ohT[b][:, :], tile_of(m.a, t), start=False, stop=True).then_inc(pre, 1)

            def segment(k, b):
                q = 4 * k + b
                pe.wait_ge(relued, q + 1)
                after(pe, taken, q - 1)
                nc.tensor.matmul(p_seg[b % 2][:, 0:D + 1], oh[b][:, :], msg[b][:, :], start=True, stop=True).then_inc(summed, 1)
            pipelined(pe, EB, [(1, turn), (2, sum_up), (3, segment)], 4)


def steps(eng, sem, start):
    count = [0]

    def step(ins):
        count[0] += 1
        ins.then_inc(sem, 1)
        eng.wait_ge(sem, start + count[0])
    return step


def row_to_all(v, rows):
    return v.rearrange("(a d) -> a d", a=1).to_broadcast([rows, v.shape[0]])


def gru_phase(nc, m, w2, b2, w_ih, b_ih, w_hh, b_hh):
    with ExitStack() as ctx:
        a = Pool_(nc, ctx)
        w2s = a.sb("g_w2", [B, 2, D])
        wih = a.sb("g_wih", [B, 2, 3 * D])
        whh = a.sb("g_whh", [B, 2, 3 * D])
        b2s = a.sb("g_b2", [T, D])
        bih = a.sb("g_bih", [T, 3 * D])
        bhh = a.sb("g_bhh", [T, 3 * D])
        sums = [a.sb(f"g_sums{b}", [T, D + 1]) for b in range(2)]
        hid = [a.sb(f"g_hid{b}", [T, D]) for b in range(2)]
        shT = [a.sb(f"g_shT{b}", [B, 4, T]) for b in range(4)]
        agg = [a.sb(f"g_agg{b}", [T, D]) for b in range(2)]
        aggT = [a.sb(f"g_aggT{b}", [B, 2, T]) for b in range(2)]
        rz = [a.sb(f"g_rz{b}", [T, 2 * D]) for b in range(2)]
        cand = [a.sb(f"g_cand{b}", [T, D]) for b in range(2)]
        part = a.sb("g_part", [T, D])
        p_sh = a.ps("g_psh", [B, 512])
        p_agg = a.ps("g_pagg", [T, 512])
        p_aggT = a.ps("g_paggT", [B, 512])
        p_rz = [a.ps(f"g_prz{b}", [T, 512]) for b in range(2)]
        p_n = [a.ps(f"g_pn{b}", [T, 512]) for b in range(2)]
        w_in = a.sem("g_w_in")
        bias_ok = a.sem("g_bias_ok")
        (staged, turned, copied, agg_mul, agg_done, agg_turned, agg_copied, gates, preact, opened, pre_n, squashed,
         mixed, chain_n, chain_x) = (a.sem("g_" + s) for s in (
             "staged", "turned", "copied", "agg_mul", "agg_done", "agg_turned", "agg_copied", "gates", "preact",
             "opened", "pre_n", "squashed", "mixed", "chain_n", "chain_x"))
        block = a.block()

        @block.sync
        def _(sp):
            for dst, src in ((w2s, w2), (wih, w_ih), (whh, w_hh)):
                sp.dma_start(dst[:, :, :], src.rearrange("(k p) n -> p k n", p=B)).then_inc(w_in, 16)
            for dst, src in ((b2s, b2), (bih, b_ih), (bhh, b_hh)):
                sp.dma_start(dst[:, :], row_to_all(src, T)).then_inc(w_in, 16)

        @block.gpsimd
        def _(pool):
            def stage(k, b):
                t = 2 * k + b
                after(pool, turned, t - 1)
                after(pool, agg_done, t - 1)
                nc.gpsimd.tensor_copy(sums[b][:, :], tile_of(m.acc, t))
                nc.gpsimd.tensor_copy(hid[b][:, :], tile_of(m.hn, t)).then_inc(staged, 1)
            pipelined(pool, NT, [(0, stage)])

        @block.tensor
        def _(pe):
            pe.wait_ge(w_in, 96)

            def turn(k, b):
                t = 2 * k + b
                pe.wait_ge(staged, t + 1)
                after(pe, copied, t)
                for j in range(2):
                    nc.tensor.transpose(p_sh[:, j * T:(j + 1) * T], sums[b][:, j * B:(j + 1) * B], m.ident[0:T, 0:T])
                for j in range(2):
                    last = nc.tensor.transpose(p_sh[:, (2 + j) * T:(3 + j) * T], hid[b][:, j * B:(j + 1) * B],
                                               m.ident[0:T, 0:T])
                last.then_inc(turned, 1)

            def aggregate(k, b):
                t = 4 * k + b
                pe.wait_ge(copied, t + 1)
                after(pe, agg_done, t)
                for j in range(2):
                    last = nc.tensor.matmul(p_agg[:, 0:D], shT[b][:, j, :], w2s[:, j, :], start=(j == 0), stop=(j == 1))
                last.then_inc(agg_mul, 1)

            def turn_agg(k, b):
                t = 4 * k + b
                pe.wait_ge(agg_done, t + 1)
                after(pe, agg_copied, t)
                for j in range(2):
                    last = nc.tensor.transpose(p_aggT[:, j * T:(j + 1) * T], agg[b % 2][:, j * B:(j + 1) * B],
                                               m.ident[0:T, 0:T])
                last.then_inc(agg_turned, 1)

            def gate(k, b):
                t = 4 * k + b
                pe.wait_ge(agg_copied, t + 1)
                after(pe, preact, t - 1)
                after(pe, pre_n, t - 1)
                c = b % 2
                for j in range(2):
                    nc.tensor.matmul(p_rz[c][:, :], aggT[c][:, j, :], wih[:, j, 0:2 * D], start=(j == 0), stop=False)
                for j in range(2):
                    nc.tensor.matmul(p_rz[c][:, :], shT[b][:, 2 + j, :], whh[:, j, 0:2 * D], start=False, stop=(j == 1))
                for j in range(2):
                    nc.tensor.matmul(p_n[c][:, 0:D], aggT[c][:, j, :], wih[:, j, 2 * D:], start=(j == 0), stop=(j == 1))
                for j in range(2):
                    last = nc.tensor.matmul(p_n[c][:, D:2 * D], shT[b][:, 2 + j, :], whh[:, j, 2 * D:],
                                            start=(j == 0), stop=(j == 1))
                last.then_inc(gates, 1)
            pipelined(pe, NT, [(3, gate), (2, turn_agg), (1, aggregate), (0, lambda k, b: turn(2 * k + b // 2, b % 2))], 4)

        @block.scalar
        def _(act):
            def copy(k, b):
                t = 4 * k + b
                act.wait_ge(turned, t + 1)
                after(act, gates, t - 3)
                nc.scalar.copy(shT[b][:, :, :].rearrange("p k n -> p (k n)"), p_sh[:, 0:4 * T]).then_inc(copied, 1)

            def copy_agg(k, b):
                t = 4 * k + b
                act.wait_ge(agg_turned, t + 1)
                after(act, gates, t - 1)
                nc.scalar.copy(aggT[b % 2][:, :, :].rearrange("p k n -> p (k n)"), p_aggT[:, 0:2 * T]).then_inc(agg_copied, 1)

            def open_gates(k, b):
                t = 4 * k + b
                act.wait_ge(preact, t + 1)
                nc.scalar.activation(rz[b % 2][:, :], rz[b % 2][:, :], ACT.Sigmoid).then_inc(opened, 1)

            def squash(k, b):
                t = 4 * k + b
                act.wait_ge(pre_n, t + 1)
                nc.scalar.activation(cand[b % 2][:, :], cand[b % 2][:, :], ACT.Tanh).then_inc(squashed, 1)
            pipelined(act, NT, [(3, open_gates), (3, squash), (2, copy_agg), (0, copy)], 4)

        @block.vector
        def _(dve):
            dve.wait_ge(w_in, 96)
            nc.vector.tensor_tensor(bih[:, 0:2 * D], bih[:, 0:2 * D], bhh[:, 0:2 * D], ALU.add).then_inc(bias_ok, 1)
            dve.wait_ge(bias_ok, 1)

            def biased(k, b):
                t = 4 * k + b
                dve.wait_ge(agg_mul, t + 1)
                after(dve, agg_turned, t - 1)
                nc.vector.scalar_tensor_tensor(out=agg[b % 2][:, :], in0=b2s[:, :], scalar=sums[b % 2][:, D:D + 1],
                                               in1=p_agg[:, 0:D], op0=ALU.mult, op1=ALU.add).then_inc(agg_done, 1)

            def pre(k, b):
                t = 4 * k + b
                c = b % 2
                step = steps(dve, chain_n, 3 * t)
                dve.wait_ge(gates, t + 1)
                after(dve, mixed, t - 1)
                nc.vector.tensor_tensor(rz[c][:, :], p_rz[c][:, :], bih[:, 0:2 * D], ALU.add).then_inc(preact, 1)
                step(nc.vector.tensor_tensor(cand[c][:, :], p_n[c][:, D:2 * D], bhh[:, 2 * D:], ALU.add))
                dve.wait_ge(opened, t + 1)
                step(nc.vector.tensor_tensor(cand[c][:, :], cand[c][:, :], rz[c][:, 0:D], ALU.mult))
                step(nc.vector.tensor_tensor(cand[c][:, :], cand[c][:, :], bih[:, 2 * D:], ALU.add))
                nc.vector.tensor_tensor(cand[c][:, :], cand[c][:, :], p_n[c][:, 0:D], ALU.add).then_inc(pre_n, 1)

            def mix(k, b):
                t = 4 * k + b
                c = b % 2
                step = steps(dve, chain_x, 4 * t)
                dve.wait_ge(squashed, t + 1)
                step(nc.vector.tensor_tensor(part[:, :], tile_of(m.hn, t), cand[c][:, :], ALU.subtract))
                step(nc.vector.tensor_tensor(part[:, :], part[:, :], rz[c][:, D:2 * D], ALU.mult))
                step(nc.vector.tensor_tensor(part[:, :], part[:, :], cand[c][:, :], ALU.add))
                step(nc.vector.tensor_tensor(tile_of(m.x, t), tile_of(m.x, t), part[:, :], ALU.add))
                dve.sem_inc(mixed, 1)
            pipelined(dve, NT, [(4, mix), (3, pre), (1, biased)], 4)


def normalize(nc, m, name, dst):
    with ExitStack() as ctx:
        a = Pool_(nc, ctx)
        stats = a.sb(name + "stats", [T, NT, 6])
        mv = a.sb(name + "mv", [T, NT, 2])
        rstd = a.sb(name + "rstd", [T, NT])
        stat, var_ok, rooted, chain = (a.sem(name + s) for s in ("stat", "var", "root", "ch"))
        block = a.block()

        @block.vector
        def _(dve):
            link = chained(dve, chain)
            ln_stats(nc, dve, link, var_ok, rooted, 0, lambda t: tile_of(m.x, t), mv, stats, stat, rstd)
            with dve.Fori(0, NT) as t:
                nc.vector.tensor_scalar(tile_of(dst, t), tile_of(m.x, t), mv[:, bass.ds(t, 1), 0],
                                        rstd[:, bass.ds(t, 1)], ALU.subtract, ALU.mult)

        @block.scalar
        def _(act):
            ln_root(nc, act, var_ok, rooted, 0, rstd)


def router_phase(nc, m, wr, br):
    with ExitStack() as ctx:
        a = Pool_(nc, ctx)
        w = a.sb("r_w", [B, 2, NEX])
        bias = a.sb("r_b", [T, NEX])
        stats = a.sb("r_stats", [T, NT, 6])
        ln = [a.sb(f"r_ln{b}", [T, D]) for b in range(2)]
        lnT = [a.sb(f"r_lnT{b}", [B, 2, T]) for b in range(2)]
        logit = [a.sb(f"r_logit{b}", [T, NEX]) for b in range(2)]
        top = [a.sb(f"r_top{b}", [T, 8]) for b in range(2)]
        at = [a.sb(f"r_at{b}", [T, 8], U32) for b in range(2)]
        gap = a.sb("r_gap", [T, NT])
        den = a.sb("r_den", [T, NT])
        p_t = [a.ps(f"r_pt{b}", [B, 512]) for b in range(2)]
        p_l = [a.ps(f"r_pl{b}", [T, 512]) for b in range(2)]
        w_in, stat, var_ok, rooted, chain, chain_t = (a.sem("r_" + s) for s in ("w", "stat", "var", "root", "ch", "cht"))
        staged, turned, copied, mul, found, gap_ok, exp_ok = (
            a.sem("r_" + s) for s in ("staged", "turned", "copied", "mul", "found", "gap_ok", "exp_ok"))
        block = a.block()

        @block.sync
        def _(sp):
            sp.dma_start(w[:, :, :], wr.rearrange("(k p) n -> p k n", p=B)).then_inc(w_in, 16)
            sp.dma_start(bias[:, :], row_to_all(br, T)).then_inc(w_in, 16)

        @block.vector
        def _(dve):
            link = chained(dve, chain)
            ln_stats(nc, dve, link, var_ok, rooted, 0, lambda t: tile_of(m.ln, t), m.mv, stats, stat, m.rstd)
            dve.wait_ge(w_in, 32)

            def choose(k, b):
                t = 2 * k + b
                step = steps(dve, chain_t, 3 * t)
                dve.wait_ge(mul, t + 1)
                step(nc.vector.tensor_tensor(logit[b][:, :], p_l[b][:, 0:NEX], bias[:, :], ALU.add))
                dve.sem_inc(m.tick, 1)
                step(nc.vector.max(top[b][:, :], logit[b][:, :]))
                dve.sem_inc(m.tick, 1)
                step(nc.vector.max_index(at[b][:, :], top[b][:, :], logit[b][:, :]))
                nc.vector.tensor_copy(m.expert[:, bass.ds(t, 1)], at[b][:, 0:1])
                nc.vector.tensor_copy(m.expert[:, bass.ds(t + NT, 1)], at[b][:, 1:2])
                nc.vector.tensor_tensor(gap[:, bass.ds(t, 1)], top[b][:, 1:2], top[b][:, 0:1],
                                        ALU.subtract).then_inc(found, 1)
            pipelined(dve, NT, [(0, choose)])
            dve.wait_ge(exp_ok, 1)
            link(nc.vector.tensor_scalar(den[:, :], gap[:, :], 1.0, None, ALU.add))
            link(nc.vector.reciprocal(m.weight[:, 0:NT], den[:, :]))
            link(nc.vector.tensor_tensor(m.weight[:, NT:2 * NT], gap[:, :], m.weight[:, 0:NT], ALU.mult))

        @block.gpsimd
        def _(pool):
            def stage(k, b):
                t = 2 * k + b
                after(pool, turned, t - 1)
                nc.gpsimd.tensor_copy(ln[b][:, :], tile_of(m.ln, t)).then_inc(staged, 1)
            pipelined(pool, NT, [(0, stage)])

        @block.scalar
        def _(act):
            ln_root(nc, act, var_ok, rooted, 0, m.rstd)

            def copy(k, b):
                t = 2 * k + b
                act.wait_ge(turned, t + 1)
                after(act, mul, t - 1)
                nc.scalar.copy(lnT[b][:, :, :].rearrange("p k n -> p (k n)"), p_t[b][:, 0:2 * T]).then_inc(copied, 1)
            pipelined(act, NT, [(0, copy)])
            act.wait_ge(found, NT)
            nc.scalar.activation(gap[:, :], gap[:, :], ACT.Exp).then_inc(exp_ok, 1)

        @block.tensor
        def _(pe):
            pe.wait_ge(w_in, 32)

            def turn(k, b):
                t = 2 * k + b
                pe.wait_ge(staged, t + 1)
                after(pe, copied, t - 1)
                for j in range(2):
                    last = nc.tensor.transpose(p_t[b][:, j * T:(j + 1) * T], ln[b][:, j * B:(j + 1) * B],
                                               m.ident[0:T, 0:T])
                last.then_inc(turned, 1)

            def multiply(k, b):
                t = 2 * k + b
                pe.wait_ge(copied, t + 1)
                after(pe, found, t - 1)
                for j in range(2):
                    last = nc.tensor.matmul(p_l[b][:, 0:NEX], lnT[b][:, j, :], w[:, j, :], start=(j == 0), stop=(j == 1))
                last.then_inc(mul, 1)
            pipelined(pe, NT, [(1, multiply), (0, turn)])


def send_tokens(nc, m, tokens):
    per = MB * B // B
    some = 8
    with ExitStack() as ctx:
        a = Pool_(nc, ctx)
        blank = a.sb("t_blank", [B, some, D])
        xn = [a.sb(f"t_xn{b}", [T, D]) for b in range(2)]
        pos = [a.sb(f"t_pos{b}", [T, 2], I32) for b in range(2)]
        cleared, filled, built = (a.sem("t_" + s) for s in ("cleared", "filled", "built"))
        sent = m.indirect_sems(2)
        block = a.block()
        view = tokens.rearrange("(p r) c -> p r c", p=B)

        @block.sync
        def _(sp):
            sp.wait_ge(cleared, 1)
            with sp.Fori(0, per // some) as i:
                sp.dma_start(view[:, bass.ds(i * some, some), :], blank[:, :, :]).then_inc(filled, 16)

        @block.vector
        def _(dve):
            nc.vector.memset(blank[:, :, :], 0.0).then_inc(cleared, 1)

            def build(k, b):
                t = 2 * k + b
                after(dve, sent[b], 32 * k)
                nc.vector.tensor_copy(pos[b][:, 0:1], m.slot[:, bass.ds(t, 1)])
                nc.vector.tensor_copy(pos[b][:, 1:2], m.slot[:, bass.ds(t + NT, 1)])
                nc.vector.tensor_scalar(xn[b][:, :], tile_of(m.ln, t), m.mv[:, bass.ds(t, 1), 0],
                                        m.rstd[:, bass.ds(t, 1)], ALU.subtract, ALU.mult).then_inc(built, 1)
            pipelined(dve, NT, [(0, build)])

        @block.gpsimd
        def _(pool):
            pool.wait_ge(filled, 16 * (per // some))

            def scatter(k, b):
                pool.wait_ge(built, 2 * k + b + 1)
                pool.sem_inc(m.tick, 1)
                for g in range(2):
                    nc.gpsimd.indirect_dma_start(
                        out=tokens, out_offset=bass.IndirectOffsetOnAxis(ap=pos[b][:, g:g + 1].bitcast(U32), axis=0),
                        in_=xn[b][:, :], in_offset=None).then_inc(sent[b], 16)
            pipelined(pool, NT, [(0, scatter)])
            for b in range(2):
                pool.wait_ge(sent[b], 32 * ((NT + 1 - b) // 2))


def expert_phase(nc, m, tokens, answers, w1, w2, ln_g, ln_b, b1, b2):
    with ExitStack() as ctx:
        a = Pool_(nc, ctx)
        w1s = a.sb("e_w1", [B, NEX * 2, HID])
        w2s = a.sb("e_w2", [B, NEX * 8, D])
        gain = a.sb("e_gain", [B, NEX * 2])
        shift = a.sb("e_shift", [B, NEX * 2])
        b1s = a.sb("e_b1", [B, NEX * 8])
        b2s = a.sb("e_b2", [B, NEX, D])
        tok = [a.sb(f"e_tok{b}", [B, D]) for b in range(2)]
        tokT = [a.sb(f"e_tokT{b}", [B, 2, B]) for b in range(2)]
        wg = [a.sb(f"e_wg{b}", [B, 2, HID]) for b in range(2)]
        hid = [a.sb(f"e_hid{b}", [B, 8, B]) for b in range(2)]
        ans = [a.sb(f"e_ans{b}", [B, D]) for b in range(2)]
        p_t = a.ps("e_pt", [B, 512])
        p_h = [[a.ps(f"e_ph{b}{i}", [B, 512]) for i in range(2)] for b in range(2)]
        p_y = [a.ps(f"e_py{b}", [B, 512]) for b in range(2)]
        w_in, small_in, shifted, bias_ok = (a.sem("e_" + s) for s in ("w", "small", "shifted", "bias_ok"))
        tok_in = [a.sem(f"e_tok_in{b}") for b in range(2)]
        stored = [a.sem(f"e_stored{b}") for b in range(2)]
        turned, copied, weighted, up, act_ok, down, answered = (
            a.sem("e_" + s) for s in ("turned", "copied", "weighted", "up", "act_ok", "down", "answered"))
        block = a.block()

        @block.sync
        def _(sp):
            sp.dma_start(gain[:, :], ln_g).then_inc(small_in, 16)
            sp.dma_start(shift[:, :], ln_b).then_inc(small_in, 16)
            sp.dma_start(b1s[:, :], b1).then_inc(small_in, 16)
            sp.dma_start(b2s[:, :, :].rearrange("p e d -> p (e d)"), row_to_all(b2, B)).then_inc(small_in, 16)
            for e in range(NEX):
                sp.dma_start(w1s[:, 2 * e:2 * e + 2, :], w1[e].rearrange("(k p) h -> p k h", p=B)).then_inc(w_in, 16)
                sp.dma_start(w2s[:, 8 * e:8 * e + 8, :], w2[e].rearrange("(j p) d -> p j d", p=B)).then_inc(w_in, 16)

            def load(k, b):
                q = 2 * k + b
                after(sp, turned, q - 1)
                sp.sem_inc(m.tick, 1)
                sp.dma_start(tok[b][:, :], tokens[bass.ds(q * B, B), :]).then_inc(tok_in[b], 16)

            def store(k, b):
                q = 2 * k + b
                sp.wait_ge(answered, q + 1)
                sp.sem_inc(m.tick, 1)
                sp.dma_start(answers[bass.ds(q * B, B), :], ans[b][:, :]).then_inc(stored[b], 16)
            pipelined(sp, MB, [(4, store), (0, load)])
            for b in range(2):
                sp.wait_ge(stored[b], 16 * (MB // 2))

        @block.tensor
        def _(pe):
            pe.wait_ge(small_in, 64)
            pe.wait_ge(w_in, 32 * NEX)
            for e in range(NEX):
                for j in range(8):
                    for k in range(2):
                        last = nc.tensor.matmul(p_t[:, 8 * e + j:8 * e + j + 1], w1s[:, 2 * e + k, j * B:(j + 1) * B],
                                                shift[:, 2 * e + k:2 * e + k + 1], start=(k == 0), stop=(k == 1))
            last.then_inc(shifted, 1)
            pe.wait_ge(bias_ok, 1)

            def turn(k, b):
                q = 2 * k + b
                pe.wait_ge(tok_in[b], 16 * (k + 1))
                after(pe, copied, q)
                for j in range(2):
                    last = nc.tensor.transpose(p_t[:, j * B:(j + 1) * B], tok[b][:, j * B:(j + 1) * B], m.ident[:, :])
                last.then_inc(turned, 1)

            def rise(k, b):
                q = 2 * k + b
                pe.wait_ge(copied, q + 1)
                pe.wait_ge(weighted, q + 1)
                after(pe, act_ok, q - 1)
                for j in range(8):
                    for i in range(2):
                        last = nc.tensor.matmul(p_h[b][j // 4][:, (j % 4) * B:(j % 4 + 1) * B],
                                                wg[b][:, i, j * B:(j + 1) * B], tokT[b][:, i, :],
                                                start=(i == 0), stop=(i == 1))
                last.then_inc(up, 1)

            def fall(k, b):
                q = 2 * k + b
                e = pe.value_load(m.block_expert[0:1, bass.ds(q, 1)], min_val=0, max_val=NEX - 1)
                pe.wait_ge(act_ok, q + 1)
                after(pe, answered, q - 1)
                for j in range(8):
                    last = nc.tensor.matmul(p_y[b][:, 0:D], hid[b][:, j, :], tile_of(w2s, e * 8 + j),
                                            start=(j == 0), stop=(j == 7))
                last.then_inc(down, 1)
            pipelined(pe, MB, [(2, fall), (1, rise), (0, turn)])

        @block.scalar
        def _(act):
            act.wait_ge(bias_ok, 1)

            def copy(k, b):
                q = 2 * k + b
                act.wait_ge(turned, q + 1)
                after(act, up, q - 1)
                nc.scalar.copy(tokT[b][:, :, :].rearrange("p k n -> p (k n)"), p_t[:, 0:2 * B]).then_inc(copied, 1)

            def gelu(k, b):
                q = 2 * k + b
                e = act.value_load(m.block_expert[0:1, bass.ds(q, 1)], min_val=0, max_val=NEX - 1)
                act.wait_ge(up, q + 1)
                after(act, down, q - 1)
                for j in range(8):
                    last = nc.scalar.activation(hid[b][:, j, :], p_h[b][j // 4][:, (j % 4) * B:(j % 4 + 1) * B],
                                                ACT.Gelu, bias=b1s[:, bass.ds(e * 8 + j, 1)])
                last.then_inc(act_ok, 1)
            pipelined(act, MB, [(1, gelu), (0, copy)])

        @block.vector
        def _(dve):
            dve.wait_ge(small_in, 64)
            dve.wait_ge(shifted, 1)
            nc.vector.tensor_tensor(b1s[:, :], p_t[:, 0:8 * NEX], b1s[:, :], ALU.add).then_inc(bias_ok, 1)
            dve.wait_ge(w_in, 32 * NEX)

            def weigh(k, b):
                q = 2 * k + b
                e = dve.value_load(m.block_expert[0:1, bass.ds(q, 1)], min_val=0, max_val=NEX - 1)
                after(dve, up, q - 1)
                for i in range(2):
                    last = nc.vector.tensor_scalar(wg[b][:, i, :], tile_of(w1s, e * 2 + i),
                                                   gain[:, bass.ds(e * 2 + i, 1)], None, ALU.mult)
                last.then_inc(weighted, 1)

            def answer(k, b):
                q = 2 * k + b
                e = dve.value_load(m.block_expert[0:1, bass.ds(q, 1)], min_val=0, max_val=NEX - 1)
                dve.wait_ge(down, q + 1)
                after(dve, stored[b], 16 * k)
                nc.vector.tensor_tensor(ans[b][:, :], p_y[b][:, 0:D], tile_of(b2s, e), ALU.add).then_inc(answered, 1)
            pipelined(dve, MB, [(3, answer), (0, weigh)])


def combine_phase(nc, m, answers):
    with ExitStack() as ctx:
        a = Pool_(nc, ctx)
        pos = [a.sb(f"c_pos{b}", [T, 2], I32) for b in range(2)]
        got = [[a.sb(f"c_got{b}{g}", [T, D]) for g in range(2)] for b in range(2)]
        built, added, chain = (a.sem("c_" + s) for s in ("built", "added", "chain"))
        got_in = m.indirect_sems(2)
        block = a.block()

        @block.gpsimd
        def _(pool):
            def gather(k, b):
                pool.wait_ge(built, 2 * k + b + 1)
                pool.sem_inc(m.tick, 1)
                for g in range(2):
                    nc.gpsimd.indirect_dma_start(
                        out=got[b][g][:, :], out_offset=None, in_=answers,
                        in_offset=bass.IndirectOffsetOnAxis(ap=pos[b][:, g:g + 1].bitcast(U32), axis=0)
                    ).then_inc(got_in[b], 16)
            pipelined(pool, NT, [(0, gather)])

        @block.vector
        def _(dve):
            def build(k, b):
                t = 2 * k + b
                after(dve, added, t - 1)
                nc.vector.tensor_copy(pos[b][:, 0:1], m.slot[:, bass.ds(t, 1)])
                nc.vector.tensor_copy(pos[b][:, 1:2], m.slot[:, bass.ds(t + NT, 1)]).then_inc(built, 1)

            def add(k, b):
                t = 2 * k + b
                step = steps(dve, chain, t)
                dve.wait_ge(got_in[b], 32 * (k + 1))
                step(nc.vector.scalar_tensor_tensor(out=tile_of(m.x, t), in0=got[b][0][:, :],
                                                    scalar=m.weight[:, bass.ds(t, 1)], in1=tile_of(m.x, t),
                                                    op0=ALU.mult, op1=ALU.add))
                nc.vector.scalar_tensor_tensor(out=tile_of(m.x, t), in0=got[b][1][:, :],
                                               scalar=m.weight[:, bass.ds(t + NT, 1)], in1=tile_of(m.x, t),
                                               op0=ALU.mult, op1=ALU.add).then_inc(added, 1)
            pipelined(dve, NT, [(1, add), (0, build)])


def attention_rows(nc, m, wg, a_src, a_dst, table):
    with ExitStack() as ctx:
        a = Pool_(nc, ctx)
        w = a.sb("h_w", [B, 2, D])
        a_s = a.sb("h_as", [T, D])
        a_d = a.sb("h_ad", [T, D])
        ln = [a.sb(f"h_ln{b}", [T, D]) for b in range(2)]
        lnT = [a.sb(f"h_lnT{b}", [B, 2, T]) for b in range(2)]
        row = [a.sb(f"h_row{b}", [T, HC]) for b in range(2)]
        junk = a.sb("h_junk", [T, 2, D])
        to = [a.sb(f"h_to{b}", [T, 1]) for b in range(2)]
        p_t = [a.ps(f"h_pt{b}", [B, 512]) for b in range(2)]
        p_h = [a.ps(f"h_ph{b}", [T, 512]) for b in range(2)]
        w_in, staged, turned, copied, mul, made, one, chain, chain_p = (
            a.sem("h_" + s) for s in ("w", "staged", "turned", "copied", "mul", "made", "one", "chain", "chain_p"))
        stored = [a.sem(f"h_stored{b}") for b in range(2)]
        block = a.block()

        @block.sync
        def _(sp):
            sp.dma_start(w[:, :, :], wg.rearrange("(k p) n -> p k n", p=B)).then_inc(w_in, 16)
            sp.dma_start(a_s[:, :], row_to_all(a_src, T)).then_inc(w_in, 16)
            sp.dma_start(a_d[:, :], row_to_all(a_dst, T)).then_inc(w_in, 16)

            def store(k, b):
                t = 2 * k + b
                sp.wait_ge(made, t + 1)
                sp.sem_inc(m.tick, 1)
                sp.dma_start(table[bass.ds(t * T, T), :], row[b][:, :]).then_inc(stored[b], 16)
            pipelined(sp, NT, [(0, store)])
            for b in range(2):
                sp.wait_ge(stored[b], 16 * ((NT + 1 - b) // 2))

        @block.gpsimd
        def _(pool):
            def stage(k, b):
                t = 2 * k + b
                after(pool, turned, t - 1)
                nc.gpsimd.tensor_copy(ln[b][:, :], tile_of(m.ln, t)).then_inc(staged, 1)
            pipelined(pool, NT, [(0, stage)])

        @block.scalar
        def _(act):
            def copy(k, b):
                t = 2 * k + b
                act.wait_ge(turned, t + 1)
                after(act, mul, t - 1)
                nc.scalar.copy(lnT[b][:, :, :].rearrange("p k n -> p (k n)"), p_t[b][:, 0:2 * T]).then_inc(copied, 1)
            pipelined(act, NT, [(0, copy)])

        @block.tensor
        def _(pe):
            pe.wait_ge(w_in, 48)

            def turn(k, b):
                t = 2 * k + b
                pe.wait_ge(staged, t + 1)
                after(pe, copied, t - 1)
                for j in range(2):
                    last = nc.tensor.transpose(p_t[b][:, j * T:(j + 1) * T], ln[b][:, j * B:(j + 1) * B],
                                               m.ident[0:T, 0:T])
                last.then_inc(turned, 1)

            def multiply(k, b):
                t = 2 * k + b
                pe.wait_ge(copied, t + 1)
                after(pe, made, t - 1)
                for j in range(2):
                    last = nc.tensor.matmul(p_h[b][:, 0:D], lnT[b][:, j, :], w[:, j, :], start=(j == 0), stop=(j == 1))
                last.then_inc(mul, 1)
            pipelined(pe, NT, [(1, multiply), (0, turn)])

        @block.vector
        def _(dve):
            for b in range(2):
                last = nc.vector.memset(row[b][:, D + 1:D + 2], 1.0)
            last.then_inc(one, 1)
            dve.wait_ge(one, 1)
            dve.wait_ge(w_in, 48)

            def make(k, b):
                t = 2 * k + b
                step = steps(dve, chain, 2 * t)
                dve.wait_ge(mul, t + 1)
                after(dve, stored[b], 16 * k)
                step(nc.vector.tensor_copy(row[b][:, 0:D], p_h[b][:, 0:D]))
                nc.vector.tensor_tensor_reduce(out=junk[:, 0, :], in0=row[b][:, 0:D], in1=a_s[:, :], scale=1.0,
                                               scalar=0.0, op0=ALU.mult, op1=ALU.add,
                                               accum_out=row[b][:, D:D + 1])
                step(nc.vector.tensor_tensor_reduce(out=junk[:, 1, :], in0=row[b][:, 0:D], in1=a_d[:, :], scale=1.0,
                                                    scalar=0.0, op0=ALU.mult, op1=ALU.add, accum_out=to[b][:, :]))
                nc.vector.tensor_copy(m.to[:, bass.ds(t, 1)], to[b][:, :])
                nc.vector.tensor_copy(tile_of(m.acc, t), row[b][:, :])
                nc.vector.tensor_tensor(tile_of(m.x, t), tile_of(m.x, t), tile_of(m.ln, t), ALU.add).then_inc(made, 1)
            pipelined(dve, NT, [(0, make)])
            dve.wait_ge(made, NT)
            link = chained(dve, chain_p)
            link(nc.vector.tensor_tensor(m.peak[:, :], m.acc[:, :, D], m.to[:, :], ALU.add))
            link(nc.vector.scalar_tensor_tensor(out=m.peak[:, :], in0=m.peak[:, :], scalar=0.2, in1=m.peak[:, :],
                                                op0=ALU.mult, op1=ALU.max))


def attention_phase(nc, m, recs, table, bias):
    with ExitStack() as ctx:
        a = Pool_(nc, ctx)
        peak = m.peak
        rec = [a.sb(f"a_rec{b}", [B, 2]) for b in range(4)]
        got = [a.sb(f"a_got{b}", [B, HC]) for b in range(4)]
        mark = [a.sb(f"a_mark{b}", [B, T]) for b in range(2)]
        top = [a.sb(f"a_top{b}", [T, 4]) for b in range(2)]
        shrink = [a.sb(f"a_shrink{b}", [T, 1]) for b in range(4)]
        score = [a.sb(f"a_score{b}", [T, B]) for b in range(2)]
        probT = [a.sb(f"a_probT{b}", [B, T]) for b in range(2)]
        bias_s = a.sb("a_bias", [T, D])
        den = a.sb("a_den", [T, NT])
        out = a.sb("a_out", [T, D])
        p_m = [a.ps(f"a_pm{b}", [T, 512]) for b in range(2)]
        p_p = [a.ps(f"a_pp{b}", [B, 512]) for b in range(2)]
        p_o = [a.ps(f"a_po{b}", [T, 512]) for b in range(2)]
        rec_in = [a.sem(f"a_rec_in{b}") for b in range(4)]
        got_in = m.indirect_sems(4)
        (w_in, cleared, marked, turned, scored, prob, prob_turned, prob_copied, summed, shrunk, chain_m, chain_s,
         taken, chain, chain_o) = (
            a.sem("a_" + s) for s in ("w", "cleared", "marked", "turned", "scored", "prob", "prob_turned",
                                      "prob_copied", "summed", "shrunk", "chain_m", "chain_s", "taken", "chain",
                                      "chain_o"))
        block = a.block()

        @block.sync
        def _(sp):
            sp.dma_start(bias_s[:, :], row_to_all(bias, T)).then_inc(w_in, 16)

            def load(k, b):
                q = 4 * k + b
                after(sp, got_in[b], 16 * k)
                sp.sem_inc(m.tick, 1)
                after(sp, marked, q - 3)
                sp.sem_inc(m.tick, 1)
                sp.dma_start(rec[b][:, :], recs[bass.ds(q * B, B), :]).then_inc(rec_in[b], 16)
            pipelined(sp, EB, [(0, load)], 4)

        @block.gpsimd
        def _(pool):
            def gather(k, b):
                q = 4 * k + b
                pool.wait_ge(rec_in[b], 16 * (k + 1))
                after(pool, summed, q - 3)
                pool.sem_inc(m.tick, 1)
                nc.gpsimd.indirect_dma_start(
                    out=got[b][:, :], out_offset=None, in_=table,
                    in_offset=bass.IndirectOffsetOnAxis(ap=rec[b][:, 1:2].bitcast(U32), axis=0)).then_inc(got_in[b], 16)
            pipelined(pool, EB, [(0, gather)], 4)

        @block.vector
        def _(dve):
            link = chained(dve, chain)

            def select(k, b):
                q = 4 * k + b
                c = b % 2
                dve.wait_ge(rec_in[b], 16 * (k + 1))
                dve.wait_ge(got_in[b], 16 * (k + 1))
                after(dve, turned, q - 1)
                step = steps(dve, chain_m, q)
                step(nc.vector.tensor_scalar(mark[c][:, :], m.ramp[:, 0:T], rec[b][:, 0:1], BIG,
                                             ALU.is_equal, ALU.mult))
                nc.vector.tensor_scalar(mark[c][:, :], mark[c][:, :], BIG, got[b][:, D:D + 1],
                                        ALU.subtract, ALU.add).then_inc(marked, 1)

            def score_it(k, b):
                q = 4 * k + b
                c = b % 2
                t = dve.value_load(m.dst_tile[0:1, bass.ds(q, 1)], min_val=0, max_val=NT - 1)
                dve.wait_ge(turned, q + 1)
                after(dve, shrunk, q - 1)
                after(dve, prob_turned, q - 1)
                step = steps(dve, chain_s, 6 * q)
                step(nc.vector.tensor_reduce(top[c][:, 0:1], p_m[c][:, 0:B], AX_X, ALU.max))
                nc.vector.tensor_scalar(score[c][:, :], p_m[c][:, 0:B], m.to[:, bass.ds(t, 1)], None, ALU.add)
                step(nc.vector.tensor_scalar(top[c][:, 0:1], top[c][:, 0:1], m.to[:, bass.ds(t, 1)], None, ALU.add))
                step(nc.vector.scalar_tensor_tensor(out=top[c][:, 1:2], in0=top[c][:, 0:1], scalar=0.2,
                                                    in1=top[c][:, 0:1], op0=ALU.mult, op1=ALU.max))
                step(nc.vector.tensor_scalar(top[c][:, 2:3], top[c][:, 1:2], peak[:, bass.ds(t, 1)], -1.0,
                                             ALU.max, ALU.mult))
                step(nc.vector.tensor_tensor(top[c][:, 3:4], top[c][:, 2:3], peak[:, bass.ds(t, 1)], ALU.add))
                step(nc.vector.tensor_scalar(peak[:, bass.ds(t, 1)], top[c][:, 2:3], -1.0, None, ALU.mult))
                nc.vector.scalar_tensor_tensor(out=score[c][:, :], in0=score[c][:, :], scalar=0.2,
                                               in1=score[c][:, :], op0=ALU.mult, op1=ALU.max).then_inc(scored, 1)

            def take(k, b):
                q = 4 * k + b
                c = b % 2
                t = dve.value_load(m.dst_tile[0:1, bass.ds(q, 1)], min_val=0, max_val=NT - 1)
                dve.wait_ge(summed, q + 1)
                dve.wait_ge(shrunk, q + 1)
                after(dve, taken, q)
                nc.vector.scalar_tensor_tensor(out=tile_of(m.acc, t), in0=tile_of(m.acc, t),
                                               scalar=shrink[b][:, :], in1=p_o[c][:, 0:HC],
                                               op0=ALU.mult, op1=ALU.add).then_inc(taken, 1)
            pipelined(dve, EB, [(4, take), (1, score_it), (0, select)], 4)
            dve.wait_ge(taken, EB)
            dve.wait_ge(w_in, 16)
            link(nc.vector.reciprocal(den[:, :], m.acc[:, :, D + 1]))
            with dve.Fori(0, NT) as t:
                step = steps(dve, chain_o, 2 * t)
                step(nc.vector.scalar_tensor_tensor(out=out[:, :], in0=m.acc[:, bass.ds(t, 1), 0:D].rearrange("p a d -> p (a d)"),
                                                    scalar=den[:, bass.ds(t, 1)], in1=bias_s[:, :],
                                                    op0=ALU.mult, op1=ALU.add))
                step(nc.vector.scalar_tensor_tensor(out=tile_of(m.x, t), in0=out[:, :], scalar=0.0, in1=tile_of(m.x, t),
                                                    op0=ALU.max, op1=ALU.add))

        @block.scalar
        def _(act):
            def weigh(k, b):
                q = 4 * k + b
                c = b % 2
                act.wait_ge(scored, q + 1)
                after(act, taken, q - 3)
                nc.scalar.activation(score[c][:, :], score[c][:, :], ACT.Exp, bias=top[c][:, 2:3]).then_inc(prob, 1)
                nc.scalar.activation(shrink[b][:, :], top[c][:, 3:4], ACT.Exp).then_inc(shrunk, 1)

            def copy(k, b):
                q = 4 * k + b
                act.wait_ge(prob_turned, q + 1)
                after(act, summed, q - 1)
                nc.scalar.copy(probT[b % 2][:, :], p_p[b % 2][:, 0:T]).then_inc(prob_copied, 1)
            pipelined(act, EB, [(2, copy), (1, weigh)], 4)

        @block.tensor
        def _(pe):
            def turn(k, b):
                q = 4 * k + b
                c = b % 2
                pe.wait_ge(marked, q + 1)
                after(pe, scored, q - 1)
                nc.tensor.transpose(p_m[c][0:T, 0:B], mark[c][:, :], m.ident[:, :]).then_inc(turned, 1)

            def turn_prob(k, b):
                q = 4 * k + b
                c = b % 2
                pe.wait_ge(prob, q + 1)
                after(pe, prob_copied, q - 1)
                nc.tensor.transpose(p_p[c][:, 0:T], score[c][:, :], m.ident[0:T, 0:T]).then_inc(prob_turned, 1)

            def gather_sum(k, b):
                q = 4 * k + b
                c = b % 2
                pe.wait_ge(prob_copied, q + 1)
                after(pe, taken, q - 1)
                pe.wait_ge(got_in[b], 16 * (k + 1))
                nc.tensor.matmul(p_o[c][:, 0:HC], probT[c][:, :], got[b][:, :], start=True, stop=True).then_inc(summed, 1)
            pipelined(pe, EB, [(3, gather_sum), (2, turn_prob), (0, turn)], 4)


H1, H2 = 256, 128
X1, X2, NX = 128, 64, 4


def mlp_phase(nc, m, io):
    with ExitStack() as ctx:
        a = Pool_(nc, ctx)
        gw = a.sb("f_gw", [B, 2, NX])
        gb = a.sb("f_gb", [T, NX])
        sw1 = a.sb("f_sw1", [B, 2, H1])
        sb1 = a.sb("f_sb1", [B, 2])
        sw2 = a.sb("f_sw2", [B, 2, H2])
        sb2 = a.sb("f_sb2", [H2, 1])
        sw3 = a.sb("f_sw3", [H2, D])
        sb3 = a.sb("f_sb3", [T, D])
        ew1 = a.sb("f_ew1", [B, NX * 2, X1])
        eb1 = a.sb("f_eb1", [X1, NX])
        ew2 = a.sb("f_ew2", [X1, NX, X2])
        eb2 = a.sb("f_eb2", [X2, NX])
        ew3 = a.sb("f_ew3", [X2 + 1, NX, D])
        ln = [a.sb(f"f_ln{b}", [T, D]) for b in range(2)]
        lnT = [a.sb(f"f_lnT{b}", [B, 2, T]) for b in range(2)]
        gates = [a.sb(f"f_gates{b}", [T, 8]) for b in range(2)]
        top = [a.sb(f"f_top{b}", [T, 8]) for b in range(2)]
        at = [a.sb(f"f_at{b}", [T, 8], U32) for b in range(2)]
        atf = [a.sb(f"f_atf{b}", [T, 2]) for b in range(2)]
        small = [a.sb(f"f_small{b}", [T, 8]) for b in range(2)]
        share = [a.sb(f"f_share{b}", [T, 2 * NX]) for b in range(2)]
        s1 = a.sb("f_s1", [B, 2, T])
        s2 = [a.sb(f"f_s2{b}", [H2, T]) for b in range(2)]
        e1 = [a.sb(f"f_e1{b}", [X1, NX, T]) for b in range(2)]
        e2 = [a.sb(f"f_e2{b}", [X2 + 1, NX, T]) for b in range(2)]
        p_t = a.ps("f_pt", [B, 512])
        p_s = a.ps("f_ps", [B, 512])
        p_e1 = a.ps("f_pe1", [B, 512])
        p_e2 = a.ps("f_pe2", [X2, 512])
        p_s3 = a.ps("f_ps3", [T, 512])
        p_e3 = [a.ps(f"f_pe3{i}", [T, 512]) for i in range(2)]
        (w_in, staged, turned, copied, gated, gate_read, e1_mul, e1_ok, s1_mul, s1_ok, s2_mul, s2_ok, e2_mul, e2_ok,
         out_mul, added, chain_g, chain_a, top_ok, exp_ok, gap_ok, gap_exp, shared_ok, ready, stored) = (
            a.sem("f_" + s) for s in (
                "w", "staged", "turned", "copied", "gated", "gate_read", "e1_mul", "e1_ok", "s1_mul", "s1_ok",
                "s2_mul", "s2_ok", "e2_mul", "e2_ok", "out_mul", "added", "chain_g", "chain_a", "top_ok", "exp_ok",
                "gap_ok", "gap_exp", "shared_ok", "ready", "stored"))
        loads = ((gw[:, :, :], io["L1_ffn_gW"].rearrange("(k p) n -> p k n", p=B)),
                 (gb[:, :], row_to_all(io["L1_ffn_gb"], T)),
                 (sw1[:, :, :], io["L1_ffn_sW1"].rearrange("(k p) n -> p k n", p=B)),
                 (sb1[:, :], io["sb1_cols"]),
                 (sw2[:, :, :], io["L1_ffn_sW2"].rearrange("(k p) n -> p k n", p=B)),
                 (sb2[:, :], io["sb2_cols"]),
                 (sw3[:, :], io["L1_ffn_sW3"]),
                 (sb3[:, :], row_to_all(io["L1_ffn_sb3"], T)),
                 (ew1[:, :, :], io["L1_ffn_eW1"].rearrange("e (k p) n -> p (e k) n", p=B)),
                 (eb1[:, :], io["eb1_cols"]),
                 (ew2[:, :, :], io["L1_ffn_eW2"].rearrange("e p n -> p e n")),
                 (eb2[:, :], io["eb2_cols"]),
                 (ew3[0:X2, :, :], io["L1_ffn_eW3"].rearrange("e p n -> p e n")),
                 (ew3[X2:X2 + 1, :, :], io["L1_ffn_eb3"].rearrange("(a e) n -> a e n", a=1)))
        block = a.block()

        @block.sync
        def _(sp):
            for dst, src in loads:
                sp.dma_start(dst, src).then_inc(w_in, 16)
            sp.wait_ge(added, NT)
            sp.dma_start(io["out"].rearrange("(t p) d -> p t d", p=T), m.x[:, :, :]).then_inc(stored, 16)
            sp.wait_ge(stored, 16)

        @block.gpsimd
        def _(pool):
            def stage(k, b):
                t = 2 * k + b
                after(pool, turned, t - 1)
                nc.gpsimd.tensor_copy(ln[b][:, :], tile_of(m.ln, t)).then_inc(staged, 1)
            pipelined(pool, NT, [(0, stage)])

        @block.tensor
        def _(pe):
            pe.wait_ge(w_in, 16 * len(loads))
            pe.wait_ge(ready, 1)

            def turn(k, b):
                t = 2 * k + b
                pe.wait_ge(staged, t + 1)
                after(pe, gate_read, t)
                for j in range(2):
                    last = nc.tensor.transpose(p_t[:, j * T:(j + 1) * T], ln[b][:, j * B:(j + 1) * B],
                                               m.ident[0:T, 0:T])
                last.then_inc(turned, 1)

            def first(k, b):
                t = 2 * k + b
                pe.wait_ge(copied, t + 1)
                for j in range(2):
                    last = nc.tensor.matmul(p_t[0:T, 256:256 + NX], lnT[b][:, j, :], gw[:, j, :],
                                            start=(j == 0), stop=(j == 1))
                last.then_inc(gated, 1)
                after(pe, s2_ok, t)
                for i in range(2):
                    for j in range(2):
                        last = nc.tensor.matmul(p_s[:, i * T:(i + 1) * T], sw1[:, j, i * B:(i + 1) * B],
                                                lnT[b][:, j, :], start=(j == 0), stop=(j == 1))
                last.then_inc(s1_mul, 1)
                after(pe, e1_ok, t)
                for e in range(NX):
                    for j in range(2):
                        last = nc.tensor.matmul(p_e1[:, e * T:(e + 1) * T], ew1[:, 2 * e + j, :], lnT[b][:, j, :],
                                                start=(j == 0), stop=(j == 1))
                last.then_inc(e1_mul, 1)

            def second(k, b):
                t = 2 * k + b
                pe.wait_ge(s1_ok, t + 1)
                for j in range(2):
                    last = nc.tensor.matmul(p_s[:, 256:256 + T], sw2[:, j, :], s1[:, j, :],
                                            start=(j == 0), stop=(j == 1))
                last.then_inc(s2_mul, 1)
                pe.wait_ge(e1_ok, t + 1)
                after(pe, e2_ok, t)
                for e in range(NX):
                    last = nc.tensor.matmul(p_e2[:, e * T:(e + 1) * T], ew2[:, e, :], e1[b][:, e, :],
                                            start=True, stop=True)
                last.then_inc(e2_mul, 1)

            def third(k, b):
                t = 2 * k + b
                pe.wait_ge(s2_ok, t + 1)
                pe.wait_ge(e2_ok, t + 1)
                after(pe, added, t)
                nc.tensor.matmul(p_s3[:, 0:D], s2[b][:, :], sw3[:, :], start=True, stop=True)
                for e in range(NX):
                    last = nc.tensor.matmul(p_e3[e // 2][:, (e % 2) * D:(e % 2 + 1) * D], e2[b][:, e, :],
                                            ew3[:, e, :], start=True, stop=True)
                last.then_inc(out_mul, 1)
            pipelined(pe, NT, [(3, third), (2, second), (1, first), (0, turn)])

        @block.scalar
        def _(act):
            act.wait_ge(w_in, 16 * len(loads))

            def copy(k, b):
                t = 2 * k + b
                act.wait_ge(turned, t + 1)
                after(act, e1_mul, t - 1)
                nc.scalar.copy(lnT[b][:, :, :].rearrange("p k n -> p (k n)"), p_t[:, 0:2 * T]).then_inc(copied, 1)

            def first(k, b):
                t = 2 * k + b
                act.wait_ge(s1_mul, t + 1)
                after(act, s2_mul, t)
                for i in range(2):
                    last = nc.scalar.activation(s1[:, i, :], p_s[:, i * T:(i + 1) * T], ACT.Relu, bias=sb1[:, i:i + 1])
                last.then_inc(s1_ok, 1)
                act.wait_ge(e1_mul, t + 1)
                after(act, e2_mul, t - 1)
                for e in range(NX):
                    last = nc.scalar.activation(e1[b][:, e, :], p_e1[:, e * T:(e + 1) * T], ACT.Relu,
                                                bias=eb1[:, e:e + 1])
                last.then_inc(e1_ok, 1)

            def second(k, b):
                t = 2 * k + b
                act.wait_ge(s2_mul, t + 1)
                after(act, out_mul, t - 1)
                nc.scalar.activation(s2[b][:, :], p_s[:, 256:256 + T], ACT.Relu, bias=sb2[:, 0:1]).then_inc(s2_ok, 1)
                act.wait_ge(e2_mul, t + 1)
                for e in range(NX):
                    last = nc.scalar.activation(e2[b][0:X2, e, :], p_e2[:, e * T:(e + 1) * T], ACT.Relu,
                                                bias=eb2[:, e:e + 1])
                last.then_inc(e2_ok, 1)

            def gate_exp(k, b):
                t = 2 * k + b
                act.wait_ge(top_ok, t + 1)
                nc.scalar.activation(gates[b][:, 0:NX], gates[b][:, 0:NX], ACT.Exp, bias=small[b][:, 0:1]).then_inc(exp_ok, 1)
                act.wait_ge(gap_ok, t + 1)
                nc.scalar.activation(small[b][:, 3:4], small[b][:, 3:4], ACT.Exp).then_inc(gap_exp, 1)
            pipelined(act, NT, [(2, second), (1, first), (2, gate_exp), (0, copy)])

        @block.vector
        def _(dve):
            for b in range(2):
                nc.vector.memset(gates[b][:, :], -1.0)
                last = nc.vector.memset(e2[b][X2:X2 + 1, :, :], 1.0)
            last.then_inc(ready, 1)
            dve.wait_ge(ready, 1)
            dve.wait_ge(w_in, 16 * len(loads))

            def gate(k, b):
                t = 2 * k + b
                g, s = gates[b], small[b]
                step = steps(dve, chain_g, 13 * t)
                dve.wait_ge(gated, t + 1)
                nc.vector.tensor_tensor(g[:, 0:NX], p_t[0:T, 256:256 + NX], gb[:, :], ALU.add).then_inc(gate_read, 1)
                dve.wait_ge(gate_read, t + 1)
                step(nc.vector.tensor_reduce(s[:, 0:1], g[:, 0:NX], AX_X, ALU.max))
                nc.vector.tensor_scalar(s[:, 0:1], s[:, 0:1], -1.0, None, ALU.mult).then_inc(top_ok, 1)
                dve.wait_ge(exp_ok, t + 1)
                step(nc.vector.tensor_reduce(s[:, 1:2], g[:, 0:NX], AX_X, ALU.add))
                step(nc.vector.reciprocal(s[:, 2:3], s[:, 1:2]))
                step(nc.vector.tensor_scalar(g[:, 0:NX], g[:, 0:NX], s[:, 2:3], None, ALU.mult))
                dve.sem_inc(m.tick, 1)
                step(nc.vector.max(top[b][:, :], g[:, :]))
                dve.sem_inc(m.tick, 1)
                step(nc.vector.max_index(at[b][:, :], top[b][:, :], g[:, :]))
                step(nc.vector.tensor_copy(atf[b][:, :], at[b][:, 0:2]))
                nc.vector.tensor_tensor(s[:, 3:4], top[b][:, 1:2], top[b][:, 0:1], ALU.subtract).then_inc(gap_ok, 1)
                dve.wait_ge(gap_exp, t + 1)
                step(nc.vector.tensor_scalar(s[:, 4:5], s[:, 3:4], 1.0, None, ALU.add))
                step(nc.vector.reciprocal(s[:, 5:6], s[:, 4:5]))
                step(nc.vector.tensor_tensor(s[:, 6:7], s[:, 3:4], s[:, 5:6], ALU.mult))
                step(nc.vector.tensor_scalar(share[b][:, 0:NX], m.ramp[0:T, 0:NX], atf[b][:, 0:1], s[:, 5:6],
                                             ALU.is_equal, ALU.mult))
                step(nc.vector.tensor_scalar(share[b][:, NX:2 * NX], m.ramp[0:T, 0:NX], atf[b][:, 1:2], s[:, 6:7],
                                             ALU.is_equal, ALU.mult))
                step(nc.vector.tensor_tensor(share[b][:, 0:NX], share[b][:, 0:NX], share[b][:, NX:2 * NX], ALU.add))

            def add(k, b):
                t = 2 * k + b
                step = steps(dve, chain_a, (1 + NX) * t)
                dve.wait_ge(out_mul, t + 1)
                step(nc.vector.tensor_tensor(tile_of(m.x, t), tile_of(m.x, t), sb3[:, :], ALU.add))
                step(nc.vector.tensor_tensor(tile_of(m.x, t), tile_of(m.x, t), p_s3[:, 0:D], ALU.add))
                for e in range(NX):
                    ins = nc.vector.scalar_tensor_tensor(
                        out=tile_of(m.x, t), in0=p_e3[e // 2][:, (e % 2) * D:(e % 2 + 1) * D],
                        scalar=share[b][:, e:e + 1], in1=tile_of(m.x, t), op0=ALU.mult, op1=ALU.add)
                    if e < NX - 1:
                        step(ins)
                ins.then_inc(added, 1)
            pipelined(dve, NT, [(3, add), (1, gate)])


class Mem:

    def indirect_sems(self, n):
        first = len(self.kept.sems)
        return [self.kept.sem(f"indirect{first + b}") for b in range(n)]


def build(nc, io):
    m = Mem()
    with ExitStack() as ctx:
        a = Pool_(nc, ctx)
        m.ramp = a.sb("ramp", [B, B])
        m.part = a.sb("part", [B, 4])
        m.ident = a.sb("ident", [B, B])
        m.upper = a.sb("upper", [B, B])
        m.ones = a.sb("ones", [B, B])
        m.x = a.sb("x", [T, NT, D])
        m.src_tile = a.sb("src_tile", [1, EB], I32)
        m.dst_tile = a.sb("dst_tile", [1, EB], I32)
        m.go = a.sem("go")
        m.tick = a.sem("tick")
        m.kept = a
        setup_phase(nc, m)
        with ExitStack() as edges:
            c = Pool_(nc, edges)
            m.src_i = c.sb("src_i", [T, EC], I32)
            m.dst_i = c.sb("dst_i", [T, EC], I32)
            m.src_f = c.sb("src_f", [T, EC])
            m.dst_f = c.sb("dst_f", [T, EC])
            m.src_pos = c.sb("src_pos", [T, EC], I32)
            m.src_local = c.sb("src_local", [T, EC])
            m.dst_pos = c.sb("dst_pos", [T, EC], I32)
            m.dst_local = c.sb("dst_local", [T, EC])
            load_keys(nc, m, io["src"], io["dst"])
            dispatch(nc, m, "ds_", m.src_f[:, :], EC, NT, T, EB, m.src_pos[:, :], m.src_local[:, :],
                     io["src_tile_dram"], m.src_tile[:, :])
            dispatch(nc, m, "dd_", m.dst_f[:, :], EC, NT, T, EB, m.dst_pos[:, :], m.dst_local[:, :],
                     io["dst_tile_dram"], m.dst_tile[:, :])
            fill_records(nc, m, "fs_", io["recs"], REC, EA)
            fill_records(nc, m, "fd_", io["recs2"], 2, 0)
            scatter_records(nc, m, "ss_", io["recs"], m.src_pos, m.src_local, m.dst_i, io["edge_attr_64"])
            scatter_records(nc, m, "sd_", io["recs2"], m.dst_pos, m.dst_local, m.src_i, None)
        with ExitStack() as first:
            c = Pool_(nc, first)
            m.hn = c.sb("hn", [T, NT, D])
            m.a = c.sb("a", [T, NT, D])
            m.acc = c.sb("acc", [T, NT, D + 1])
            node_phase(nc, m, io["x"], io["w1ab"], io["L0_gnn_b1"], io["b_table"])
            message_phase(nc, m, io["recs"], io["b_table"], io["w1c"])
            gru_phase(nc, m, io["gnn_w2"], io["L0_gnn_b2"], io["w_ih"], io["L0_gnn_b_ih"], io["w_hh"],
                      io["L0_gnn_b_hh"])
        with ExitStack() as moe:
            c = Pool_(nc, moe)
            m.expert = c.sb("expert", [T, 2 * NT])
            m.weight = c.sb("weight", [T, 2 * NT])
            m.slot = c.sb("slot", [T, 2 * NT], I32)
            m.block_expert = c.sb("block_expert", [1, MB], I32)
            with ExitStack() as inner:
                d = Pool_(nc, inner)
                m.ln = d.sb("ln", [T, NT, D])
                m.mv = d.sb("mv", [T, NT, 2])
                m.rstd = d.sb("rstd", [T, NT])
                normalize(nc, m, "l1_", m.ln)
                router_phase(nc, m, io["L0_ffn_Wr"], io["L0_ffn_br"])
                dispatch(nc, m, "dm_", m.expert[:, :], 2 * NT, NEX, 1, MB, m.slot[:, :], None,
                         io["expert_dram"], m.block_expert[:, :])
                send_tokens(nc, m, io["tokens"])
            expert_phase(nc, m, io["tokens"], io["answers"], io["L0_ffn_W1"], io["L0_ffn_W2"], io["ln_g_cols"],
                         io["ln_b_cols"], io["b1_cols"], io["b2_row"])
            combine_phase(nc, m, io["answers"])
        m.ln = a.sb("ln2", [T, NT, D])
        with ExitStack() as gat:
            c = Pool_(nc, gat)
            m.to = c.sb("to", [T, NT])
            m.peak = c.sb("peak", [T, NT])
            m.acc = c.sb("acc2", [T, NT, HC])
            normalize(nc, m, "l2_", m.ln)
            attention_rows(nc, m, io["wg"], io["L1_gnn_a_src"], io["L1_gnn_a_dst"], io["table"])
            attention_phase(nc, m, io["recs2"], io["table"], io["L1_gnn_bias"])
        normalize(nc, m, "l3_", m.ln)
        mlp_phase(nc, m, io)


_AS_GIVEN = ["x", "src", "dst", "edge_attr_64", "L0_gnn_b1", "L0_gnn_b2", "L0_gnn_b_ih", "L0_gnn_b_hh", "L0_ffn_Wr",
             "L0_ffn_br", "L0_ffn_W1", "L0_ffn_W2", "L1_gnn_a_src", "L1_gnn_a_dst", "L1_gnn_bias", "L1_ffn_sW1",
             "L1_ffn_sW2", "L1_ffn_sW3", "L1_ffn_sb3", "L1_ffn_eW1", "L1_ffn_eW2", "L1_ffn_eW3", "L1_ffn_eb3",
             "L1_ffn_gW", "L1_ffn_gb"]
_SCRATCH = [("recs", (EB * B, REC), F32), ("recs2", (EB * B, 2), F32), ("b_table", (N, D), F32),
            ("src_tile_dram", (4 * B,), I32), ("dst_tile_dram", (4 * B,), I32), ("expert_dram", (4 * B,), I32),
            ("tokens", (MB * B, D), F32), ("answers", (MB * B, D), F32), ("table", (N, HC), F32)]


def kernel(**inputs):
    import numpy as _np
    import concourse.bacc as _bacc
    from concourse import mybir as _mybir
    from concourse.bass_utils import run_bass_kernel_spmd as _run

    nc = _bacc.Bacc("TRN2", target_bir_lowering=False, num_devices=1)
    given = {k: _np.asarray(v) for k, v in inputs.items()}
    arrays = {k: given[k] for k in _AS_GIVEN}
    w1 = given["L0_gnn_W1"]
    arrays["w1ab"] = _np.concatenate([w1[:, :D].T, w1[:, D:2 * D].T], axis=1)
    arrays["w1c"] = w1[:, 2 * D:].T
    arrays["gnn_w2"] = given["L0_gnn_W2"].T
    arrays["w_ih"] = given["L0_gnn_W_ih"].T
    arrays["w_hh"] = given["L0_gnn_W_hh"].T
    arrays["wg"] = given["L1_gnn_W"].T
    arrays["ln_g_cols"] = given["L0_ffn_ln_g"].reshape(NEX * 2, B).T
    arrays["ln_b_cols"] = given["L0_ffn_ln_b"].reshape(NEX * 2, B).T
    arrays["b1_cols"] = given["L0_ffn_b1"].reshape(NEX * 8, B).T
    arrays["b2_row"] = given["L0_ffn_b2"].reshape(NEX * D)
    arrays["sb1_cols"] = given["L1_ffn_sb1"].reshape(2, B).T
    arrays["sb2_cols"] = given["L1_ffn_sb2"].reshape(1, H2).T
    arrays["eb1_cols"] = given["L1_ffn_eb1"].T
    arrays["eb2_cols"] = given["L1_ffn_eb2"].T
    arrays = {"in_" + k: _np.ascontiguousarray(v) for k, v in arrays.items()}
    io = {k[3:]: nc.dram_tensor(k, v.shape, _mybir.dt.from_np(v.dtype), kind="ExternalInput").ap()
          for k, v in arrays.items()}
    for name, shape, dt in _SCRATCH:
        io[name] = nc.dram_tensor("scratch_" + name, shape, dt, kind="Internal").ap()
    io["out"] = nc.dram_tensor("out", (N, D), F32, kind="ExternalOutput").ap()
    build(nc, io)
    r = _run(nc, [arrays], core_ids=[0])
    return r.results[0]["out"]
```

```python
from contextlib import ExitStack, contextmanager

import concourse.bass as bass
from concourse import mybir

F32 = mybir.dt.float32
BF16 = mybir.dt.bfloat16
I32 = mybir.dt.int32
U32 = mybir.dt.uint32
ALU = mybir.AluOpType
ACT = mybir.ActivationFunctionType
AX_X = mybir.AxisListType.X

N, D = 3125, 256
E = 53125
EA = 64
T = 125
NT = N // T
EC = E // T
B = 128
G = 5
EARLY = 36
REC = EA + 2
EB = (E + (B - 1) * NT) // B
U = 12
EB += -EB % 8
PB = (E + (2 * B - 1) * NT) // (2 * B)
UP = 12
NEX, HID = 8, 1024
TOK2 = 2 * NT
MB = (2 * N + (B - 1) * NEX) // B
MB += MB % 2
EPS = 1e-5
BIG = 1e30
HC = D + 2


def pipelined(eng, n, stages, U=2, row=None):
    most = max(st[0] for st in stages)
    first, end = (most + 2 * U - 1) // U, n // U

    def peeled(s):
        found = {}
        for lag, fn, *top in stages:
            if 0 <= s - lag < n:
                if top and s - lag not in found:
                    found[s - lag] = eng.value_load(row[0:1, s - lag:s - lag + 1], min_val=0, max_val=top[0])
                fn((s - lag) // U, (s - lag) % U, *([found[s - lag]] if top else []))

    if end - first < 2:
        for s in range(n + most):
            peeled(s)
        return
    for s in range(U * first):
        peeled(s)
    looking = [(st[0], st[2]) for st in stages if len(st) > 2]
    with eng.Fori(first, end) as k:
        numbers = []
        if looking:
            back = max(lag for lag, _ in looking)
            back += -back % 4
            ahead = U - min(lag for lag, _ in looking)
            _, numbers = eng.bass.values_load_multi_w_load_instructions(
                row[0:1, bass.ds(k * U - back, back + ahead)], engines=[eng.engine], min_val=0,
                max_val=looking[0][1],
                skip_runtime_bounds_check_because="dispatch has clamped every number of the row to 0..J-1")
        for par in range(U):
            for lag, fn, *top in stages:
                fn(k + (par - lag) // U, (par - lag) % U, *([numbers[back + par - lag]] if top else []))
    for s in range(U * end, n + most):
        peeled(s)


def in_twos(fn):
    return lambda k, b, *number: fn(2 * k + b // 2, b % 2, *number)


def after(eng, sem, count):
    if not isinstance(count, int) or count > 0:
        eng.wait_ge(sem, count)


def held(eng, *values):
    return [v if isinstance(v, int) else eng.snap(v) for v in values]


class Pool_:

    def __init__(self, nc, ctx):
        self.nc, self.ctx, self.sems, self.opened = nc, ctx, [], None

    def sb(self, name, shape, dt=F32):
        return self.ctx.enter_context(self.nc.sbuf_tensor("sb_" + name, shape, dt))

    def ps(self, name, shape, dt=F32):
        return self.ctx.enter_context(self.nc.psum_tensor("ps_" + name, shape, dt))

    def sem(self, name):
        self.sems.append(self.ctx.enter_context(self.nc.semaphore(name)))
        return self.sems[-1]

    def block(self):
        if self.opened is not None:
            return self.opened
        def clear():
            for s in self.sems:
                self.nc.gpsimd.sem_clear(s)
        self.ctx.callback(clear)
        self.opened = self.ctx.enter_context(self.nc.Block())
        return self.opened


@contextmanager
def phase(nc, shared=None):
    if shared is not None:
        yield shared
    else:
        with ExitStack() as ctx:
            yield Pool_(nc, ctx)


def chained(eng, sem):
    count = [0]

    def link(ins):
        count[0] += 1
        ins.then_inc(sem, 1)
        eng.wait_ge(sem, count[0])
    return link


def setup_phase(nc, m, shared=None):
    with phase(nc, shared) as a:
        ramp_i = a.sb("ramp_i", [B, B], I32)
        part_i = a.sb("part_i", [B, 4], I32)
        ramped = a.sem("ramped")
        chain = a.sem("setup_chain")
        block = a.block()

        @block.gpsimd
        def _(pool):
            nc.gpsimd.iota(ramp_i[:, :], pattern=[[1, B]], base=0, channel_multiplier=0).then_inc(ramped, 1)
            nc.gpsimd.iota(part_i[:, :], pattern=[[B, 4]], base=0, channel_multiplier=1).then_inc(ramped, 1)

        @block.vector
        def _(dve):
            link = chained(dve, chain)
            dve.wait_ge(ramped, 2)
            link(nc.vector.tensor_copy(m.ramp[:, :], ramp_i[:, :]))
            link(nc.vector.tensor_copy(m.part[:, :], part_i[:, :]))
            link(nc.vector.tensor_scalar(m.ident[:, :], m.ramp[:, :], m.part[:, 0:1], None, ALU.is_equal))
            link(nc.vector.tensor_copy(m.ident_b[:, :], m.ident[:, :]))
            link(nc.vector.tensor_scalar(m.upper[:, :], m.ramp[:, :], m.part[:, 0:1], None, ALU.is_gt))
            nc.vector.memset(m.ones[:, :], 1.0).then_inc(m.go, 1)


def dispatch(nc, m, name, key, C, J, width, blocks, pos_i, local, bucket_dram, bucket_row, unit, shared=None):
    with phase(nc, shared) as a:
        ge = a.sb(name + "ge", [T, J + 1, C], BF16)
        oh = ge[:, 0:J, :]
        always = a.sb(name + "always", [T, 1], BF16)
        scan = a.sb(name + "scan", [T, J, C])
        cum = a.sb(name + "cum", [T, J + 1])
        count = a.sb(name + "count", [T, J])
        base = a.sb(name + "base", [T, J])
        posf = a.sb(name + "posf", [T, C])
        total = a.sb(name + "total", [B, J])
        total_i = a.sb(name + "total_i", [B, J], I32)
        nblk = a.sb(name + "nblk", [B, J])
        end = a.sb(name + "end", [B, J])
        one = a.sb(name + "one", [B, J])
        past = a.sb(name + "past", [B, 4, J])
        bkt = a.sb(name + "bkt", [B, 4])
        bkt_i = a.sb(name + "bkt_i", [B, 4], I32)
        p_before = a.ps(name + "p_before", [T, 512])
        p_total = a.ps(name + "p_total", [B, 512])
        counted = a.sem(name + "counted")
        summed = a.sem(name + "summed")
        bucketed = a.sem(name + "bucketed")
        stored = a.sem(name + "stored")
        chain = a.sem(name + "chain")
        block = a.block()

        @block.vector
        def _(dve):
            link = chained(dve, chain)
            for j in range(J + 1):
                last = nc.vector.tensor_scalar(ge[:, j, :], key, float(width * j), None, ALU.is_ge)
            link(last)
            nc.vector.memset(one[:, :], 1.0)
            link(nc.vector.memset(cum[:, 0:1], 0.0))
            nc.vector.memset(always[:, :], 1.0)
            if local is not None:
                link(nc.vector.tensor_reduce(posf[:, :], ge[:, 1:J, :].rearrange("p j c -> p c j"), AX_X, ALU.add))
                link(nc.vector.scalar_tensor_tensor(out=local, in0=posf[:, :], scalar=-float(width), in1=key,
                                                    op0=ALU.mult, op1=ALU.add))
            link(nc.vector.tensor_tensor(oh, ge[:, 0:J, :], ge[:, 1:J + 1, :], ALU.subtract))
            flat = "p j c -> p (j c)"
            link(nc.vector.tensor_tensor_scan(scan[:, :, :].rearrange(flat), always[:, :].to_broadcast([T, J * C]),
                                              oh.rearrange(flat), 0.0, ALU.mult, ALU.add))
            link(nc.vector.tensor_copy(cum[:, 1:J + 1], scan[:, :, C - 1]))
            nc.vector.tensor_tensor(count[:, :], cum[:, 1:J + 1], cum[:, 0:J], ALU.subtract).then_inc(counted, 1)
            dve.wait_ge(summed, 1)
            link(nc.vector.tensor_scalar(total_i[:, :], p_total[:, 0:J], float(unit - 1), None, ALU.add))
            link(nc.vector.tensor_scalar(total_i[:, :], total_i[:, :], unit.bit_length() - 1, None,
                                         ALU.arith_shift_right))
            link(nc.vector.tensor_copy(nblk[:, :], total_i[:, :]))
            link(nc.vector.tensor_tensor_scan(end[:, :], one[:, :], nblk[:, :], 0.0, ALU.mult, ALU.add))
            for i in range(4):
                last = nc.vector.tensor_scalar(past[:, i, :], end[:, :], m.part[:, i:i + 1], None, ALU.is_le)
            link(last)
            link(nc.vector.tensor_reduce(bkt[:, :], past[:, :, :], AX_X, ALU.add))
            nc.vector.tensor_scalar(bkt_i[:, :], bkt[:, :], float(J - 1), None, ALU.min).then_inc(bucketed, 1)
            link(nc.vector.tensor_tensor(total[:, :], end[:, :], nblk[:, :], ALU.subtract))
            link(nc.vector.scalar_tensor_tensor(out=base[:, :], in0=total[0:T, :], scalar=float(unit),
                                                in1=cum[:, 0:J], op0=ALU.mult, op1=ALU.subtract))
            link(nc.vector.scalar_tensor_tensor(out=base[:, :], in0=base[:, :], scalar=-1.0,
                                                in1=p_before[:, 0:J], op0=ALU.add, op1=ALU.add))
            for j in range(J):
                last = nc.vector.scalar_tensor_tensor(out=scan[:, j, :], in0=scan[:, j, :],
                                                      scalar=base[:, j:j + 1], in1=oh[:, j, :],
                                                      op0=ALU.add, op1=ALU.mult)
            link(last)
            link(nc.vector.tensor_reduce(posf[:, :], scan[:, :, :].rearrange("p j c -> p c j"), AX_X, ALU.add))
            link(nc.vector.tensor_copy(pos_i, posf[:, :]))

        @block.tensor
        def _(pe):
            pe.wait_ge(counted, 1)
            nc.tensor.matmul(p_before[:, 0:J], m.upper[0:T, 0:T], count[:, :], start=True, stop=True)
            nc.tensor.matmul(p_total[:, 0:J], m.ones[0:T, 0:B], count[:, :], start=True, stop=True).then_inc(summed, 1)

        @block.sync
        def _(sp):
            sp.wait_ge(bucketed, 1)
            with nc.allow_non_contiguous_dma(reason="a few hundred block numbers"):
                sp.dma_start(bucket_dram.rearrange("(i p) -> p i", p=B), bkt_i[:, :]).then_inc(stored, 16)
            sp.wait_ge(stored, 16)
            sp.dma_start(bucket_row, bucket_dram.rearrange("(a n) -> a n", a=1)[:, 0:blocks]).then_inc(stored, 16)
            sp.wait_ge(stored, 32)


def load_keys(nc, m, src, dst, shared=None):
    with phase(nc, shared) as a:
        loaded = a.sem("keys_loaded")
        chain = a.sem("keys_chain")
        block = a.block()

        @block.sync
        def _(sp):
            sp.dma_start(m.src_i[:, :], src.rearrange("(p c) -> p c", p=T)).then_inc(loaded, 16)
            sp.dma_start(m.dst_i[:, :], dst.rearrange("(p c) -> p c", p=T)).then_inc(loaded, 16)

        @block.vector
        def _(dve):
            link = chained(dve, chain)
            dve.wait_ge(loaded, 32)
            link(nc.vector.tensor_copy(m.src_f[:, :], m.src_i[:, :]))
            link(nc.vector.tensor_copy(m.dst_f[:, :], m.dst_i[:, :]))


def fill_records(nc, m, name, recs, cols, key_col, shared=None):
    per = recs.shape[0] // B
    some = max(n for n in range(1, 41) if per % n == 0)
    with phase(nc, shared) as a:
        blank = a.sb(name + "blank", [B, some, cols])
        cleared = a.sem(name + "cleared")
        filled = a.sem(name + "filled")
        block = a.block()
        view = recs.rearrange("(p r) c -> p r c", p=B)

        @block.vector
        def _(dve):
            nc.vector.memset(blank[:, :, :], 0.0).then_inc(cleared, 1)
            dve.wait_ge(cleared, 1)
            nc.vector.memset(blank[:, :, key_col:key_col + 1], -1.0).then_inc(cleared, 1)

        @block.sync
        def _(sp):
            sp.wait_ge(cleared, 2)
            with sp.Fori(0, per // some) as i:
                sp.dma_start(view[:, bass.ds(i * some, some), :], blank[:, :, :]).then_inc(filled, 16)
            sp.wait_ge(filled, 16 * (per // some))


def scatter_records(nc, m, name, recs, pos_i, local, other_i, attrs, shared=None, first=0, last=EC // G):
    W = recs.shape[1]
    groups = last - first
    with phase(nc, shared) as a:
        rec = [a.sb(f"{name}rec{b}", [T, G, W]) for b in range(2)]
        pos = [a.sb(f"{name}pos{b}", [T, G], I32) for b in range(2)]
        attr_in = [a.sem(f"{name}attr_in{b}") for b in range(2)]
        built = a.sem(name + "built")
        sent = m.indirect_sems(2)
        block = a.block()

        if attrs is not None:
            view = attrs.rearrange("(p c) a -> p c a", p=T)

            @block.sync
            def _(sp):
                def load(k, b):
                    after(sp, sent[b], 16 * G * k)
                    sp.dma_start(rec[b][:, :, 0:EA], view[:, bass.ds((first + 2 * k + b) * G, G), :]).then_inc(attr_in[b], 16)
                pipelined(sp, groups, [(0, load)])

        @block.gpsimd
        def _(pool):
            def build(k, b):
                c = bass.ds((first + 2 * k + b) * G, G)
                after(pool, sent[b], 16 * G * k)
                pool.sem_inc(m.tick, 1)
                nc.gpsimd.tensor_copy(rec[b][:, :, W - 2], local[:, c])
                nc.gpsimd.tensor_copy(rec[b][:, :, W - 1].bitcast(I32), other_i[:, c])
                nc.gpsimd.tensor_copy(pos[b][:, :], pos_i[:, c]).then_inc(built, 1)

            def scatter(k, b):
                pool.wait_ge(built, 2 * k + b + 1)
                if attrs is not None:
                    pool.wait_ge(attr_in[b], 16 * (k + 1))
                pool.sem_inc(m.tick, 1)
                for g in range(G):
                    nc.gpsimd.indirect_dma_start(
                        out=recs, out_offset=bass.IndirectOffsetOnAxis(ap=pos[b][:, g:g + 1].bitcast(U32), axis=0),
                        in_=rec[b][:, g, :], in_offset=None).then_inc(sent[b], 16)
            pipelined(pool, groups, [(1, scatter), (0, build)])
            for b in range(2):
                pool.wait_ge(sent[b], 16 * G * ((groups + 1 - b) // 2))


def ln_stats(nc, dve, link, act_sem, sqrt_sem, n, src, mv, stats, stat_sem, rstd):
    with dve.Fori(0, NT // 5) as k:
        for i in range(5):
            nc.vector.bn_stats(stats[:, bass.ds(k * 5 + i, 1), :].rearrange("p a s -> p (a s)"),
                               src(k * 5 + i)).then_inc(stat_sem, 1)
    dve.wait_ge(stat_sem, 2 * NT * n + NT)
    for t in range(NT):
        last = nc.vector.bn_aggr(mv[:, t, :], stats[:, t, :])
    last.then_inc(stat_sem, NT)
    dve.wait_ge(stat_sem, 2 * NT * (n + 1))
    nc.vector.tensor_scalar(rstd[:, :], mv[:, :, 1], EPS, None, ALU.add).then_inc(act_sem, 1)
    dve.wait_ge(sqrt_sem, n + 1)
    link(nc.vector.reciprocal(rstd[:, :], rstd[:, :]))


def ln_root(nc, act, act_sem, sqrt_sem, n, rstd):
    act.wait_ge(act_sem, n + 1)
    nc.scalar.activation(rstd[:, :], rstd[:, :], ACT.Sqrt).then_inc(sqrt_sem, 1)


def tile_of(x, t):
    return x[:, bass.ds(t, 1), :].rearrange("p a d -> p (a d)")


def node_phase(nc, m, x, w1ab, b1, b_table, shared=None):
    with phase(nc, shared) as a:
        w = a.sb("w1ab", [B, 2, 2 * D])
        bias = a.sb("b1_all", [T, D])
        stats = a.sb("n_stats", [T, NT, 6])
        mv = a.sb("n_mv", [T, NT, 2])
        rstd = a.sb("n_rstd", [T, NT])
        left = a.sb("n_left", [T, D])
        rows = [a.sb(f"b_rows{b}", [T, D]) for b in range(2)]
        hT = [a.sb(f"n_hT{b}", [B, 2, T]) for b in range(2)]
        p_t = [a.ps(f"n_pt{b}", [B, 512]) for b in range(2)]
        p_ab = [a.ps(f"n_pab{b}", [T, 512]) for b in range(2)]
        x_in, w_in, stat, var_ok, rooted, chain = (a.sem("n_" + s) for s in ("x_in", "w_in", "stat", "var", "root", "ch"))
        hn = [a.sb(f"n_hn{b}", [T, D]) for b in range(2)]
        kept, parts = a.sem("n_kept"), a.sem("n_parts")
        normed, turned, copied, multiplied, split = (a.sem("n_" + s) for s in ("normed", "turned", "copied", "mul", "split"))
        stored = [a.sem(f"n_stored{b}") for b in range(2)]
        block = a.block()

        @block.scalar
        def _(act):
            act.dma_start(m.x[:, :, :], x.rearrange("(t p) d -> p t d", p=T)).then_inc(x_in, 16)
            act.dma_start(w[:, :, :], w1ab.rearrange("(k p) n -> p k n", p=B)).then_inc(w_in, 16)
            act.dma_start(bias[:, :], b1.rearrange("(a d) -> a d", a=1).to_broadcast([T, D])).then_inc(w_in, 16)

        @block.vector
        def _(dve):
            link = chained(dve, chain)
            dve.wait_ge(x_in, 16)
            ln_stats(nc, dve, link, var_ok, rooted, 0, lambda t: tile_of(m.x, t), mv, stats, stat, rstd)
            dve.wait_ge(w_in, 32)

            def norm(k, b):
                t = 2 * k + b
                after(dve, turned, t - 1)
                after(dve, kept, t - 1)
                nc.vector.tensor_scalar(hn[b][:, :], tile_of(m.x, t), mv[:, bass.ds(t, 1), 0],
                                        rstd[:, bass.ds(t, 1)], ALU.subtract, ALU.mult).then_inc(normed, 1)

            def spread(k, b):
                t = 2 * k + b
                dve.wait_ge(multiplied, t + 1)
                after(dve, stored[b], 16 * k)
                step = steps(dve, parts, 3 * t)
                high, middle, low = (tile_of(m.a, t)[:, i * D:(i + 1) * D] for i in range(3))
                step(nc.vector.tensor_copy(high, p_ab[b][:, 0:D]))
                step(nc.vector.tensor_tensor(left[:, :], p_ab[b][:, 0:D], high, ALU.subtract))
                step(nc.vector.tensor_copy(middle, left[:, :]))
                nc.vector.tensor_tensor(low, left[:, :], middle, ALU.subtract)
                nc.vector.tensor_tensor(rows[b][:, :], p_ab[b][:, D:2 * D], bias[:, :], ALU.add).then_inc(split, 1)
            pipelined(dve, NT, [(0, norm), (2, spread)])

        @block.scalar
        def _(act):
            ln_root(nc, act, var_ok, rooted, 0, rstd)

            def keep(k, b):
                act.wait_ge(normed, 2 * k + b + 1)
                nc.scalar.copy(tile_of(m.hn, 2 * k + b), hn[b][:, :]).then_inc(kept, 1)

            def copy(k, b):
                t = 2 * k + b
                act.wait_ge(turned, t + 1)
                after(act, multiplied, t - 1)
                nc.scalar.copy(hT[b][:, :, :].rearrange("p k n -> p (k n)"), p_t[b][:, 0:2 * T]).then_inc(copied, 1)

            def store(k, b):
                t = 2 * k + b
                act.wait_ge(split, t + 1)
                act.dma_start(b_table[bass.ds(t * T, T), :], rows[b][:, :]).then_inc(stored[b], 16)
            pipelined(act, NT, [(3, store), (0, keep), (0, copy)])
            for b in range(2):
                act.wait_ge(stored[b], 16 * ((NT + 1 - b) // 2))

        @block.tensor
        def _(pe):
            pe.wait_ge(w_in, 32)

            def turn(k, b):
                t = 2 * k + b
                pe.wait_ge(normed, t + 1)
                after(pe, copied, t - 1)
                for j in range(2):
                    last = nc.tensor.transpose(p_t[b][:, j * T:(j + 1) * T],
                                               hn[b][:, j * B:(j + 1) * B],
                                               m.ident[0:T, 0:T])
                last.then_inc(turned, 1)

            def multiply(k, b):
                t = 2 * k + b
                pe.wait_ge(copied, t + 1)
                after(pe, split, t - 1)
                for j in range(2):
                    last = nc.tensor.matmul(p_ab[b][:, :], hT[b][:, j, :], w[:, j, :], start=(j == 0), stop=(j == 1))
                last.then_inc(multiplied, 1)
            pipelined(pe, NT, [(0, turn), (1, multiply)])


def message_phase(nc, m, recs, b_table, w1c, shared=None):
    with phase(nc, shared) as a:
        w = a.sb("w1c", [EA, D])
        rec = [a.sb(f"m_rec{b}", [B, REC]) for b in range(U)]
        got = [a.sb(f"m_got{b}", [B, D]) for b in range(U)]
        oh = [a.sb(f"m_oh{b}", [B, T]) for b in range(U)]
        oh_b = [a.sb(f"m_oh_b{b}", [B, T], BF16) for b in range(4)]
        attrT = [a.sb(f"m_attrT{b}", [EA, B]) for b in range(4)]
        ohT = [a.sb(f"m_ohT{b}", [T, B], BF16) for b in range(4)]
        msg = [a.sb(f"m_msg{b}", [B, D + 1]) for b in range(4)]
        p_t = [a.ps(f"m_pt{b}", [B, 512]) for b in range(2)]
        p_oh = [a.ps(f"m_poh{b}", [T, 1024], BF16) for b in range(2)]
        p_pre = [a.ps(f"m_pre{b}", [B, 512]) for b in range(2)]
        p_seg = [a.ps(f"m_seg{b}", [T, 512]) for b in range(2)]
        w_in = a.sem("m_w_in")
        rec_in = [a.sem(f"m_rec_in{b}") for b in range(U)]
        got_in = m.indirect_sems(U)
        marked, turned, copied, pre, added, relued, summed, taken, cleared = (
            a.sem("m_" + s) for s in ("marked", "turned", "copied", "pre", "added", "relued", "summed", "taken", "cleared"))
        block = a.block()

        @block.sync
        def _(sp):
            sp.dma_start(w[:, :], w1c).then_inc(w_in, 16)

            def load(k, b):
                q = U * k + b
                after(sp, got_in[b], 16 * k)
                sp.sem_inc(m.tick, 1)
                after(sp, turned, q - U + 1)
                sp.sem_inc(m.tick, 1)
                sp.dma_start(rec[b][:, :], recs[bass.ds(q * B, B), :]).then_inc(rec_in[b], 16)
            pipelined(sp, EB, [(0, load)], U)

        @block.gpsimd
        def _(pool):
            def gather(k, b):
                q = U * k + b
                pool.wait_ge(rec_in[b], 16 * (k + 1))
                after(pool, added, q - U + 1)
                pool.sem_inc(m.tick, 1)
                nc.gpsimd.indirect_dma_start(
                    out=got[b][:, :], out_offset=None, in_=b_table,
                    in_offset=bass.IndirectOffsetOnAxis(ap=rec[b][:, EA + 1:EA + 2].bitcast(U32), axis=0)
                ).then_inc(got_in[b], 16)
            pipelined(pool, EB, [(0, gather)], U)

        @block.vector
        def _(dve):
            for b in range(4):
                nc.vector.memset(msg[b][:, D:D + 1], 1.0)
            nc.vector.memset(m.acc[:, :, :], 0.0).then_inc(cleared, 1)
            dve.wait_ge(cleared, 1)

            def mark(k, b):
                q = U * k + b
                dve.wait_ge(rec_in[b], 16 * (k + 1))
                after(dve, summed, q - U + 1)
                after(dve, turned, q - 3)
                nc.vector.tensor_scalar(oh_b[b % 4][:, :], m.ramp[:, 0:T], rec[b][:, EA:EA + 1], None, ALU.is_equal)
                nc.vector.tensor_scalar(oh[b][:, :], m.ramp[:, 0:T], rec[b][:, EA:EA + 1], None,
                                        ALU.is_equal).then_inc(marked, 1)

            def add(k, b):
                q = U * k + b
                dve.wait_ge(pre, q + 1)
                dve.wait_ge(got_in[b], 16 * (k + 1))
                after(dve, summed, q - 3)
                nc.vector.tensor_tensor(msg[b % 4][:, 0:D], p_pre[b % 2][:, 0:D], got[b][:, :], ALU.add).then_inc(added, 1)

            def take(k, b, t):
                q = U * k + b
                dve.wait_ge(summed, q + 1)
                after(dve, taken, q)
                nc.vector.tensor_tensor(tile_of(m.acc, t), tile_of(m.acc, t), p_seg[b % 2][:, 0:D + 1],
                                        ALU.add).then_inc(taken, 1)
            pipelined(dve, EB, [(7, take, NT - 1), (4, add), (0, mark)], U, m.src_tile)

        @block.scalar
        def _(act):
            def copy(k, b):
                q = U * k + b
                act.wait_ge(turned, q + 1)
                after(act, pre, q - 3)
                nc.scalar.copy(attrT[b % 4][:, :], p_t[b % 2][0:EA, 0:B])
                nc.scalar.copy(ohT[b % 4][:, :], p_oh[b % 2][:, 0:B]).then_inc(copied, 1)

            def relu(k, b):
                q = U * k + b
                act.wait_ge(added, q + 1)
                nc.scalar.activation(msg[b % 4][:, 0:D], msg[b % 4][:, 0:D], ACT.Relu).then_inc(relued, 1)
            pipelined(act, EB, [(5, relu), (2, copy)], U)

        @block.tensor
        def _(pe):
            pe.wait_ge(w_in, 16)
            pe.wait_ge(cleared, 1)

            def turn(k, b):
                q = U * k + b
                pe.wait_ge(marked, q + 1)
                pe.wait_ge(rec_in[b], 16 * (k + 1))
                after(pe, copied, q - 1)
                nc.tensor.transpose(p_t[b % 2][0:REC, 0:B], rec[b][:, :], m.ident[:, :])
                nc.tensor.transpose(p_oh[b % 2][:, 0:B], oh_b[b % 4][:, :], m.ident_b[:, :]).then_inc(turned, 1)

            def sum_up(k, b, t):
                q = U * k + b
                pe.wait_ge(copied, q + 1)
                after(pe, added, q - 1)
                nc.tensor.matmul(p_pre[b % 2][:, 0:D], attrT[b % 4][:, :], w[:, :], start=True, stop=False)
                for i in range(3):
                    last = nc.tensor.matmul(p_pre[b % 2][:, 0:D], ohT[b % 4][:, :],
                                            tile_of(m.a, t)[:, i * D:(i + 1) * D], start=False, stop=(i == 2))
                last.then_inc(pre, 1)

            def segment(k, b):
                q = U * k + b
                pe.wait_ge(relued, q + 1)
                after(pe, taken, q - 1)
                nc.tensor.matmul(p_seg[b % 2][:, 0:D + 1], oh[b][:, :], msg[b % 4][:, :], start=True, stop=True).then_inc(summed, 1)
            pipelined(pe, EB, [(6, segment), (3, sum_up, NT - 1), (1, turn)], U, m.src_tile)


def steps(eng, sem, start):
    count = [0]

    def step(ins):
        count[0] += 1
        ins.then_inc(sem, 1)
        eng.wait_ge(sem, start + count[0])
    return step


def row_to_all(v, rows):
    return v.rearrange("(a d) -> a d", a=1).to_broadcast([rows, v.shape[0]])


def gru_phase(nc, m, w2, b2, w_ih, b_ih, w_hh, b_hh, shared=None):
    with phase(nc, shared) as a:
        w2s = a.sb("g_w2", [B, 2, D])
        wih = a.sb("g_wih", [B, 2, 3 * D])
        whh = a.sb("g_whh", [B, 2, 3 * D])
        b2s = a.sb("g_b2", [T, D])
        bih = a.sb("g_bih", [T, 3 * D])
        bhh = a.sb("g_bhh", [T, 3 * D])
        sums = [a.sb(f"g_sums{b}", [T, D + 1]) for b in range(2)]
        hid = [a.sb(f"g_hid{b}", [T, D]) for b in range(2)]
        shT = [a.sb(f"g_shT{b}", [B, 4, T]) for b in range(4)]
        agg = [a.sb(f"g_agg{b}", [T, D]) for b in range(2)]
        aggT = [a.sb(f"g_aggT{b}", [B, 2, T]) for b in range(2)]
        rz = [a.sb(f"g_rz{b}", [T, 2 * D]) for b in range(2)]
        cand = [a.sb(f"g_cand{b}", [T, D]) for b in range(2)]
        part = a.sb("g_part", [T, D])
        p_sh = a.ps("g_psh", [B, 512])
        p_agg = a.ps("g_pagg", [T, 512])
        p_aggT = a.ps("g_paggT", [B, 512])
        p_rz = [a.ps(f"g_prz{b}", [T, 512]) for b in range(2)]
        p_n = [a.ps(f"g_pn{b}", [T, 512]) for b in range(2)]
        w_in = a.sem("g_w_in")
        bias_ok = a.sem("g_bias_ok")
        (staged, turned, copied, agg_mul, agg_done, agg_turned, agg_copied, gates, preact, opened, pre_n, squashed,
         mixed, chain_n, chain_x) = (a.sem("g_" + s) for s in (
             "staged", "turned", "copied", "agg_mul", "agg_done", "agg_turned", "agg_copied", "gates", "preact",
             "opened", "pre_n", "squashed", "mixed", "chain_n", "chain_x"))
        block = a.block()

        @block.sync
        def _(sp):
            for dst, src in ((w2s, w2), (wih, w_ih), (whh, w_hh)):
                sp.dma_start(dst[:, :, :], src.rearrange("(k p) n -> p k n", p=B)).then_inc(w_in, 16)
            for dst, src in ((b2s, b2), (bih, b_ih), (bhh, b_hh)):
                sp.dma_start(dst[:, :], row_to_all(src, T)).then_inc(w_in, 16)

        @block.tensor
        def _(pe):
            pe.wait_ge(w_in, 96)

            def turn(k, b):
                t = 2 * k + b
                pe.wait_ge(staged, t + 1)
                after(pe, copied, t)
                for j in range(2):
                    nc.tensor.transpose(p_sh[:, j * T:(j + 1) * T], sums[b][:, j * B:(j + 1) * B], m.ident[0:T, 0:T])
                for j in range(2):
                    last = nc.tensor.transpose(p_sh[:, (2 + j) * T:(3 + j) * T], hid[b][:, j * B:(j + 1) * B],
                                               m.ident[0:T, 0:T])
                last.then_inc(turned, 1)

            def aggregate(k, b):
                t = 4 * k + b
                pe.wait_ge(copied, t + 1)
                after(pe, agg_done, t)
                for j in range(2):
                    last = nc.tensor.matmul(p_agg[:, 0:D], shT[b][:, j, :], w2s[:, j, :], start=(j == 0), stop=(j == 1))
                last.then_inc(agg_mul, 1)

            def turn_agg(k, b):
                t = 4 * k + b
                pe.wait_ge(agg_done, t + 1)
                after(pe, agg_copied, t)
                for j in range(2):
                    last = nc.tensor.transpose(p_aggT[:, j * T:(j + 1) * T], agg[b % 2][:, j * B:(j + 1) * B],
                                               m.ident[0:T, 0:T])
                last.then_inc(agg_turned, 1)

            def gate(k, b):
                t = 4 * k + b
                pe.wait_ge(agg_copied, t + 1)
                after(pe, preact, t - 1)
                after(pe, pre_n, t - 1)
                c = b % 2
                for j in range(2):
                    nc.tensor.matmul(p_rz[c][:, :], aggT[c][:, j, :], wih[:, j, 0:2 * D], start=(j == 0), stop=False)
                for j in range(2):
                    nc.tensor.matmul(p_rz[c][:, :], shT[b][:, 2 + j, :], whh[:, j, 0:2 * D], start=False, stop=(j == 1))
                for j in range(2):
                    nc.tensor.matmul(p_n[c][:, 0:D], aggT[c][:, j, :], wih[:, j, 2 * D:], start=(j == 0), stop=(j == 1))
                for j in range(2):
                    last = nc.tensor.matmul(p_n[c][:, D:2 * D], shT[b][:, 2 + j, :], whh[:, j, 2 * D:],
                                            start=(j == 0), stop=(j == 1))
                last.then_inc(gates, 1)
            pipelined(pe, NT, [(3, turn_agg), (2, aggregate), (1, in_twos(turn)), (4, gate)], 4)

        @block.scalar
        def _(act):
            def stage(k, b):
                t = 2 * k + b
                after(act, turned, t - 1)
                after(act, agg_done, t - 1)
                nc.scalar.copy(sums[b][:, :], tile_of(m.acc, t))
                nc.scalar.copy(hid[b][:, :], tile_of(m.hn, t)).then_inc(staged, 1)

            def copy(k, b):
                t = 4 * k + b
                act.wait_ge(turned, t + 1)
                after(act, gates, t - 3)
                nc.scalar.copy(shT[b][:, :, :].rearrange("p k n -> p (k n)"), p_sh[:, 0:4 * T]).then_inc(copied, 1)

            def copy_agg(k, b):
                t = 4 * k + b
                act.wait_ge(agg_turned, t + 1)
                after(act, gates, t - 1)
                nc.scalar.copy(aggT[b % 2][:, :, :].rearrange("p k n -> p (k n)"), p_aggT[:, 0:2 * T]).then_inc(agg_copied, 1)

            def open_gates(k, b):
                t = 4 * k + b
                act.wait_ge(preact, t + 1)
                nc.scalar.activation(rz[b % 2][:, :], rz[b % 2][:, :], ACT.Sigmoid).then_inc(opened, 1)

            def squash(k, b):
                t = 4 * k + b
                act.wait_ge(pre_n, t + 1)
                nc.scalar.activation(cand[b % 2][:, :], cand[b % 2][:, :], ACT.Tanh).then_inc(squashed, 1)
            pipelined(act, NT, [(3, copy_agg), (1, copy), (5, open_gates), (5, squash), (0, in_twos(stage))], 4)

        @block.vector
        def _(dve):
            dve.wait_ge(w_in, 96)
            nc.vector.tensor_tensor(bih[:, 0:2 * D], bih[:, 0:2 * D], bhh[:, 0:2 * D], ALU.add).then_inc(bias_ok, 1)
            dve.wait_ge(bias_ok, 1)

            def biased(k, b):
                t = 4 * k + b
                dve.wait_ge(agg_mul, t + 1)
                after(dve, agg_turned, t - 1)
                nc.vector.scalar_tensor_tensor(out=agg[b % 2][:, :], in0=b2s[:, :], scalar=sums[b % 2][:, D:D + 1],
                                               in1=p_agg[:, 0:D], op0=ALU.mult, op1=ALU.add).then_inc(agg_done, 1)

            def pre(k, b):
                t = 4 * k + b
                c = b % 2
                step = steps(dve, chain_n, 3 * t)
                dve.wait_ge(gates, t + 1)
                after(dve, mixed, t - 1)
                nc.vector.tensor_tensor(rz[c][:, :], p_rz[c][:, :], bih[:, 0:2 * D], ALU.add).then_inc(preact, 1)
                step(nc.vector.tensor_tensor(cand[c][:, :], p_n[c][:, D:2 * D], bhh[:, 2 * D:], ALU.add))

            def pre_new(k, b):
                t = 4 * k + b
                c = b % 2
                step = steps(dve, chain_n, 3 * t + 1)
                dve.wait_ge(opened, t + 1)
                step(nc.vector.tensor_tensor(cand[c][:, :], cand[c][:, :], rz[c][:, 0:D], ALU.mult))
                step(nc.vector.tensor_tensor(cand[c][:, :], cand[c][:, :], bih[:, 2 * D:], ALU.add))
                nc.vector.tensor_tensor(cand[c][:, :], cand[c][:, :], p_n[c][:, 0:D], ALU.add).then_inc(pre_n, 1)

            def mix(k, b):
                t = 4 * k + b
                c = b % 2
                step = steps(dve, chain_x, 4 * t)
                dve.wait_ge(squashed, t + 1)
                step(nc.vector.tensor_tensor(part[:, :], tile_of(m.hn, t), cand[c][:, :], ALU.subtract))
                step(nc.vector.tensor_tensor(part[:, :], part[:, :], rz[c][:, D:2 * D], ALU.mult))
                step(nc.vector.tensor_tensor(part[:, :], part[:, :], cand[c][:, :], ALU.add))
                step(nc.vector.tensor_tensor(tile_of(m.x, t), tile_of(m.x, t), part[:, :], ALU.add))
                dve.sem_inc(mixed, 1)
            pipelined(dve, NT, [(1, biased), (4, pre), (5, mix), (4, pre_new)], 4)


def normalize(nc, m, name, dst, shared=None):
    with phase(nc, shared) as a:
        stats = a.sb(name + "stats", [T, NT, 6])
        mv = a.sb(name + "mv", [T, NT, 2])
        rstd = a.sb(name + "rstd", [T, NT])
        stat, var_ok, rooted, chain = (a.sem(name + s) for s in ("stat", "var", "root", "ch"))
        block = a.block()

        @block.vector
        def _(dve):
            link = chained(dve, chain)
            ln_stats(nc, dve, link, var_ok, rooted, 0, lambda t: tile_of(m.x, t), mv, stats, stat, rstd)
            with dve.Fori(0, NT // 5) as k:
                for t in (k * 5 + i for i in range(5)):
                    nc.vector.tensor_scalar(tile_of(dst, t), tile_of(m.x, t), mv[:, bass.ds(t, 1), 0],
                                            rstd[:, bass.ds(t, 1)], ALU.subtract, ALU.mult)

        @block.scalar
        def _(act):
            ln_root(nc, act, var_ok, rooted, 0, rstd)


def load_experts(nc, m, w1, w2, shared=None):
    with phase(nc, shared) as a:
        block = a.block()

        @block.sync
        def _(sp):
            for e in range(NEX):
                sp.dma_start(m.w1s[:, 2 * e:2 * e + 2, :], w1[e].rearrange("(k p) h -> p k h", p=B)).then_inc(m.weights_in, 16)
                sp.dma_start(m.w2s[:, 8 * e:8 * e + 8, :], w2[e].rearrange("(j p) d -> p j d", p=B)).then_inc(m.weights_in, 16)


def router_phase(nc, m, wr, br, shared=None):
    with phase(nc, shared) as a:
        w = a.sb("r_w", [B, 2, NEX])
        bias = a.sb("r_b", [T, NEX])
        stats = a.sb("r_stats", [T, NT, 6])
        ln = [a.sb(f"r_ln{b}", [T, D]) for b in range(2)]
        lnT = [a.sb(f"r_lnT{b}", [B, 2, T]) for b in range(2)]
        logit = a.sb("r_logit", [T, NT, NEX])
        same = a.sb("r_same", [T, NT, NEX])
        last_first = a.sb("r_last_first", [T, NT, NEX])
        top = a.sb("r_top", [T, 2, NT])
        gap = a.sb("r_gap", [T, NT])
        den = a.sb("r_den", [T, NT])
        p_t = [a.ps(f"r_pt{b}", [B, 512]) for b in range(2)]
        p_l = [a.ps(f"r_pl{b}", [T, 512]) for b in range(2)]
        w_in, stat, var_ok, rooted, chain = (a.sem("r_" + s) for s in ("w", "stat", "var", "root", "ch"))
        staged, turned, copied, mul, found, gap_ok, exp_ok = (
            a.sem("r_" + s) for s in ("staged", "turned", "copied", "mul", "found", "gap_ok", "exp_ok"))
        block = a.block()

        @block.sync
        def _(sp):
            sp.dma_start(w[:, :, :], wr.rearrange("(k p) n -> p k n", p=B)).then_inc(w_in, 16)
            sp.dma_start(bias[:, :], row_to_all(br, T)).then_inc(w_in, 16)

        @block.vector
        def _(dve):
            link = chained(dve, chain)
            ln_stats(nc, dve, link, var_ok, rooted, 0, lambda t: tile_of(m.ln, t), m.mv, stats, stat, m.rstd)
            dve.wait_ge(w_in, 32)

            for e in range(NEX):
                last = nc.vector.memset(last_first[:, :, e:e + 1], float(NEX - e))
            link(last)

            def add_bias(k, b):
                t = 2 * k + b
                dve.wait_ge(mul, t + 1)
                nc.vector.tensor_tensor(tile_of(logit, t), p_l[b][:, 0:NEX], bias[:, :], ALU.add).then_inc(found, 1)
            pipelined(dve, NT, [(0, add_bias)])
            dve.wait_ge(found, NT)
            for i in range(2):
                expert = m.expert[:, i * NT:(i + 1) * NT]
                link(nc.vector.tensor_reduce(top[:, i, :], logit[:, :, :], AX_X, ALU.max))
                link(nc.vector.tensor_tensor(same[:, :, :], logit[:, :, :],
                                             top[:, i, :].unsqueeze(2).to_broadcast([T, NT, NEX]), ALU.is_equal))
                link(nc.vector.tensor_tensor(same[:, :, :], same[:, :, :], last_first[:, :, :], ALU.mult))
                link(nc.vector.tensor_reduce(expert, same[:, :, :], AX_X, ALU.max))
                if i == 0:
                    link(nc.vector.tensor_tensor(same[:, :, :], last_first[:, :, :],
                                                 expert.unsqueeze(2).to_broadcast([T, NT, NEX]), ALU.is_equal))
                    link(nc.vector.scalar_tensor_tensor(out=logit[:, :, :], in0=same[:, :, :], scalar=-BIG,
                                                        in1=logit[:, :, :], op0=ALU.mult, op1=ALU.add))
            link(nc.vector.tensor_scalar(m.expert[:, :], m.expert[:, :], -1.0, float(NEX), ALU.mult, ALU.add))
            nc.vector.tensor_tensor(gap[:, :], top[:, 1, :], top[:, 0, :], ALU.subtract).then_inc(gap_ok, 1)
            dve.wait_ge(exp_ok, 1)
            link(nc.vector.tensor_scalar(den[:, :], gap[:, :], 1.0, None, ALU.add))
            link(nc.vector.reciprocal(m.weight[:, 0:NT], den[:, :]))
            link(nc.vector.tensor_tensor(m.weight[:, NT:2 * NT], gap[:, :], m.weight[:, 0:NT], ALU.mult))

        @block.scalar
        def _(act):
            ln_root(nc, act, var_ok, rooted, 0, m.rstd)

            def stage(k, b):
                t = 2 * k + b
                after(act, turned, t - 1)
                nc.scalar.copy(ln[b][:, :], tile_of(m.ln, t)).then_inc(staged, 1)

            def copy(k, b):
                t = 2 * k + b
                act.wait_ge(turned, t + 1)
                after(act, mul, t - 1)
                nc.scalar.copy(lnT[b][:, :, :].rearrange("p k n -> p (k n)"), p_t[b][:, 0:2 * T]).then_inc(copied, 1)
            pipelined(act, NT, [(0, stage), (1, copy)])
            act.wait_ge(gap_ok, 1)
            nc.scalar.activation(gap[:, :], gap[:, :], ACT.Exp).then_inc(exp_ok, 1)

        @block.tensor
        def _(pe):
            pe.wait_ge(w_in, 32)

            def turn(k, b):
                t = 2 * k + b
                pe.wait_ge(staged, t + 1)
                after(pe, copied, t - 1)
                for j in range(2):
                    last = nc.tensor.transpose(p_t[b][:, j * T:(j + 1) * T], ln[b][:, j * B:(j + 1) * B],
                                               m.ident[0:T, 0:T])
                last.then_inc(turned, 1)

            def multiply(k, b):
                t = 2 * k + b
                pe.wait_ge(copied, t + 1)
                after(pe, found, t - 1)
                for j in range(2):
                    last = nc.tensor.matmul(p_l[b][:, 0:NEX], lnT[b][:, j, :], w[:, j, :], start=(j == 0), stop=(j == 1))
                last.then_inc(mul, 1)
            pipelined(pe, NT, [(2, multiply), (0, turn)])


def fill_tokens(nc, m, tokens, shared=None):
    per = MB * B // B
    some = 8
    with phase(nc, shared) as a:
        blank = a.sb("t_blank", [B, some, D])
        cleared, filled = a.sem("t_cleared"), a.sem("t_filled")
        block = a.block()
        view = tokens.rearrange("(p r) c -> p r c", p=B)

        @block.vector
        def _(dve):
            nc.vector.memset(blank[:, :, :], 0.0).then_inc(cleared, 1)

        @block.sync
        def _(sp):
            sp.wait_ge(cleared, 1)
            with sp.Fori(0, per // some) as i:
                sp.dma_start(view[:, bass.ds(i * some, some), :], blank[:, :, :]).then_inc(filled, 16)
            sp.wait_ge(filled, 16 * (per // some))


def send_tokens(nc, m, tokens, shared=None):
    BUF = 5
    with phase(nc, shared) as a:
        xn = [a.sb(f"t_xn{b}", [T, D]) for b in range(BUF)]
        pos = [a.sb(f"t_pos{b}", [T, 2], I32) for b in range(BUF)]
        built = a.sem("t_built")
        sent = m.indirect_sems(BUF)
        block = a.block()

        @block.vector
        def _(dve):
            def build(k, b):
                t = BUF * k + b
                after(dve, sent[b], 32 * k)
                nc.vector.tensor_copy(pos[b][:, 0:1], m.slot[:, bass.ds(t, 1)])
                nc.vector.tensor_copy(pos[b][:, 1:2], m.slot[:, bass.ds(t + NT, 1)])
                nc.vector.tensor_scalar(xn[b][:, :], tile_of(m.ln, t), m.mv[:, bass.ds(t, 1), 0],
                                        m.rstd[:, bass.ds(t, 1)], ALU.subtract, ALU.mult).then_inc(built, 1)
            pipelined(dve, NT, [(0, build)], BUF)

        @block.gpsimd
        def _(pool):
            def scatter(k, b):
                pool.wait_ge(built, BUF * k + b + 1)
                pool.sem_inc(m.tick, 1)
                for g in range(2):
                    nc.gpsimd.indirect_dma_start(
                        out=tokens, out_offset=bass.IndirectOffsetOnAxis(ap=pos[b][:, g:g + 1].bitcast(U32), axis=0),
                        in_=xn[b][:, :], in_offset=None).then_inc(sent[b], 16)
            pipelined(pool, NT, [(0, scatter)], BUF)
            for b in range(BUF):
                pool.wait_ge(sent[b], 32 * (NT // BUF))


def shift_biases(nc, m, ln_b, b1, shared=None):
    with phase(nc, shared) as a:
        shift = a.sb("b_shift", [B, NEX * 2])
        p_b = a.ps("b_pb", [B, 512])
        small_in, shifted = a.sem("b_small"), a.sem("b_shifted")
        block = a.block()

        @block.sync
        def _(sp):
            sp.dma_start(shift[:, :], ln_b).then_inc(small_in, 16)
            sp.dma_start(m.b1s[:, :], b1).then_inc(small_in, 16)

        @block.tensor
        def _(pe):
            pe.wait_ge(small_in, 32)
            pe.wait_ge(m.weights_in, 32 * NEX)
            for e in range(NEX):
                for j in range(8):
                    for k in range(2):
                        last = nc.tensor.matmul(p_b[:, 8 * e + j:8 * e + j + 1], m.w1s[:, 2 * e + k, j * B:(j + 1) * B],
                                                shift[:, 2 * e + k:2 * e + k + 1], start=(k == 0), stop=(k == 1))
            last.then_inc(shifted, 1)

        @block.vector
        def _(dve):
            dve.wait_ge(small_in, 32)
            dve.wait_ge(shifted, 1)
            nc.vector.tensor_tensor(m.b1s[:, :], p_b[:, 0:8 * NEX], m.b1s[:, :], ALU.add)


def expert_phase(nc, m, tokens, answers, ln_g, b2, shared=None):
    with phase(nc, shared) as a:
        w1s, w2s = m.w1s, m.w2s
        gain = a.sb("e_gain", [B, NEX * 2])
        b1s = m.b1s
        b2s = a.sb("e_b2", [B, NEX, D])
        tok = [a.sb(f"e_tok{b}", [B, D]) for b in range(2)]
        tokT = [a.sb(f"e_tokT{b}", [B, 2, B]) for b in range(2)]
        wg = [a.sb(f"e_wg{b}", [B, 2, HID]) for b in range(2)]
        hid = [a.sb(f"e_hid{b}", [B, 8, B]) for b in range(2)]
        ans = [a.sb(f"e_ans{b}", [B, D]) for b in range(2)]
        p_t = a.ps("e_pt", [B, 512])
        p_h = [[a.ps(f"e_ph{b}{i}", [B, 512]) for i in range(2)] for b in range(2)]
        p_y = [a.ps(f"e_py{b}", [B, 512]) for b in range(2)]
        small_in = a.sem("e_small")
        tok_in = [a.sem(f"e_tok_in{b}") for b in range(2)]
        stored = [a.sem(f"e_stored{b}") for b in range(2)]
        turned, copied, weighted, up, act_ok, down, answered = (
            a.sem("e_" + s) for s in ("turned", "copied", "weighted", "up", "act_ok", "down", "answered"))
        block = a.block()

        @block.sync
        def _(sp):
            sp.dma_start(gain[:, :], ln_g).then_inc(small_in, 16)
            sp.dma_start(b2s[:, :, :].rearrange("p e d -> p (e d)"), row_to_all(b2, B)).then_inc(small_in, 16)

            def load(k, b):
                q = 2 * k + b
                after(sp, turned, q - 1)
                sp.sem_inc(m.tick, 1)
                sp.dma_start(tok[b][:, :], tokens[bass.ds(q * B, B), :]).then_inc(tok_in[b], 16)

            def store(k, b):
                q = 2 * k + b
                sp.wait_ge(answered, q + 1)
                sp.sem_inc(m.tick, 1)
                sp.dma_start(answers[bass.ds(q * B, B), :], ans[b][:, :]).then_inc(stored[b], 16)
            pipelined(sp, MB, [(4, in_twos(store)), (0, in_twos(load))], 4)
            for b in range(2):
                sp.wait_ge(stored[b], 16 * (MB // 2))

        @block.tensor
        def _(pe):
            pe.wait_ge(m.weights_in, 32 * NEX)

            def turn(k, b):
                q = 2 * k + b
                pe.wait_ge(tok_in[b], 16 * (k + 1))
                after(pe, copied, q)
                for j in range(2):
                    last = nc.tensor.transpose(p_t[:, j * B:(j + 1) * B], tok[b][:, j * B:(j + 1) * B], m.ident[:, :])
                last.then_inc(turned, 1)

            def rise(k, b):
                q = 2 * k + b
                pe.wait_ge(copied, q + 1)
                pe.wait_ge(weighted, q + 1)
                after(pe, act_ok, q - 1)
                for j in range(8):
                    for i in range(2):
                        last = nc.tensor.matmul(p_h[b][j // 4][:, (j % 4) * B:(j % 4 + 1) * B],
                                                wg[b][:, i, j * B:(j + 1) * B], tokT[b][:, i, :],
                                                start=(i == 0), stop=(i == 1))
                last.then_inc(up, 1)

            def fall(k, b, e):
                q = 2 * k + b
                pe.wait_ge(act_ok, q + 1)
                after(pe, answered, q - 1)
                for j in range(8):
                    last = nc.tensor.matmul(p_y[b][:, 0:D], hid[b][:, j, :], tile_of(w2s, e * 8 + j),
                                            start=(j == 0), stop=(j == 7))
                last.then_inc(down, 1)
            pipelined(pe, MB, [(1, in_twos(rise)), (0, in_twos(turn)), (2, in_twos(fall), NEX - 1)], 4,
                      m.block_expert)

        @block.scalar
        def _(act):
            def copy(k, b):
                q = 2 * k + b
                act.wait_ge(turned, q + 1)
                after(act, up, q - 1)
                nc.scalar.copy(tokT[b][:, :, :].rearrange("p k n -> p (k n)"), p_t[:, 0:2 * B]).then_inc(copied, 1)

            def gelu(k, b, e):
                q = 2 * k + b
                act.wait_ge(up, q + 1)
                after(act, down, q - 1)
                for j in range(8):
                    last = nc.scalar.activation(hid[b][:, j, :], p_h[b][j // 4][:, (j % 4) * B:(j % 4 + 1) * B],
                                                ACT.Gelu, bias=b1s[:, bass.ds(e * 8 + j, 1)])
                last.then_inc(act_ok, 1)
            pipelined(act, MB, [(1, in_twos(gelu), NEX - 1), (0, in_twos(copy))], 4, m.block_expert)

        @block.vector
        def _(dve):
            dve.wait_ge(small_in, 32)
            dve.wait_ge(m.weights_in, 32 * NEX)

            def weigh(k, b, e):
                q = 2 * k + b
                after(dve, up, q - 1)
                for i in range(2):
                    last = nc.vector.tensor_scalar(wg[b][:, i, :], tile_of(w1s, e * 2 + i),
                                                   gain[:, bass.ds(e * 2 + i, 1)], None, ALU.mult)
                last.then_inc(weighted, 1)

            def answer(k, b, e):
                q = 2 * k + b
                dve.wait_ge(down, q + 1)
                after(dve, stored[b], 16 * k)
                nc.vector.tensor_tensor(ans[b][:, :], p_y[b][:, 0:D], tile_of(b2s, e), ALU.add).then_inc(answered, 1)
            pipelined(dve, MB, [(3, in_twos(answer), NEX - 1), (0, in_twos(weigh), NEX - 1)], 4, m.block_expert)


def combine_phase(nc, m, answers, shared=None):
    BUF = 5
    with phase(nc, shared) as a:
        pos = [a.sb(f"c_pos{b}", [T, 2], I32) for b in range(BUF)]
        got = [[a.sb(f"c_got{b}{g}", [T, D]) for g in range(2)] for b in range(BUF)]
        built, added, chain = (a.sem("c_" + s) for s in ("built", "added", "chain"))
        got_in = m.indirect_sems(BUF)
        block = a.block()

        @block.gpsimd
        def _(pool):
            def gather(k, b):
                pool.wait_ge(built, BUF * k + b + 1)
                pool.sem_inc(m.tick, 1)
                for g in range(2):
                    nc.gpsimd.indirect_dma_start(
                        out=got[b][g][:, :], out_offset=None, in_=answers,
                        in_offset=bass.IndirectOffsetOnAxis(ap=pos[b][:, g:g + 1].bitcast(U32), axis=0)
                    ).then_inc(got_in[b], 16)
            pipelined(pool, NT, [(0, gather)], BUF)

        @block.vector
        def _(dve):
            def build(k, b):
                t = BUF * k + b
                after(dve, added, t - BUF + 1)
                nc.vector.tensor_copy(pos[b][:, 0:1], m.slot[:, bass.ds(t, 1)])
                nc.vector.tensor_copy(pos[b][:, 1:2], m.slot[:, bass.ds(t + NT, 1)]).then_inc(built, 1)

            def add(k, b):
                t = BUF * k + b
                step = steps(dve, chain, t)
                dve.wait_ge(got_in[b], 32 * (k + 1))
                step(nc.vector.scalar_tensor_tensor(out=tile_of(m.x, t), in0=got[b][0][:, :],
                                                    scalar=m.weight[:, bass.ds(t, 1)], in1=tile_of(m.x, t),
                                                    op0=ALU.mult, op1=ALU.add))
                nc.vector.scalar_tensor_tensor(out=tile_of(m.x, t), in0=got[b][1][:, :],
                                               scalar=m.weight[:, bass.ds(t + NT, 1)], in1=tile_of(m.x, t),
                                               op0=ALU.mult, op1=ALU.add).then_inc(added, 1)
            pipelined(dve, NT, [(3, add), (0, build)], BUF)


def attention_rows(nc, m, wg, a_src, a_dst, table, shared=None):
    with phase(nc, shared) as a:
        w = a.sb("h_w", [B, 2, D])
        a_s = a.sb("h_as", [T, D])
        a_d = a.sb("h_ad", [T, D])
        ln = [a.sb(f"h_ln{b}", [T, D]) for b in range(2)]
        lnT = [a.sb(f"h_lnT{b}", [B, 2, T]) for b in range(2)]
        row = [a.sb(f"h_row{b}", [T, HC]) for b in range(2)]
        junk = a.sb("h_junk", [T, 2, D])
        to = [a.sb(f"h_to{b}", [T, 1]) for b in range(2)]
        p_t = [a.ps(f"h_pt{b}", [B, 512]) for b in range(2)]
        p_h = [a.ps(f"h_ph{b}", [T, 512]) for b in range(2)]
        w_in, staged, turned, copied, mul, made, kept, one, chain, chain_p = (
            a.sem("h_" + s) for s in ("w", "staged", "turned", "copied", "mul", "made", "kept", "one", "chain", "chain_p"))
        stored = [a.sem(f"h_stored{b}") for b in range(2)]
        block = a.block()

        @block.sync
        def _(sp):
            sp.dma_start(w[:, :, :], wg.rearrange("(k p) n -> p k n", p=B)).then_inc(w_in, 16)
            sp.dma_start(a_s[:, :], row_to_all(a_src, T)).then_inc(w_in, 16)
            sp.dma_start(a_d[:, :], row_to_all(a_dst, T)).then_inc(w_in, 16)

            def store(k, b):
                t = 2 * k + b
                sp.wait_ge(made, t + 1)
                sp.sem_inc(m.tick, 1)
                sp.dma_start(table[bass.ds(t * T, T), :], row[b][:, :]).then_inc(stored[b], 16)
            pipelined(sp, NT, [(0, store)])
            for b in range(2):
                sp.wait_ge(stored[b], 16 * ((NT + 1 - b) // 2))

        @block.gpsimd
        def _(pool):
            with pool.Fori(0, NT // 5) as k:
                for t in (k * 5 + i for i in range(5)):
                    nc.gpsimd.tensor_tensor(tile_of(m.x, t), tile_of(m.x, t), tile_of(m.ln, t), ALU.add)

        @block.scalar
        def _(act):
            def stage(k, b):
                t = 2 * k + b
                after(act, turned, t - 1)
                nc.scalar.copy(ln[b][:, :], tile_of(m.ln, t)).then_inc(staged, 1)

            def keep(k, b):
                t = 2 * k + b
                act.wait_ge(made, t + 1)
                nc.scalar.copy(tile_of(m.acc, t), row[b][:, :]).then_inc(kept, 1)

            def copy(k, b):
                t = 2 * k + b
                act.wait_ge(turned, t + 1)
                after(act, mul, t - 1)
                nc.scalar.copy(lnT[b][:, :, :].rearrange("p k n -> p (k n)"), p_t[b][:, 0:2 * T]).then_inc(copied, 1)
            pipelined(act, NT, [(0, stage), (1, copy), (4, keep)])

        @block.tensor
        def _(pe):
            pe.wait_ge(w_in, 48)

            def turn(k, b):
                t = 2 * k + b
                pe.wait_ge(staged, t + 1)
                after(pe, copied, t - 1)
                for j in range(2):
                    last = nc.tensor.transpose(p_t[b][:, j * T:(j + 1) * T], ln[b][:, j * B:(j + 1) * B],
                                               m.ident[0:T, 0:T])
                last.then_inc(turned, 1)

            def multiply(k, b):
                t = 2 * k + b
                pe.wait_ge(copied, t + 1)
                after(pe, made, t - 1)
                for j in range(2):
                    last = nc.tensor.matmul(p_h[b][:, 0:D], lnT[b][:, j, :], w[:, j, :], start=(j == 0), stop=(j == 1))
                last.then_inc(mul, 1)
            pipelined(pe, NT, [(2, multiply), (0, turn)])

        @block.vector
        def _(dve):
            for b in range(2):
                last = nc.vector.memset(row[b][:, D + 1:D + 2], 1.0)
            last.then_inc(one, 1)
            dve.wait_ge(one, 1)
            dve.wait_ge(w_in, 48)

            def make(k, b):
                t = 2 * k + b
                step = steps(dve, chain, 2 * t)
                dve.wait_ge(mul, t + 1)
                after(dve, stored[b], 16 * k)
                after(dve, kept, t - 1)
                step(nc.vector.tensor_copy(row[b][:, 0:D], p_h[b][:, 0:D]))
                nc.vector.tensor_tensor_reduce(out=junk[:, 0, :], in0=row[b][:, 0:D], in1=a_s[:, :], scale=1.0,
                                               scalar=0.0, op0=ALU.mult, op1=ALU.add,
                                               accum_out=row[b][:, D:D + 1])
                step(nc.vector.tensor_tensor_reduce(out=junk[:, 1, :], in0=row[b][:, 0:D], in1=a_d[:, :], scale=1.0,
                                                    scalar=0.0, op0=ALU.mult, op1=ALU.add, accum_out=to[b][:, :]))
                nc.vector.tensor_copy(m.to[:, bass.ds(t, 1)], to[b][:, :]).then_inc(made, 1)
            pipelined(dve, NT, [(0, make)])
            dve.wait_ge(made, NT)
            dve.wait_ge(kept, NT)
            link = chained(dve, chain_p)
            link(nc.vector.tensor_tensor(m.peak[:, :], m.acc[:, :, D], m.to[:, :], ALU.add))
            link(nc.vector.scalar_tensor_tensor(out=m.peak[:, :], in0=m.peak[:, :], scalar=0.2, in1=m.peak[:, :],
                                                op0=ALU.mult, op1=ALU.max))


def attention_phase(nc, m, recs, table, bias, shared=None):
    with phase(nc, shared) as a:
        peak = m.peak
        rec = [a.sb(f"a_rec{b}", [B, 2, 2]) for b in range(UP)]
        got = [a.sb(f"a_got{b}", [B, 2, HC]) for b in range(UP)]
        mark = [a.sb(f"a_mark{b}", [B, 2, T]) for b in range(4)]
        top = [a.sb(f"a_top{b}", [T, 4]) for b in range(4)]
        shrink = [a.sb(f"a_shrink{b}", [T, 1]) for b in range(UP)]
        score = [a.sb(f"a_score{b}", [T, 2 * B]) for b in range(4)]
        probT = [a.sb(f"a_probT{b}", [B, 2 * T]) for b in range(4)]
        bias_s = a.sb("a_bias", [T, D])
        den = a.sb("a_den", [T, NT])
        out = a.sb("a_out", [T, D])
        p_m = [a.ps(f"a_pm{b}", [T, 512]) for b in range(2)]
        p_p = [a.ps(f"a_pp{b}", [B, 512]) for b in range(2)]
        p_o = [a.ps(f"a_po{b}", [T, 512]) for b in range(2)]
        rec_in = [a.sem(f"a_rec_in{b}") for b in range(UP)]
        got_in = m.indirect_sems(UP)
        (w_in, placed, marked, turned, chain_m, shifted, leaked, chain_s, scored, prob, prob_turned, prob_copied,
         summed, shrunk, taken, chain, chain_o) = (
            a.sem("a_" + s) for s in ("w", "placed", "marked", "turned", "chain_m", "shifted", "leaked", "chain_s",
                                      "scored", "prob", "prob_turned", "prob_copied", "summed", "shrunk", "taken",
                                      "chain", "chain_o"))
        block = a.block()

        @block.sync
        def _(sp):
            sp.dma_start(bias_s[:, :], row_to_all(bias, T)).then_inc(w_in, 16)

            def load(k, b):
                q = UP * k + b
                after(sp, got_in[b], 32 * k)
                sp.sem_inc(m.tick, 1)
                after(sp, marked, q - UP + 1)
                sp.sem_inc(m.tick, 1)
                sp.dma_start(rec[b][:, :, :], recs[bass.ds(q * 2 * B, 2 * B), :].rearrange("(p h) c -> p h c", h=2)
                             ).then_inc(rec_in[b], 16)
            pipelined(sp, PB, [(0, load)], UP)

        @block.gpsimd
        def _(pool):
            def gather(k, b):
                q = UP * k + b
                pool.wait_ge(rec_in[b], 16 * (k + 1))
                after(pool, summed, q - UP + 1)
                pool.sem_inc(m.tick, 1)
                for h in range(2):
                    nc.gpsimd.indirect_dma_start(
                        out=got[b][:, h, :], out_offset=None, in_=table,
                        in_offset=bass.IndirectOffsetOnAxis(ap=rec[b][:, h, 1:2].bitcast(U32), axis=0)
                    ).then_inc(got_in[b], 16)
            pipelined(pool, PB, [(0, gather)], UP)

        @block.vector
        def _(dve):
            link = chained(dve, chain)

            def select_a(k, b):
                q = UP * k + b
                dve.wait_ge(rec_in[b], 16 * (k + 1))
                after(dve, turned, q - 3)
                for h in range(2):
                    last = nc.vector.tensor_scalar(mark[b % 4][:, h, :], m.ramp[:, 0:T], rec[b][:, h, 0:1], BIG,
                                                   ALU.is_equal, ALU.mult)
                last.then_inc(placed, 1)

            def select_b(k, b):
                q = UP * k + b
                dve.wait_ge(got_in[b], 32 * (k + 1))
                dve.wait_ge(placed, q + 1)
                for h in range(2):
                    last = nc.vector.tensor_scalar(mark[b % 4][:, h, :], mark[b % 4][:, h, :], BIG,
                                                   got[b][:, h, D:D + 1], ALU.subtract, ALU.add)
                last.then_inc(marked, 1)

            def peak_a(k, b):
                q = UP * k + b
                dve.wait_ge(turned, q + 1)
                after(dve, shrunk, q - 3)
                nc.vector.tensor_reduce(top[b % 4][:, 0:1], p_m[b % 2][:, 0:2 * B], AX_X, ALU.max).then_inc(chain_m, 1)

            def peak_b(k, b, t):
                dve.wait_ge(chain_m, 3 * (UP * k + b) + 1)
                nc.vector.tensor_scalar(top[b % 4][:, 0:1], top[b % 4][:, 0:1], m.to[:, bass.ds(t, 1)], None,
                                        ALU.add).then_inc(chain_m, 1)

            def peak_c(k, b):
                c = b % 4
                dve.wait_ge(chain_m, 3 * (UP * k + b) + 2)
                nc.vector.scalar_tensor_tensor(out=top[c][:, 1:2], in0=top[c][:, 0:1], scalar=0.2,
                                               in1=top[c][:, 0:1], op0=ALU.mult, op1=ALU.max).then_inc(chain_m, 1)

            def peak_d(k, b, t):
                q = UP * k + b
                dve.wait_ge(chain_m, 3 * q + 3)
                after(dve, scored, q)
                nc.vector.tensor_scalar(top[b % 4][:, 2:3], top[b % 4][:, 1:2], peak[:, bass.ds(t, 1)], -1.0,
                                        ALU.max, ALU.mult).then_inc(chain_s, 1)

            def peak_e(k, b, t):
                dve.wait_ge(chain_s, 2 * (UP * k + b) + 1)
                nc.vector.tensor_tensor(top[b % 4][:, 3:4], top[b % 4][:, 2:3], peak[:, bass.ds(t, 1)],
                                        ALU.add).then_inc(chain_s, 1)

            def peak_f(k, b, t):
                dve.wait_ge(chain_s, 2 * (UP * k + b) + 2)
                nc.vector.tensor_scalar(peak[:, bass.ds(t, 1)], top[b % 4][:, 2:3], -1.0, None,
                                        ALU.mult).then_inc(scored, 1)

            def leak(k, b):
                c = b % 4
                dve.wait_ge(shifted, UP * k + b + 1)
                nc.vector.scalar_tensor_tensor(out=score[c][:, :], in0=score[c][:, :], scalar=0.2,
                                               in1=score[c][:, :], op0=ALU.mult, op1=ALU.max).then_inc(leaked, 1)

            def take(k, b, t):
                q = UP * k + b
                dve.wait_ge(summed, q + 1)
                dve.wait_ge(shrunk, q + 1)
                after(dve, taken, q)
                nc.vector.scalar_tensor_tensor(out=tile_of(m.acc, t), in0=tile_of(m.acc, t),
                                               scalar=shrink[b][:, :], in1=p_o[b % 2][:, 0:HC],
                                               op0=ALU.mult, op1=ALU.add).then_inc(taken, 1)

            NUM = NT - 1
            pipelined(dve, PB, [(2, peak_a), (0, select_a), (2, peak_b, NUM), (0, select_b), (2, peak_c),
                                (3, leak), (2, peak_d, NUM), (8, take, NUM), (2, peak_e, NUM), (2, peak_f, NUM)],
                      UP, m.dst_tile)
            dve.wait_ge(taken, PB)
            dve.wait_ge(w_in, 16)
            link(nc.vector.reciprocal(den[:, :], m.acc[:, :, D + 1]))
            with dve.Fori(0, NT) as t:
                step = steps(dve, chain_o, 2 * t)
                step(nc.vector.scalar_tensor_tensor(out=out[:, :], in0=m.acc[:, bass.ds(t, 1), 0:D].rearrange("p a d -> p (a d)"),
                                                    scalar=den[:, bass.ds(t, 1)], in1=bias_s[:, :],
                                                    op0=ALU.mult, op1=ALU.add))
                step(nc.vector.scalar_tensor_tensor(out=tile_of(m.x, t), in0=out[:, :], scalar=0.0, in1=tile_of(m.x, t),
                                                    op0=ALU.max, op1=ALU.add))

        @block.scalar
        def _(act):
            def shift(k, b, t):
                q = UP * k + b
                act.wait_ge(chain_m, 3 * q + 1)
                after(act, prob_turned, q - 3)
                nc.scalar.activation(score[b % 4][:, :], p_m[b % 2][:, 0:2 * B], ACT.Identity,
                                     bias=m.to[:, bass.ds(t, 1)]).then_inc(shifted, 1)

            def weigh(k, b):
                q = UP * k + b
                c = b % 4
                act.wait_ge(leaked, q + 1)
                act.wait_ge(scored, q + 1)
                after(act, taken, q - UP + 1)
                nc.scalar.activation(score[c][:, :], score[c][:, :], ACT.Exp, bias=top[c][:, 2:3]).then_inc(prob, 1)
                nc.scalar.activation(shrink[b][:, :], top[c][:, 3:4], ACT.Exp).then_inc(shrunk, 1)

            def copy(k, b):
                q = UP * k + b
                act.wait_ge(prob_turned, q + 1)
                after(act, summed, q - 3)
                nc.scalar.copy(probT[b % 4][:, :], p_p[b % 2][:, 0:2 * T]).then_inc(prob_copied, 1)
            pipelined(act, PB, [(6, copy), (4, weigh), (2, shift, NT - 1)], UP, m.dst_tile)

        @block.tensor
        def _(pe):
            def turn(k, b):
                q = UP * k + b
                pe.wait_ge(marked, q + 1)
                after(pe, shifted, q - 1)
                for h in range(2):
                    last = nc.tensor.transpose(p_m[b % 2][0:T, h * B:(h + 1) * B], mark[b % 4][:, h, :], m.ident[:, :])
                last.then_inc(turned, 1)

            def turn_prob(k, b):
                q = UP * k + b
                pe.wait_ge(prob, q + 1)
                after(pe, prob_copied, q - 1)
                for h in range(2):
                    last = nc.tensor.transpose(p_p[b % 2][:, h * T:(h + 1) * T], score[b % 4][:, h * B:(h + 1) * B],
                                               m.ident[0:T, 0:T])
                last.then_inc(prob_turned, 1)

            def gather_sum(k, b):
                q = UP * k + b
                pe.wait_ge(prob_copied, q + 1)
                after(pe, taken, q - 1)
                pe.wait_ge(got_in[b], 32 * (k + 1))
                for h in range(2):
                    last = nc.tensor.matmul(p_o[b % 2][:, 0:HC], probT[b % 4][:, h * T:(h + 1) * T], got[b][:, h, :],
                                            start=(h == 0), stop=(h == 1))
                last.then_inc(summed, 1)
            pipelined(pe, PB, [(7, gather_sum), (5, turn_prob), (1, turn)], UP)


H1, H2 = 256, 128
X1, X2, NX = 128, 64, 4


def mlp_phase(nc, m, io, shared=None):
    with phase(nc, shared) as a:
        gw = a.sb("f_gw", [B, 2, NX])
        gb = a.sb("f_gb", [T, NX])
        sw1 = a.sb("f_sw1", [B, 2, H1])
        sb1 = a.sb("f_sb1", [B, 2])
        sw2 = a.sb("f_sw2", [B, 2, H2])
        sb2 = a.sb("f_sb2", [H2, 1])
        sw3 = a.sb("f_sw3", [H2, D])
        sb3 = a.sb("f_sb3", [T, D])
        ew1 = a.sb("f_ew1", [B, NX * 2, X1])
        eb1 = a.sb("f_eb1", [X1, NX])
        ew2 = a.sb("f_ew2", [X1, NX, X2])
        eb2 = a.sb("f_eb2", [X2, NX])
        ew3 = a.sb("f_ew3", [X2 + 1, NX, D])
        ln = [a.sb(f"f_ln{b}", [T, D]) for b in range(2)]
        lnT = [a.sb(f"f_lnT{b}", [B, 2, T]) for b in range(2)]
        gates = [a.sb(f"f_gates{b}", [T, 8]) for b in range(2)]
        top = [a.sb(f"f_top{b}", [T, 8]) for b in range(2)]
        at = [a.sb(f"f_at{b}", [T, 8], U32) for b in range(2)]
        atf = [a.sb(f"f_atf{b}", [T, 2]) for b in range(2)]
        small = [a.sb(f"f_small{b}", [T, 8]) for b in range(2)]
        share = [a.sb(f"f_share{b}", [T, 2 * NX]) for b in range(2)]
        s1 = [a.sb(f"f_s1{b}", [B, 2, T]) for b in range(2)]
        s2 = [a.sb(f"f_s2{b}", [H2, T]) for b in range(2)]
        e1 = [a.sb(f"f_e1{b}", [X1, NX, T]) for b in range(2)]
        e2 = [a.sb(f"f_e2{b}", [X2 + 1, NX, T]) for b in range(2)]
        p_t = a.ps("f_pt", [B, 512])
        p_s1 = a.ps("f_ps1", [B, 512])
        p_s2 = a.ps("f_ps2", [H2, 512])
        p_e1 = a.ps("f_pe1", [B, 512])
        p_e2 = a.ps("f_pe2", [X2, 512])
        p_s3 = a.ps("f_ps3", [T, 512])
        p_e3 = [a.ps(f"f_pe3{i}", [T, 512]) for i in range(2)]
        (w_in, staged, turned, copied, gated, gate_read, e1_mul, e1_ok, s1_mul, s1_ok, s2_mul, s2_ok, e2_mul, e2_ok,
         out_mul, added, chain_g, chain_d, chain_a, top_ok, exp_ok, gap_ok, gap_exp, shared_ok, ready, stored) = (
            a.sem("f_" + s) for s in (
                "w", "staged", "turned", "copied", "gated", "gate_read", "e1_mul", "e1_ok", "s1_mul", "s1_ok",
                "s2_mul", "s2_ok", "e2_mul", "e2_ok", "out_mul", "added", "chain_g", "chain_d", "chain_a", "top_ok", "exp_ok",
                "gap_ok", "gap_exp", "shared_ok", "ready", "stored"))
        loads = ((gw[:, :, :], io["L1_ffn_gW"].rearrange("(k p) n -> p k n", p=B)),
                 (gb[:, :], row_to_all(io["L1_ffn_gb"], T)),
                 (sw1[:, :, :], io["L1_ffn_sW1"].rearrange("(k p) n -> p k n", p=B)),
                 (sb1[:, :], io["sb1_cols"]),
                 (sw2[:, :, :], io["L1_ffn_sW2"].rearrange("(k p) n -> p k n", p=B)),
                 (sb2[:, :], io["sb2_cols"]),
                 (sw3[:, :], io["L1_ffn_sW3"]),
                 (sb3[:, :], row_to_all(io["L1_ffn_sb3"], T)),
                 (ew1[:, :, :], io["L1_ffn_eW1"].rearrange("e (k p) n -> p (e k) n", p=B)),
                 (eb1[:, :], io["eb1_cols"]),
                 (ew2[:, :, :], io["L1_ffn_eW2"].rearrange("e p n -> p e n")),
                 (eb2[:, :], io["eb2_cols"]),
                 (ew3[0:X2, :, :], io["L1_ffn_eW3"].rearrange("e p n -> p e n")),
                 (ew3[X2:X2 + 1, :, :], io["L1_ffn_eb3"].rearrange("(a e) n -> a e n", a=1)))
        block = a.block()

        @block.sync
        def _(sp):
            for dst, src in loads:
                sp.dma_start(dst, src).then_inc(w_in, 16)
            sp.wait_ge(added, NT)
            sp.dma_start(io["out"].rearrange("(t p) d -> p t d", p=T), m.x[:, :, :]).then_inc(stored, 16)
            sp.wait_ge(stored, 16)

        @block.gpsimd
        def _(pool):
            def stage(k, b):
                t = 2 * k + b
                after(pool, turned, t - 1)
                nc.gpsimd.tensor_copy(ln[b][:, :], tile_of(m.ln, t)).then_inc(staged, 1)
            pipelined(pool, NT, [(0, stage)])

        @block.tensor
        def _(pe):
            pe.wait_ge(w_in, 16 * len(loads))
            pe.wait_ge(ready, 1)

            def turn(k, b):
                t = 2 * k + b
                pe.wait_ge(staged, t + 1)
                after(pe, gate_read, t)
                for j in range(2):
                    last = nc.tensor.transpose(p_t[:, j * T:(j + 1) * T], ln[b][:, j * B:(j + 1) * B],
                                               m.ident[0:T, 0:T])
                last.then_inc(turned, 1)

            def gate(k, b):
                t = 2 * k + b
                pe.wait_ge(copied, t + 1)
                for j in range(2):
                    last = nc.tensor.matmul(p_t[0:T, 256:256 + NX], lnT[b][:, j, :], gw[:, j, :],
                                            start=(j == 0), stop=(j == 1))
                last.then_inc(gated, 1)

            def first(k, b):
                t = 2 * k + b
                after(pe, s1_ok, t)
                for i in range(2):
                    for j in range(2):
                        last = nc.tensor.matmul(p_s1[:, i * T:(i + 1) * T], sw1[:, j, i * B:(i + 1) * B],
                                                lnT[b][:, j, :], start=(j == 0), stop=(j == 1))
                last.then_inc(s1_mul, 1)
                after(pe, e1_ok, t)
                for e in range(NX):
                    for j in range(2):
                        last = nc.tensor.matmul(p_e1[:, e * T:(e + 1) * T], ew1[:, 2 * e + j, :], lnT[b][:, j, :],
                                                start=(j == 0), stop=(j == 1))
                last.then_inc(e1_mul, 1)

            def second(k, b):
                t = 2 * k + b
                pe.wait_ge(s1_ok, t + 1)
                after(pe, s2_ok, t)
                for j in range(2):
                    last = nc.tensor.matmul(p_s2[:, 0:T], sw2[:, j, :], s1[b][:, j, :],
                                            start=(j == 0), stop=(j == 1))
                last.then_inc(s2_mul, 1)
                pe.wait_ge(e1_ok, t + 1)
                after(pe, e2_ok, t)
                for e in range(NX):
                    last = nc.tensor.matmul(p_e2[:, e * T:(e + 1) * T], ew2[:, e, :], e1[b][:, e, :],
                                            start=True, stop=True)
                last.then_inc(e2_mul, 1)

            def third(k, b):
                t = 2 * k + b
                pe.wait_ge(s2_ok, t + 1)
                pe.wait_ge(e2_ok, t + 1)
                after(pe, added, t)
                nc.tensor.matmul(p_s3[:, 0:D], s2[b][:, :], sw3[:, :], start=True, stop=True)
                for e in range(NX):
                    last = nc.tensor.matmul(p_e3[e // 2][:, (e % 2) * D:(e % 2 + 1) * D], e2[b][:, e, :],
                                            ew3[:, e, :], start=True, stop=True)
                last.then_inc(out_mul, 1)
            pipelined(pe, NT, [(1, gate), (3, third), (2, second), (0, turn), (1, first)])

        @block.scalar
        def _(act):
            act.wait_ge(w_in, 16 * len(loads))

            def copy(k, b):
                t = 2 * k + b
                act.wait_ge(turned, t + 1)
                after(act, e1_mul, t - 1)
                nc.scalar.copy(lnT[b][:, :, :].rearrange("p k n -> p (k n)"), p_t[:, 0:2 * T]).then_inc(copied, 1)

            def first(k, b):
                t = 2 * k + b
                act.wait_ge(s1_mul, t + 1)
                after(act, s2_mul, t - 1)
                for i in range(2):
                    last = nc.scalar.activation(s1[b][:, i, :], p_s1[:, i * T:(i + 1) * T], ACT.Relu, bias=sb1[:, i:i + 1])
                last.then_inc(s1_ok, 1)
                act.wait_ge(e1_mul, t + 1)
                after(act, e2_mul, t - 1)
                for e in range(NX):
                    last = nc.scalar.activation(e1[b][:, e, :], p_e1[:, e * T:(e + 1) * T], ACT.Relu,
                                                bias=eb1[:, e:e + 1])
                last.then_inc(e1_ok, 1)

            def second(k, b):
                t = 2 * k + b
                act.wait_ge(s2_mul, t + 1)
                after(act, out_mul, t - 1)
                nc.scalar.activation(s2[b][:, :], p_s2[:, 0:T], ACT.Relu, bias=sb2[:, 0:1]).then_inc(s2_ok, 1)
                act.wait_ge(e2_mul, t + 1)
                for e in range(NX):
                    last = nc.scalar.activation(e2[b][0:X2, e, :], p_e2[:, e * T:(e + 1) * T], ACT.Relu,
                                                bias=eb2[:, e:e + 1])
                last.then_inc(e2_ok, 1)

            def gate_exp(k, b):
                t = 2 * k + b
                act.wait_ge(top_ok, t + 1)
                nc.scalar.activation(gates[b][:, 0:NX], gates[b][:, 0:NX], ACT.Exp, bias=small[b][:, 0:1]).then_inc(exp_ok, 1)

            def gap_exp_(k, b):
                act.wait_ge(gap_ok, 2 * k + b + 1)
                nc.scalar.activation(small[b][:, 3:4], small[b][:, 3:4], ACT.Exp).then_inc(gap_exp, 1)
            pipelined(act, NT, [(1, gate_exp), (2, second), (0, copy), (1, first), (1, gap_exp_)])

        @block.vector
        def _(dve):
            for b in range(2):
                nc.vector.memset(gates[b][:, :], -1.0)
                last = nc.vector.memset(e2[b][X2:X2 + 1, :, :], 1.0)
            last.then_inc(ready, 1)
            dve.wait_ge(ready, 1)
            dve.wait_ge(w_in, 16 * len(loads))

            def gate(k, b):
                t = 2 * k + b
                g, s = gates[b], small[b]
                step = steps(dve, chain_g, 7 * t)
                dve.wait_ge(gated, t + 1)
                nc.vector.tensor_tensor(g[:, 0:NX], p_t[0:T, 256:256 + NX], gb[:, :], ALU.add).then_inc(gate_read, 1)
                dve.wait_ge(gate_read, t + 1)
                step(nc.vector.tensor_reduce(s[:, 0:1], g[:, 0:NX], AX_X, ALU.max))
                nc.vector.tensor_scalar(s[:, 0:1], s[:, 0:1], -1.0, None, ALU.mult).then_inc(top_ok, 1)
                dve.wait_ge(exp_ok, t + 1)
                step(nc.vector.tensor_reduce(s[:, 1:2], g[:, 0:NX], AX_X, ALU.add))
                step(nc.vector.reciprocal(s[:, 2:3], s[:, 1:2]))
                step(nc.vector.tensor_scalar(g[:, 0:NX], g[:, 0:NX], s[:, 2:3], None, ALU.mult))
                dve.sem_inc(m.tick, 1)
                step(nc.vector.max(top[b][:, :], g[:, :]))
                dve.sem_inc(m.tick, 1)
                step(nc.vector.max_index(at[b][:, :], top[b][:, :], g[:, :]))
                step(nc.vector.tensor_copy(atf[b][:, :], at[b][:, 0:2]))
                nc.vector.tensor_tensor(s[:, 3:4], top[b][:, 1:2], top[b][:, 0:1], ALU.subtract).then_inc(gap_ok, 1)

            def divide(k, b):
                t = 2 * k + b
                s = small[b]
                step = steps(dve, chain_d, 6 * t)
                dve.wait_ge(gap_exp, t + 1)
                step(nc.vector.tensor_scalar(s[:, 4:5], s[:, 3:4], 1.0, None, ALU.add))
                step(nc.vector.reciprocal(s[:, 5:6], s[:, 4:5]))
                step(nc.vector.tensor_tensor(s[:, 6:7], s[:, 3:4], s[:, 5:6], ALU.mult))
                step(nc.vector.tensor_scalar(share[b][:, 0:NX], m.ramp[0:T, 0:NX], atf[b][:, 0:1], s[:, 5:6],
                                             ALU.is_equal, ALU.mult))
                step(nc.vector.tensor_scalar(share[b][:, NX:2 * NX], m.ramp[0:T, 0:NX], atf[b][:, 1:2], s[:, 6:7],
                                             ALU.is_equal, ALU.mult))
                step(nc.vector.tensor_tensor(share[b][:, 0:NX], share[b][:, 0:NX], share[b][:, NX:2 * NX], ALU.add))

            def add(k, b):
                t = 2 * k + b
                step = steps(dve, chain_a, (1 + NX) * t)
                dve.wait_ge(out_mul, t + 1)
                step(nc.vector.tensor_tensor(tile_of(m.x, t), tile_of(m.x, t), sb3[:, :], ALU.add))
                step(nc.vector.tensor_tensor(tile_of(m.x, t), tile_of(m.x, t), p_s3[:, 0:D], ALU.add))
                for e in range(NX):
                    ins = nc.vector.scalar_tensor_tensor(
                        out=tile_of(m.x, t), in0=p_e3[e // 2][:, (e % 2) * D:(e % 2 + 1) * D],
                        scalar=share[b][:, e:e + 1], in1=tile_of(m.x, t), op0=ALU.mult, op1=ALU.add)
                    if e < NX - 1:
                        step(ins)
                ins.then_inc(added, 1)
            pipelined(dve, NT, [(2, divide), (1, gate), (3, add)])


class Mem:

    def indirect_sems(self, n):
        first = len(self.kept.sems)
        return [self.kept.sem(f"indirect{first + b}") for b in range(n)]


def build(nc, io):
    m = Mem()
    with ExitStack() as ctx:
        a = Pool_(nc, ctx)
        m.ramp = a.sb("ramp", [B, B])
        m.part = a.sb("part", [B, 4])
        m.ident = a.sb("ident", [B, B])
        m.ident_b = a.sb("ident_b", [B, B], BF16)
        m.upper = a.sb("upper", [B, B])
        m.ones = a.sb("ones", [B, B])
        m.x = a.sb("x", [T, NT, D])
        m.src_tile = a.sb("src_tile", [1, EB], I32)
        m.dst_tile = a.sb("dst_tile", [1, PB], I32)
        m.go = a.sem("go")
        m.tick = a.sem("tick")
        m.weights_in = a.sem("weights_in")
        m.kept = a
        setup_phase(nc, m)
        m.src_i = a.sb("src_i", [T, EC], I32)
        m.dst_pos = a.sb("dst_pos", [T, EC], I32)
        m.dst_local = a.sb("dst_local", [T, EC])
        with ExitStack() as first:
            c = Pool_(nc, first)
            m.hn = c.sb("hn", [T, NT, D])
            m.a = c.sb("a", [T, NT, 3 * D], BF16)
            with ExitStack() as edges:
                d = Pool_(nc, edges)
                m.dst_i = d.sb("dst_i", [T, EC], I32)
                m.src_f = d.sb("src_f", [T, EC])
                m.dst_f = d.sb("dst_f", [T, EC])
                m.src_pos = d.sb("src_pos", [T, EC], I32)
                m.src_local = d.sb("src_local", [T, EC])
                load_keys(nc, m, io["src"], io["dst"])
                with phase(nc) as side:
                    fill_records(nc, m, "fs_", io["recs"], REC, EA, side)
                    fill_records(nc, m, "fd_", io["recs2"], 2, 0, side)
                    dispatch(nc, m, "ds_", m.src_f[:, :], EC, NT, T, EB, m.src_pos[:, :], m.src_local[:, :],
                             io["src_tile_dram"], m.src_tile[:, :], B, side)
                with phase(nc) as side:
                    node_phase(nc, m, io["x"], io["w1ab"], io["L0_gnn_b1"], io["b_table"], side)
                    scatter_records(nc, m, "ss_", io["recs"], m.src_pos, m.src_local, m.dst_i, io["edge_attr_64"],
                                    side)
                    dispatch(nc, m, "dd_", m.dst_f[:, :], EC, NT, T, PB, m.dst_pos[:, :], m.dst_local[:, :],
                             io["dst_tile_dram"], m.dst_tile[:, :], 2 * B, side)
            m.acc = c.sb("acc", [T, NT, D + 1])
            message_phase(nc, m, io["recs"], io["b_table"], io["w1c"])
            with phase(nc) as side:
                fill_tokens(nc, m, io["tokens"], side)
                scatter_records(nc, m, "sg_", io["recs2"], m.dst_pos, m.dst_local, m.src_i, None, side, 0, EARLY)
                gru_phase(nc, m, io["gnn_w2"], io["L0_gnn_b2"], io["w_ih"], io["L0_gnn_b_ih"], io["w_hh"],
                          io["L0_gnn_b_hh"], side)
        with ExitStack() as moe:
            c = Pool_(nc, moe)
            m.expert = c.sb("expert", [T, 2 * NT])
            m.weight = c.sb("weight", [T, 2 * NT])
            m.slot = c.sb("slot", [T, 2 * NT], I32)
            m.block_expert = c.sb("block_expert", [1, MB], I32)
            m.b1s = c.sb("b1s", [B, NEX * 8])
            m.w1s = c.sb("w1s", [B, NEX * 2, HID])
            m.w2s = c.sb("w2s", [B, NEX * 8, D])
            with ExitStack() as inner:
                d = Pool_(nc, inner)
                m.ln = d.sb("ln", [T, NT, D])
                m.mv = d.sb("mv", [T, NT, 2])
                m.rstd = d.sb("rstd", [T, NT])
                with phase(nc) as side:
                    load_experts(nc, m, io["L0_ffn_W1"], io["L0_ffn_W2"], side)
                    normalize(nc, m, "l1_", m.ln, side)
                router_phase(nc, m, io["L0_ffn_Wr"], io["L0_ffn_br"])
                dispatch(nc, m, "dm_", m.expert[:, :], 2 * NT, NEX, 1, MB, m.slot[:, :], None,
                         io["expert_dram"], m.block_expert[:, :], B)
                with phase(nc) as side:
                    send_tokens(nc, m, io["tokens"], side)
                    shift_biases(nc, m, io["ln_b_cols"], io["b1_cols"], side)
            with phase(nc) as side:
                expert_phase(nc, m, io["tokens"], io["answers"], io["ln_g_cols"], io["b2_row"], side)
                scatter_records(nc, m, "sd_", io["recs2"], m.dst_pos, m.dst_local, m.src_i, None, side, EARLY)
            combine_phase(nc, m, io["answers"])
        m.ln = a.sb("ln2", [T, NT, D])
        with ExitStack() as gat:
            c = Pool_(nc, gat)
            m.to = c.sb("to", [T, NT])
            m.peak = c.sb("peak", [T, NT])
            m.acc = c.sb("acc2", [T, NT, HC])
            normalize(nc, m, "l2_", m.ln)
            attention_rows(nc, m, io["wg"], io["L1_gnn_a_src"], io["L1_gnn_a_dst"], io["table"])
            attention_phase(nc, m, io["recs2"], io["table"], io["L1_gnn_bias"])
        normalize(nc, m, "l3_", m.ln)
        mlp_phase(nc, m, io)


_AS_GIVEN = ["x", "src", "dst", "edge_attr_64", "L0_gnn_b1", "L0_gnn_b2", "L0_gnn_b_ih", "L0_gnn_b_hh", "L0_ffn_Wr",
             "L0_ffn_br", "L0_ffn_W1", "L0_ffn_W2", "L1_gnn_a_src", "L1_gnn_a_dst", "L1_gnn_bias", "L1_ffn_sW1",
             "L1_ffn_sW2", "L1_ffn_sW3", "L1_ffn_sb3", "L1_ffn_eW1", "L1_ffn_eW2", "L1_ffn_eW3", "L1_ffn_eb3",
             "L1_ffn_gW", "L1_ffn_gb"]
_SCRATCH = [("recs", (EB * B, REC), F32), ("recs2", (PB * 2 * B, 2), F32), ("b_table", (N, D), F32),
            ("src_tile_dram", (4 * B,), I32), ("dst_tile_dram", (4 * B,), I32), ("expert_dram", (4 * B,), I32),
            ("tokens", (MB * B, D), F32), ("answers", (MB * B, D), F32), ("table", (N, HC), F32)]


def kernel(**inputs):
    import numpy as _np
    import concourse.bacc as _bacc
    from concourse import mybir as _mybir
    from concourse.bass_utils import run_bass_kernel_spmd as _run

    nc = _bacc.Bacc("TRN2", target_bir_lowering=False, num_devices=1)
    given = {k: _np.asarray(v) for k, v in inputs.items()}
    arrays = {k: given[k] for k in _AS_GIVEN}
    w1 = given["L0_gnn_W1"]
    arrays["w1ab"] = _np.concatenate([w1[:, :D].T, w1[:, D:2 * D].T], axis=1)
    arrays["w1c"] = w1[:, 2 * D:].T
    arrays["gnn_w2"] = given["L0_gnn_W2"].T
    arrays["w_ih"] = given["L0_gnn_W_ih"].T
    arrays["w_hh"] = given["L0_gnn_W_hh"].T
    arrays["wg"] = given["L1_gnn_W"].T
    arrays["ln_g_cols"] = given["L0_ffn_ln_g"].reshape(NEX * 2, B).T
    arrays["ln_b_cols"] = given["L0_ffn_ln_b"].reshape(NEX * 2, B).T
    arrays["b1_cols"] = given["L0_ffn_b1"].reshape(NEX * 8, B).T
    arrays["b2_row"] = given["L0_ffn_b2"].reshape(NEX * D)
    arrays["sb1_cols"] = given["L1_ffn_sb1"].reshape(2, B).T
    arrays["sb2_cols"] = given["L1_ffn_sb2"].reshape(1, H2).T
    arrays["eb1_cols"] = given["L1_ffn_eb1"].T
    arrays["eb2_cols"] = given["L1_ffn_eb2"].T
    arrays = {"in_" + k: _np.ascontiguousarray(v) for k, v in arrays.items()}
    io = {k[3:]: nc.dram_tensor(k, v.shape, _mybir.dt.from_np(v.dtype), kind="ExternalInput").ap()
          for k, v in arrays.items()}
    for name, shape, dt in _SCRATCH:
        io[name] = nc.dram_tensor("scratch_" + name, shape, dt, kind="Internal").ap()
    io["out"] = nc.dram_tensor("out", (N, D), F32, kind="ExternalOutput").ap()
    build(nc, io)
    r = _run(nc, [arrays], core_ids=[0])
    return r.results[0]["out"]
```

```python
from contextlib import ExitStack, contextmanager

import concourse.bass as bass
from concourse import mybir

F32 = mybir.dt.float32
BF16 = mybir.dt.bfloat16
I32 = mybir.dt.int32
U32 = mybir.dt.uint32
ALU = mybir.AluOpType
ACT = mybir.ActivationFunctionType
AX_X = mybir.AxisListType.X

N, D = 3125, 256
E = 53125
EA = 64
T = 125
NT = N // T
EC = E // T
B = 128
G = 17
EARLY = 9
REC = EA + 2
EB = (E + (B - 1) * NT) // B
U = 20
EB += -EB % 8
PB = (E + (2 * B - 1) * NT) // (2 * B)
UP = 20
NEX, HID = 8, 1024
MB = (2 * N + (B - 1) * NEX) // B
MB += MB % 2
EPS = 1e-5
BIG = 1e30
HC = D + 2


def pipelined(eng, n, stages, U=2, row=None):
    most = max(st[0] for st in stages)
    first, end = (most + 2 * U - 1) // U, n // U
    if end - first < 2:
        first = end = (n + most + U - 1) // U
    looking = [(st[0], st[2]) for st in stages if len(st) > 2]
    back = max((lag for lag, _ in looking), default=0)
    back += -back % 4
    ahead = U - min((lag for lag, _ in looking), default=0)

    def numbers(start, count):
        if not looking or count <= 0:
            return []
        return eng.bass.values_load_multi_w_load_instructions(
            row[0:1, bass.ds(start, count)], engines=[eng.engine], min_val=0, max_val=looking[0][1],
            skip_runtime_bounds_check_because="dispatch has clamped every number of the row to 0..J-1")[1]

    def peeled(k):
        start = max(U * k - back, 0)
        found = numbers(start, min(U * k + ahead, n) - start)
        for s in range(U * k, min(U * k + U, n + most)):
            for lag, fn, *top in stages:
                if 0 <= s - lag < n:
                    fn((s - lag) // U, (s - lag) % U, *([found[s - lag - start]] if top else []))

    for k in range(first):
        peeled(k)
    if end > first:
        with eng.Fori(first, end) as k:
            found = numbers(k * U - back, back + ahead)
            for par in range(U):
                for lag, fn, *top in stages:
                    fn(k + (par - lag) // U, (par - lag) % U, *([found[back + par - lag]] if top else []))
        for k in range(end, (n + most + U - 1) // U):
            peeled(k)


def in_twos(fn):
    return lambda k, b, *number: fn(2 * k + b // 2, b % 2, *number)


def after(eng, sem, count):
    if not isinstance(count, int) or count > 0:
        eng.wait_ge(sem, count)


class Pool_:

    def __init__(self, nc, ctx):
        self.nc, self.ctx, self.sems, self.opened = nc, ctx, [], None

    def sb(self, name, shape, dt=F32):
        return self.ctx.enter_context(self.nc.sbuf_tensor("sb_" + name, shape, dt))

    def ps(self, name, shape, dt=F32):
        return self.ctx.enter_context(self.nc.psum_tensor("ps_" + name, shape, dt))

    def sem(self, name):
        self.sems.append(self.ctx.enter_context(self.nc.semaphore(name)))
        return self.sems[-1]

    def block(self):
        if self.opened is not None:
            return self.opened
        def clear():
            for s in self.sems:
                self.nc.gpsimd.sem_clear(s)
        self.ctx.callback(clear)
        self.opened = self.ctx.enter_context(self.nc.Block())
        return self.opened


@contextmanager
def phase(nc, shared=None):
    if shared is not None:
        yield shared
    else:
        with ExitStack() as ctx:
            yield Pool_(nc, ctx)


def chained(eng, sem):
    count = [0]

    def link(ins):
        count[0] += 1
        ins.then_inc(sem, 1)
        eng.wait_ge(sem, count[0])
    return link


def setup_phase(nc, m, shared=None):
    with phase(nc, shared) as a:
        ramp_i = a.sb("ramp_i", [B, B], I32)
        part_i = a.sb("part_i", [B, 4], I32)
        ramped = a.sem("ramped")
        chain = a.sem("setup_chain")
        block = a.block()

        @block.gpsimd
        def _(pool):
            nc.gpsimd.iota(ramp_i[:, :], pattern=[[1, B]], base=0, channel_multiplier=0).then_inc(ramped, 1)
            nc.gpsimd.iota(part_i[:, :], pattern=[[B, 4]], base=0, channel_multiplier=1).then_inc(ramped, 1)

        @block.vector
        def _(dve):
            link = chained(dve, chain)
            dve.wait_ge(ramped, 2)
            link(nc.vector.tensor_copy(m.ramp[:, :], ramp_i[:, :]))
            link(nc.vector.tensor_copy(m.part[:, :], part_i[:, :]))
            link(nc.vector.tensor_scalar(m.ident[:, :], m.ramp[:, :], m.part[:, 0:1], None, ALU.is_equal))
            link(nc.vector.tensor_copy(m.ident_b[:, :], m.ident[:, :]))
            link(nc.vector.tensor_scalar(m.upper[:, :], m.ramp[:, :], m.part[:, 0:1], None, ALU.is_gt))
            nc.vector.memset(m.ones[:, :], 1.0)


def dispatch(nc, m, name, key, C, J, width, blocks, pos_i, local, bucket_dram, bucket_row, unit, shared=None):
    with phase(nc, shared) as a:
        oh = a.sb(name + "oh", [T, J, C], BF16)
        near = a.sb(name + "near", [T, C])
        near_i = a.sb(name + "near_i", [T, C], I32)
        always = a.sb(name + "always", [T, 1], BF16)
        scan = a.sb(name + "scan", [T, J, C])
        cum = a.sb(name + "cum", [T, J + 1])
        count = a.sb(name + "count", [T, J])
        base = a.sb(name + "base", [T, J])
        posf = a.sb(name + "posf", [T, C])
        total = a.sb(name + "total", [B, J])
        total_i = a.sb(name + "total_i", [B, J], I32)
        nblk = a.sb(name + "nblk", [B, J])
        end = a.sb(name + "end", [B, J])
        one = a.sb(name + "one", [B, J])
        past = a.sb(name + "past", [B, 4, J])
        bkt = a.sb(name + "bkt", [B, 4])
        bkt_i = a.sb(name + "bkt_i", [B, 4], I32)
        p_before = a.ps(name + "p_before", [T, 512])
        p_total = a.ps(name + "p_total", [B, 512])
        counted = a.sem(name + "counted")
        summed = a.sem(name + "summed")
        bucketed = a.sem(name + "bucketed")
        stored = a.sem(name + "stored")
        chain = a.sem(name + "chain")
        block = a.block()

        @block.vector
        def _(dve):
            link = chained(dve, chain)
            first = key
            if local is not None:
                link(nc.vector.tensor_scalar(near_i[:, :], key, 1.0 / width, None, ALU.mult))
                link(nc.vector.tensor_copy(near[:, :], near_i[:, :]))
                link(nc.vector.scalar_tensor_tensor(out=local, in0=near[:, :], scalar=-float(width), in1=key,
                                                    op0=ALU.mult, op1=ALU.add))
                for limit, beyond, shift in ((0.0, ALU.is_lt, width), (float(width), ALU.is_ge, -width)):
                    link(nc.vector.tensor_scalar(near[:, :], local, limit, float(shift), beyond, ALU.mult))
                    link(nc.vector.tensor_tensor(local, local, near[:, :], ALU.add))
                link(nc.vector.tensor_tensor(near[:, :], key, local, ALU.subtract))
                first = near[:, :]
            nc.vector.memset(one[:, :], 1.0)
            nc.vector.memset(always[:, :], 1.0)
            link(nc.vector.memset(cum[:, 0:1], 0.0))
            for j in range(J):
                last = nc.vector.tensor_scalar(oh[:, j, :], first, float(width * j), None, ALU.is_equal)
            link(last)
            flat = "p j c -> p (j c)"
            link(nc.vector.tensor_tensor_scan(scan[:, :, :].rearrange(flat), always[:, :].to_broadcast([T, J * C]),
                                              oh[:, :, :].rearrange(flat), 0.0, ALU.mult, ALU.add))
            link(nc.vector.tensor_copy(cum[:, 1:J + 1], scan[:, :, C - 1]))
            nc.vector.tensor_tensor(count[:, :], cum[:, 1:J + 1], cum[:, 0:J], ALU.subtract).then_inc(counted, 1)
            dve.wait_ge(summed, 1)
            link(nc.vector.tensor_scalar(total_i[:, :], p_total[:, 0:J], float(unit - 1), None, ALU.add))
            link(nc.vector.tensor_scalar(total_i[:, :], total_i[:, :], unit.bit_length() - 1, None,
                                         ALU.arith_shift_right))
            link(nc.vector.tensor_copy(nblk[:, :], total_i[:, :]))
            link(nc.vector.tensor_tensor_scan(end[:, :], one[:, :], nblk[:, :], 0.0, ALU.mult, ALU.add))
            for i in range(4):
                last = nc.vector.tensor_scalar(past[:, i, :], end[:, :], m.part[:, i:i + 1], None, ALU.is_le)
            link(last)
            link(nc.vector.tensor_reduce(bkt[:, :], past[:, :, :], AX_X, ALU.add))
            nc.vector.tensor_scalar(bkt_i[:, :], bkt[:, :], float(J - 1), None, ALU.min).then_inc(bucketed, 1)
            link(nc.vector.tensor_tensor(total[:, :], end[:, :], nblk[:, :], ALU.subtract))
            link(nc.vector.scalar_tensor_tensor(out=base[:, :], in0=total[0:T, :], scalar=float(unit),
                                                in1=cum[:, 0:J], op0=ALU.mult, op1=ALU.subtract))
            link(nc.vector.scalar_tensor_tensor(out=base[:, :], in0=base[:, :], scalar=-1.0,
                                                in1=p_before[:, 0:J], op0=ALU.add, op1=ALU.add))
            for j in range(J):
                last = nc.vector.scalar_tensor_tensor(out=scan[:, j, :], in0=scan[:, j, :],
                                                      scalar=base[:, j:j + 1], in1=oh[:, j, :],
                                                      op0=ALU.add, op1=ALU.mult)
            link(last)
            link(nc.vector.tensor_reduce(posf[:, :], scan[:, :, :].rearrange("p j c -> p c j"), AX_X, ALU.add))
            link(nc.vector.tensor_copy(pos_i, posf[:, :]))

        @block.tensor
        def _(pe):
            pe.wait_ge(counted, 1)
            nc.tensor.matmul(p_before[:, 0:J], m.upper[0:T, 0:T], count[:, :], start=True, stop=True)
            nc.tensor.matmul(p_total[:, 0:J], m.ones[0:T, 0:B], count[:, :], start=True, stop=True).then_inc(summed, 1)

        @block.sync
        def _(sp):
            sp.wait_ge(bucketed, 1)
            with nc.allow_non_contiguous_dma(reason="a few hundred block numbers"):
                sp.dma_start(bucket_dram.rearrange("(i p) -> p i", p=B), bkt_i[:, :]).then_inc(stored, 16)
            sp.wait_ge(stored, 16)
            sp.dma_start(bucket_row, bucket_dram.rearrange("(a n) -> a n", a=1)[:, 0:blocks]).then_inc(stored, 16)
            sp.wait_ge(stored, 32)


def load_keys(nc, m, src, dst, shared=None):
    with phase(nc, shared) as a:
        loaded = a.sem("keys_loaded")
        chain = a.sem("keys_chain")
        block = a.block()

        @block.sync
        def _(sp):
            sp.dma_start(m.src_i[:, :], src.rearrange("(p c) -> p c", p=T)).then_inc(loaded, 16)
            sp.dma_start(m.dst_i[:, :], dst.rearrange("(p c) -> p c", p=T)).then_inc(loaded, 16)

        @block.vector
        def _(dve):
            link = chained(dve, chain)
            dve.wait_ge(loaded, 32)
            link(nc.vector.tensor_copy(m.src_f[:, :], m.src_i[:, :]))
            link(nc.vector.tensor_copy(m.dst_f[:, :], m.dst_i[:, :]))


def fill_records(nc, m, name, recs, cols, key_col, queue, shared=None):
    per = recs.shape[0] // B
    some = max(n for n in range(1, 41) if per % n == 0)
    with phase(nc, shared) as a:
        blank = a.sb(name + "blank", [B, some, cols])
        cleared = a.sem(name + "cleared")
        filled = a.sem(name + "filled")
        block = a.block()
        view = recs.rearrange("(p r) c -> p r c", p=B)

        @block.vector
        def _(dve):
            nc.vector.memset(blank[:, :, :], 0.0).then_inc(cleared, 1)
            dve.wait_ge(cleared, 1)
            nc.vector.memset(blank[:, :, key_col:key_col + 1], -1.0).then_inc(cleared, 1)

        @(block.sync if queue is nc.sync else block.scalar)
        def _(q):
            q.wait_ge(cleared, 2)
            with q.Fori(0, per // some) as i:
                q.dma_start(view[:, bass.ds(i * some, some), :], blank[:, :, :]).then_inc(filled, 16)
            q.wait_ge(filled, 16 * (per // some))


def scatter_records(nc, m, name, recs, pos_i, local, other_i, attrs, shared=None, first=0, last=EC // G):
    W = recs.shape[1]
    groups = last - first
    with phase(nc, shared) as a:
        rec = [a.sb(f"{name}rec{b}", [T, G, W]) for b in range(2)]
        pos = [a.sb(f"{name}pos{b}", [T, G], I32) for b in range(2)]
        attr_in = [a.sem(f"{name}attr_in{b}") for b in range(2)]
        built = a.sem(name + "built")
        sent = m.indirect_sems(2)
        block = a.block()

        if attrs is not None:
            view = attrs.rearrange("(p c) a -> p c a", p=T)

            @block.sync
            def _(sp):
                def load(k, b):
                    after(sp, sent[b], 16 * G * k)
                    sp.dma_start(rec[b][:, :, 0:EA], view[:, bass.ds((first + 2 * k + b) * G, G), :]).then_inc(attr_in[b], 16)
                pipelined(sp, groups, [(0, load)])

        @block.gpsimd
        def _(pool):
            def build(k, b):
                c = bass.ds((first + 2 * k + b) * G, G)
                after(pool, sent[b], 16 * G * k)
                pool.sem_inc(m.tick, 1)
                nc.gpsimd.tensor_copy(rec[b][:, :, W - 2], local[:, c])
                nc.gpsimd.tensor_copy(rec[b][:, :, W - 1].bitcast(I32), other_i[:, c])
                nc.gpsimd.tensor_copy(pos[b][:, :], pos_i[:, c]).then_inc(built, 1)

            def scatter(k, b):
                pool.wait_ge(built, 2 * k + b + 1)
                if attrs is not None:
                    pool.wait_ge(attr_in[b], 16 * (k + 1))
                pool.sem_inc(m.tick, 1)
                for g in range(G):
                    nc.gpsimd.indirect_dma_start(
                        out=recs, out_offset=bass.IndirectOffsetOnAxis(ap=pos[b][:, g:g + 1].bitcast(U32), axis=0),
                        in_=rec[b][:, g, :], in_offset=None).then_inc(sent[b], 16)
            pipelined(pool, groups, [(1, scatter), (0, build)])
            for b in range(2):
                pool.wait_ge(sent[b], 16 * G * ((groups + 1 - b) // 2))


def ln_stats(nc, dve, link, act_sem, sqrt_sem, n, src, mv, stats, stat_sem, rstd):
    if src is not None:
        with dve.Fori(0, NT // 5) as k:
            for i in range(5):
                nc.vector.bn_stats(tile_of(stats, k * 5 + i), src(k * 5 + i)).then_inc(stat_sem, 1)
    else:
        dve.sem_inc(stat_sem, NT)
    dve.wait_ge(stat_sem, 2 * NT * n + NT)
    for t in range(NT):
        last = nc.vector.bn_aggr(mv[:, t, :], stats[:, t, :])
    last.then_inc(stat_sem, NT)
    dve.wait_ge(stat_sem, 2 * NT * (n + 1))
    nc.vector.tensor_scalar(rstd[:, :], mv[:, :, 1], EPS, None, ALU.add).then_inc(act_sem, 1)
    dve.wait_ge(sqrt_sem, n + 1)
    link(nc.vector.reciprocal(rstd[:, :], rstd[:, :]))


def ln_root(nc, act, act_sem, sqrt_sem, n, rstd):
    act.wait_ge(act_sem, n + 1)
    nc.scalar.activation(rstd[:, :], rstd[:, :], ACT.Sqrt).then_inc(sqrt_sem, 1)


def tile_of(x, t):
    return x[:, bass.ds(t, 1), :].rearrange("p a d -> p (a d)")


def node_phase(nc, m, x, w1ab, b1, b_table, shared=None):
    with phase(nc, shared) as a:
        w = a.sb("w1ab", [B, 2, 2 * D])
        bias = a.sb("b1_all", [T, D])
        stats = a.sb("n_stats", [T, NT, 6])
        mv = a.sb("n_mv", [T, NT, 2])
        rstd = a.sb("n_rstd", [T, NT])
        left = a.sb("n_left", [T, D])
        rows = [a.sb(f"b_rows{b}", [T, D]) for b in range(2)]
        hT = [a.sb(f"n_hT{b}", [B, 2, T]) for b in range(2)]
        p_t = [a.ps(f"n_pt{b}", [B, 512]) for b in range(2)]
        p_ab = [a.ps(f"n_pab{b}", [T, 512]) for b in range(2)]
        x_in, w_in, stat, var_ok, rooted, chain = (a.sem("n_" + s) for s in ("x_in", "w_in", "stat", "var", "root", "ch"))
        hn = [a.sb(f"n_hn{b}", [T, D]) for b in range(2)]
        kept, parts = a.sem("n_kept"), a.sem("n_parts")
        normed, turned, copied, multiplied, split = (a.sem("n_" + s) for s in ("normed", "turned", "copied", "mul", "split"))
        stored = [a.sem(f"n_stored{b}") for b in range(2)]
        block = a.block()

        @block.scalar
        def _(act):
            act.dma_start(m.x[:, :, :], x.rearrange("(t p) d -> p t d", p=T)).then_inc(x_in, 16)
            act.dma_start(w[:, :, :], w1ab.rearrange("(k p) n -> p k n", p=B)).then_inc(w_in, 16)
            act.dma_start(bias[:, :], b1.rearrange("(a d) -> a d", a=1).to_broadcast([T, D])).then_inc(w_in, 16)

        @block.vector
        def _(dve):
            link = chained(dve, chain)
            dve.wait_ge(x_in, 16)
            ln_stats(nc, dve, link, var_ok, rooted, 0, lambda t: tile_of(m.x, t), mv, stats, stat, rstd)
            dve.wait_ge(w_in, 32)

            def norm(k, b):
                t = 2 * k + b
                after(dve, turned, t - 1)
                after(dve, kept, t - 1)
                nc.vector.tensor_scalar(hn[b][:, :], tile_of(m.x, t), mv[:, bass.ds(t, 1), 0],
                                        rstd[:, bass.ds(t, 1)], ALU.subtract, ALU.mult).then_inc(normed, 1)

            def spread(k, b):
                t = 2 * k + b
                dve.wait_ge(multiplied, t + 1)
                after(dve, stored[b], 16 * k)
                step = steps(dve, parts, 3 * t)
                high, middle, low = (tile_of(m.a, t)[:, i * D:(i + 1) * D] for i in range(3))
                step(nc.vector.tensor_copy(high, p_ab[b][:, 0:D]))
                step(nc.vector.tensor_tensor(left[:, :], p_ab[b][:, 0:D], high, ALU.subtract))
                step(nc.vector.tensor_copy(middle, left[:, :]))
                nc.vector.tensor_tensor(low, left[:, :], middle, ALU.subtract)
                nc.vector.tensor_tensor(rows[b][:, :], p_ab[b][:, D:2 * D], bias[:, :], ALU.add).then_inc(split, 1)
            pipelined(dve, NT, [(0, norm), (2, spread)])

        @block.scalar
        def _(act):
            ln_root(nc, act, var_ok, rooted, 0, rstd)

            def keep(k, b):
                act.wait_ge(normed, 2 * k + b + 1)
                nc.scalar.copy(tile_of(m.hn, 2 * k + b), hn[b][:, :]).then_inc(kept, 1)

            def copy(k, b):
                t = 2 * k + b
                act.wait_ge(turned, t + 1)
                after(act, multiplied, t - 1)
                nc.scalar.copy(hT[b][:, :, :].rearrange("p k n -> p (k n)"), p_t[b][:, 0:2 * T]).then_inc(copied, 1)

            def store(k, b):
                t = 2 * k + b
                act.wait_ge(split, t + 1)
                act.dma_start(b_table[bass.ds(t * T, T), :], rows[b][:, :]).then_inc(stored[b], 16)
            pipelined(act, NT, [(3, store), (0, keep), (0, copy)])
            for b in range(2):
                act.wait_ge(stored[b], 16 * ((NT + 1 - b) // 2))

        @block.tensor
        def _(pe):
            pe.wait_ge(w_in, 32)

            def turn(k, b):
                t = 2 * k + b
                pe.wait_ge(normed, t + 1)
                after(pe, copied, t - 1)
                for j in range(2):
                    last = nc.tensor.transpose(p_t[b][:, j * T:(j + 1) * T],
                                               hn[b][:, j * B:(j + 1) * B],
                                               m.ident[0:T, 0:T])
                last.then_inc(turned, 1)

            def multiply(k, b):
                t = 2 * k + b
                pe.wait_ge(copied, t + 1)
                after(pe, split, t - 1)
                for j in range(2):
                    last = nc.tensor.matmul(p_ab[b][:, :], hT[b][:, j, :], w[:, j, :], start=(j == 0), stop=(j == 1))
                last.then_inc(multiplied, 1)
            pipelined(pe, NT, [(0, turn), (1, multiply)])


def message_phase(nc, m, recs, b_table, w1c, shared=None):
    with phase(nc, shared) as a:
        w = a.sb("w1c", [2 * EA, D])
        rec = [a.sb(f"m_rec{b}", [B, 2, REC]) for b in range(U // 2)]
        got = [a.sb(f"m_got{b}", [B, D]) for b in range(U)]
        oh = [a.sb(f"m_oh{b}", [B, T]) for b in range(U)]
        oh_b = [a.sb(f"m_oh_b{b}", [B, T], BF16) for b in range(4)]
        attr = [a.sb(f"m_attr{b}", [B, 2, EA]) for b in range(2)]
        attrT = [a.sb(f"m_attrT{b}", [2 * EA, B]) for b in range(2)]
        ohT = [a.sb(f"m_ohT{b}", [T, B], BF16) for b in range(4)]
        msg = [a.sb(f"m_msg{b}", [B, D + 1]) for b in range(4)]
        p_t = [a.ps(f"m_pt{b}", [B, 512]) for b in range(2)]
        p_oh = [a.ps(f"m_poh{b}", [T, 1024], BF16) for b in range(2)]
        p_pre = [a.ps(f"m_pre{b}", [B, 512]) for b in range(2)]
        p_seg = [a.ps(f"m_seg{b}", [T, 512]) for b in range(2)]
        w_in = a.sem("m_w_in")
        rec_in = [a.sem(f"m_rec_in{b}") for b in range(U // 2)]
        got_in = m.indirect_sems(U)
        packed = a.sem("m_packed")
        marked, turned, copied, pre, added, relued, summed, taken, cleared = (
            a.sem("m_" + s) for s in ("marked", "turned", "copied", "pre", "added", "relued", "summed", "taken", "cleared"))
        block = a.block()

        @block.sync
        def _(sp):
            for h in range(2):
                sp.dma_start(w[h * EA:(h + 1) * EA, :], w1c).then_inc(w_in, 16)

            def load(k, b):
                q = U * k + 2 * b
                for h in range(2):
                    after(sp, got_in[2 * b + h], 16 * k)
                    sp.sem_inc(m.tick, 1)
                after(sp, turned, q + 1 - U + 1)
                sp.sem_inc(m.tick, 1)
                sp.dma_start(rec[b][:, :, :], recs[bass.ds(q * B, 2 * B), :].rearrange("(h p) c -> p h c", h=2)
                             ).then_inc(rec_in[b], 16)
            pipelined(sp, EB // 2, [(0, load)], U // 2)

        @block.gpsimd
        def _(pool):
            def gather(k, b):
                q = U * k + b
                pool.wait_ge(rec_in[b // 2], 16 * (k + 1))
                after(pool, added, q - U + 1)
                pool.sem_inc(m.tick, 1)
                nc.gpsimd.indirect_dma_start(
                    out=got[b][:, :], out_offset=None, in_=b_table,
                    in_offset=bass.IndirectOffsetOnAxis(ap=rec[b // 2][:, b % 2, EA + 1:EA + 2].bitcast(U32), axis=0)
                ).then_inc(got_in[b], 16)
            pipelined(pool, EB, [(0, gather)], U)

        @block.vector
        def _(dve):
            for b in range(4):
                nc.vector.memset(msg[b][:, D:D + 1], 1.0)
            nc.vector.memset(m.acc[:, :, :], 0.0).then_inc(cleared, 1)
            dve.wait_ge(cleared, 1)

            def mark(k, b):
                q = U * k + b
                dve.wait_ge(rec_in[b // 2], 16 * (k + 1))
                after(dve, summed, q - U + 1)
                after(dve, turned, q - 3)
                nc.vector.tensor_scalar(oh_b[b % 4][:, :], m.ramp[:, 0:T], rec[b // 2][:, b % 2, EA:EA + 1], None, ALU.is_equal)
                nc.vector.tensor_scalar(oh[b][:, :], m.ramp[:, 0:T], rec[b // 2][:, b % 2, EA:EA + 1], None,
                                        ALU.is_equal).then_inc(marked, 1)

            def add(k, b):
                q = U * k + b
                dve.wait_ge(pre, q + 1)
                dve.wait_ge(got_in[b], 16 * (k + 1))
                after(dve, summed, q - 3)
                nc.vector.tensor_tensor(msg[b % 4][:, 0:D], p_pre[b % 2][:, 0:D], got[b][:, :], ALU.add).then_inc(added, 1)

            def take(k, b, t):
                q = U * k + b
                dve.wait_ge(summed, q + 1)
                after(dve, taken, q)
                nc.vector.tensor_tensor(tile_of(m.acc, t), tile_of(m.acc, t), p_seg[b % 2][:, 0:D + 1],
                                        ALU.add).then_inc(taken, 1)
            pipelined(dve, EB, [(7, take, NT - 1), (4, add), (0, mark)], U, m.src_tile)

        @block.scalar
        def _(act):
            def pack(k, b):
                q = U * k + b
                if b % 2 == 0:
                    act.wait_ge(rec_in[b // 2], 16 * (k + 1))
                    after(act, turned, q - 3)
                    nc.scalar.copy(attr[b // 2 % 2][:, :, :], rec[b // 2][:, :, 0:EA]).then_inc(packed, 1)

            def copy(k, b):
                q = U * k + b
                act.wait_ge(turned, q + 1)
                after(act, pre, q - 2 if b % 2 == 0 else q - 3)
                if b % 2 == 0:
                    nc.scalar.copy(attrT[b // 2 % 2][:, :], p_t[b // 2 % 2][:, 0:B])
                nc.scalar.copy(ohT[b % 4][:, :], p_oh[b % 2][:, 0:B]).then_inc(copied, 1)

            def relu(k, b):
                q = U * k + b
                act.wait_ge(added, q + 1)
                nc.scalar.activation(msg[b % 4][:, 0:D], msg[b % 4][:, 0:D], ACT.Relu).then_inc(relued, 1)
            pipelined(act, EB, [(5, relu), (2, copy), (0, pack)], U)

        @block.tensor
        def _(pe):
            pe.wait_ge(w_in, 32)
            pe.wait_ge(cleared, 1)

            def turn(k, b):
                q = U * k + b
                pe.wait_ge(marked, q + 1)
                after(pe, copied, q - 1)
                if b % 2 == 0:
                    pe.wait_ge(packed, (U // 2) * k + b // 2 + 1)
                    nc.tensor.transpose(p_t[b // 2 % 2][:, 0:B], attr[b // 2 % 2][:, :, :].rearrange("p h a -> p (h a)"),
                                        m.ident[:, :])
                nc.tensor.transpose(p_oh[b % 2][:, 0:B], oh_b[b % 4][:, :], m.ident_b[:, :]).then_inc(turned, 1)

            def sum_up(k, b, t):
                q = U * k + b
                pe.wait_ge(copied, q + 1)
                after(pe, added, q - 1)
                half = slice(b % 2 * EA, (b % 2 + 1) * EA)
                nc.tensor.matmul(p_pre[b % 2][:, 0:D], attrT[b // 2 % 2][half, :], w[half, :], start=True, stop=False)
                for i in range(3):
                    last = nc.tensor.matmul(p_pre[b % 2][:, 0:D], ohT[b % 4][:, :],
                                            tile_of(m.a, t)[:, i * D:(i + 1) * D], start=False, stop=(i == 2))
                last.then_inc(pre, 1)

            def segment(k, b):
                q = U * k + b
                pe.wait_ge(relued, q + 1)
                after(pe, taken, q - 1)
                nc.tensor.matmul(p_seg[b % 2][:, 0:D + 1], oh[b][:, :], msg[b % 4][:, :], start=True, stop=True).then_inc(summed, 1)
            pipelined(pe, EB, [(6, segment), (3, sum_up, NT - 1), (1, turn)], U, m.src_tile)


def steps(eng, sem, start):
    count = [0]

    def step(ins):
        count[0] += 1
        ins.then_inc(sem, 1)
        eng.wait_ge(sem, start + count[0])
    return step


def row_to_all(v, rows):
    return v.rearrange("(a d) -> a d", a=1).to_broadcast([rows, v.shape[0]])


def load_gru(nc, m, w2, b2, w_ih, b_ih, w_hh, b_hh, shared=None):
    with phase(nc, shared) as a:
        block = a.block()

        @block.sync
        def _(sp):
            for dst, src in zip(m.gru[0:3], (w2, w_ih, w_hh)):
                sp.dma_start(dst[:, :, :], src.rearrange("(k p) n -> p k n", p=B)).then_inc(m.gru_in, 16)
            for dst, src in zip(m.gru[3:6], (b2, b_ih, b_hh)):
                sp.dma_start(dst[:, :], row_to_all(src, T)).then_inc(m.gru_in, 16)


def gru_phase(nc, m, shared=None):
    with phase(nc, shared) as a:
        w2s, wih, whh, b2s, bih, bhh = m.gru
        sums = [a.sb(f"g_sums{b}", [T, D + 1]) for b in range(2)]
        hid = [a.sb(f"g_hid{b}", [T, D]) for b in range(2)]
        shT = [a.sb(f"g_shT{b}", [B, 4, T]) for b in range(4)]
        agg = [a.sb(f"g_agg{b}", [T, D]) for b in range(2)]
        aggT = [a.sb(f"g_aggT{b}", [B, 2, T]) for b in range(2)]
        rz = [a.sb(f"g_rz{b}", [T, 2 * D]) for b in range(2)]
        cand = [a.sb(f"g_cand{b}", [T, D]) for b in range(2)]
        part = a.sb("g_part", [T, D])
        p_sh = a.ps("g_psh", [B, 512])
        p_agg = a.ps("g_pagg", [T, 512])
        p_aggT = a.ps("g_paggT", [B, 512])
        p_rz = [a.ps(f"g_prz{b}", [T, 512]) for b in range(2)]
        p_n = [a.ps(f"g_pn{b}", [T, 512]) for b in range(2)]
        w_in = m.gru_in
        bias_ok = a.sem("g_bias_ok")
        (staged, turned, copied, agg_mul, agg_done, agg_turned, agg_copied, gates, preact, opened, pre_n, squashed,
         mixed, chain_n, chain_x) = (a.sem("g_" + s) for s in (
             "staged", "turned", "copied", "agg_mul", "agg_done", "agg_turned", "agg_copied", "gates", "preact",
             "opened", "pre_n", "squashed", "mixed", "chain_n", "chain_x"))
        block = a.block()

        @block.tensor
        def _(pe):
            pe.wait_ge(w_in, 96)

            def turn(k, b):
                t = 2 * k + b
                pe.wait_ge(staged, t + 1)
                after(pe, copied, t)
                for j in range(2):
                    nc.tensor.transpose(p_sh[:, j * T:(j + 1) * T], sums[b][:, j * B:(j + 1) * B], m.ident[0:T, 0:T])
                for j in range(2):
                    last = nc.tensor.transpose(p_sh[:, (2 + j) * T:(3 + j) * T], hid[b][:, j * B:(j + 1) * B],
                                               m.ident[0:T, 0:T])
                last.then_inc(turned, 1)

            def aggregate(k, b):
                t = 4 * k + b
                pe.wait_ge(copied, t + 1)
                after(pe, agg_done, t)
                for j in range(2):
                    last = nc.tensor.matmul(p_agg[:, 0:D], shT[b][:, j, :], w2s[:, j, :], start=(j == 0), stop=(j == 1))
                last.then_inc(agg_mul, 1)

            def turn_agg(k, b):
                t = 4 * k + b
                pe.wait_ge(agg_done, t + 1)
                after(pe, agg_copied, t)
                for j in range(2):
                    last = nc.tensor.transpose(p_aggT[:, j * T:(j + 1) * T], agg[b % 2][:, j * B:(j + 1) * B],
                                               m.ident[0:T, 0:T])
                last.then_inc(agg_turned, 1)

            def gate(k, b):
                t = 4 * k + b
                pe.wait_ge(agg_copied, t + 1)
                after(pe, preact, t - 1)
                after(pe, pre_n, t - 1)
                c = b % 2
                for j in range(2):
                    nc.tensor.matmul(p_rz[c][:, :], aggT[c][:, j, :], wih[:, j, 0:2 * D], start=(j == 0), stop=False)
                for j in range(2):
                    nc.tensor.matmul(p_rz[c][:, :], shT[b][:, 2 + j, :], whh[:, j, 0:2 * D], start=False, stop=(j == 1))
                for j in range(2):
                    nc.tensor.matmul(p_n[c][:, 0:D], aggT[c][:, j, :], wih[:, j, 2 * D:], start=(j == 0), stop=(j == 1))
                for j in range(2):
                    last = nc.tensor.matmul(p_n[c][:, D:2 * D], shT[b][:, 2 + j, :], whh[:, j, 2 * D:],
                                            start=(j == 0), stop=(j == 1))
                last.then_inc(gates, 1)
            pipelined(pe, NT, [(3, turn_agg), (2, aggregate), (1, in_twos(turn)), (4, gate)], 4)

        @block.scalar
        def _(act):
            def stage(k, b):
                t = 2 * k + b
                after(act, turned, t - 1)
                after(act, agg_done, t - 1)
                nc.scalar.copy(sums[b][:, :], tile_of(m.acc, t))
                nc.scalar.copy(hid[b][:, :], tile_of(m.hn, t)).then_inc(staged, 1)

            def copy(k, b):
                t = 4 * k + b
                act.wait_ge(turned, t + 1)
                after(act, gates, t - 3)
                nc.scalar.copy(shT[b][:, :, :].rearrange("p k n -> p (k n)"), p_sh[:, 0:4 * T]).then_inc(copied, 1)

            def copy_agg(k, b):
                t = 4 * k + b
                act.wait_ge(agg_turned, t + 1)
                after(act, gates, t - 1)
                nc.scalar.copy(aggT[b % 2][:, :, :].rearrange("p k n -> p (k n)"), p_aggT[:, 0:2 * T]).then_inc(agg_copied, 1)

            def open_gates(k, b):
                t = 4 * k + b
                act.wait_ge(preact, t + 1)
                nc.scalar.activation(rz[b % 2][:, :], rz[b % 2][:, :], ACT.Sigmoid).then_inc(opened, 1)

            def squash(k, b):
                t = 4 * k + b
                act.wait_ge(pre_n, t + 1)
                nc.scalar.activation(cand[b % 2][:, :], cand[b % 2][:, :], ACT.Tanh).then_inc(squashed, 1)
            pipelined(act, NT, [(3, copy_agg), (1, copy), (5, open_gates), (5, squash), (0, in_twos(stage))], 4)

        @block.vector
        def _(dve):
            dve.wait_ge(w_in, 96)
            nc.vector.tensor_tensor(bih[:, 0:2 * D], bih[:, 0:2 * D], bhh[:, 0:2 * D], ALU.add).then_inc(bias_ok, 1)
            dve.wait_ge(bias_ok, 1)

            def biased(k, b):
                t = 4 * k + b
                dve.wait_ge(agg_mul, t + 1)
                after(dve, agg_turned, t - 1)
                nc.vector.scalar_tensor_tensor(out=agg[b % 2][:, :], in0=b2s[:, :], scalar=sums[b % 2][:, D:D + 1],
                                               in1=p_agg[:, 0:D], op0=ALU.mult, op1=ALU.add).then_inc(agg_done, 1)

            def pre(k, b):
                t = 4 * k + b
                c = b % 2
                step = steps(dve, chain_n, 3 * t)
                dve.wait_ge(gates, t + 1)
                after(dve, mixed, t - 1)
                nc.vector.tensor_tensor(rz[c][:, :], p_rz[c][:, :], bih[:, 0:2 * D], ALU.add).then_inc(preact, 1)
                step(nc.vector.tensor_tensor(cand[c][:, :], p_n[c][:, D:2 * D], bhh[:, 2 * D:], ALU.add))

            def pre_new(k, b):
                t = 4 * k + b
                c = b % 2
                step = steps(dve, chain_n, 3 * t + 1)
                dve.wait_ge(opened, t + 1)
                step(nc.vector.tensor_tensor(cand[c][:, :], cand[c][:, :], rz[c][:, 0:D], ALU.mult))
                step(nc.vector.tensor_tensor(cand[c][:, :], cand[c][:, :], bih[:, 2 * D:], ALU.add))
                nc.vector.tensor_tensor(cand[c][:, :], cand[c][:, :], p_n[c][:, 0:D], ALU.add).then_inc(pre_n, 1)

            def mix(k, b):
                t = 4 * k + b
                c = b % 2
                step = steps(dve, chain_x, 4 * t)
                dve.wait_ge(squashed, t + 1)
                step(nc.vector.tensor_tensor(part[:, :], tile_of(m.hn, t), cand[c][:, :], ALU.subtract))
                step(nc.vector.tensor_tensor(part[:, :], part[:, :], rz[c][:, D:2 * D], ALU.mult))
                step(nc.vector.tensor_tensor(part[:, :], part[:, :], cand[c][:, :], ALU.add))
                step(nc.vector.tensor_tensor(tile_of(m.x, t), tile_of(m.x, t), part[:, :], ALU.add))
                nc.vector.bn_stats(tile_of(m.stats, t), tile_of(m.x, t)).then_inc(mixed, 1)
            pipelined(dve, NT, [(1, biased), (4, pre), (5, mix), (4, pre_new)], 4)


def normalize(nc, m, name, dst, shared=None):
    with phase(nc, shared) as a:
        stats = m.stats
        mv = a.sb(name + "mv", [T, NT, 2])
        rstd = a.sb(name + "rstd", [T, NT])
        stat, var_ok, rooted, chain, normed = (a.sem(name + s) for s in ("stat", "var", "root", "ch", "normed"))
        block = a.block()

        @block.vector
        def _(dve):
            link = chained(dve, chain)
            ln_stats(nc, dve, link, var_ok, rooted, 0, None, mv, stats, stat, rstd)
            with dve.Fori(0, NT // 5) as k:
                for t in (k * 5 + i for i in range(5)):
                    nc.vector.tensor_scalar(tile_of(dst, t), tile_of(m.x, t), mv[:, bass.ds(t, 1), 0],
                                            rstd[:, bass.ds(t, 1)], ALU.subtract, ALU.mult).then_inc(normed, 1)

        @block.scalar
        def _(act):
            ln_root(nc, act, var_ok, rooted, 0, rstd)
        return normed


def load_experts(nc, m, w1, w2, shared=None):
    with phase(nc, shared) as a:
        block = a.block()

        @block.sync
        def _(sp):
            for e in range(NEX):
                sp.dma_start(m.w1s[:, 2 * e:2 * e + 2, :], w1[e].rearrange("(k p) h -> p k h", p=B)).then_inc(m.weights_in, 16)
                sp.dma_start(m.w2s[:, 8 * e:8 * e + 8, :], w2[e].rearrange("(j p) d -> p j d", p=B)).then_inc(m.weights_in, 16)


def router_phase(nc, m, wr, br, normed, shared=None):
    with phase(nc, shared) as a:
        w = a.sb("r_w", [B, 2, NEX])
        bias = a.sb("r_b", [T, NEX])
        stats = a.sb("r_stats", [T, NT, 6])
        ln = [a.sb(f"r_ln{b}", [T, D]) for b in range(2)]
        lnT = [a.sb(f"r_lnT{b}", [B, 2, T]) for b in range(2)]
        logit = a.sb("r_logit", [T, NT, NEX])
        same = a.sb("r_same", [T, NT, NEX])
        last_first = a.sb("r_last_first", [T, NT, NEX])
        top = a.sb("r_top", [T, 2, NT])
        gap = a.sb("r_gap", [T, NT])
        den = a.sb("r_den", [T, NT])
        p_t = [a.ps(f"r_pt{b}", [B, 512]) for b in range(2)]
        p_l = [a.ps(f"r_pl{b}", [T, 512]) for b in range(2)]
        w_in, stat, var_ok, rooted, chain = (a.sem("r_" + s) for s in ("w", "stat", "var", "root", "ch"))
        staged, turned, copied, mul, found, gap_ok, exp_ok = (
            a.sem("r_" + s) for s in ("staged", "turned", "copied", "mul", "found", "gap_ok", "exp_ok"))
        block = a.block()

        @block.sync
        def _(sp):
            sp.dma_start(w[:, :, :], wr.rearrange("(k p) n -> p k n", p=B)).then_inc(w_in, 16)
            sp.dma_start(bias[:, :], row_to_all(br, T)).then_inc(w_in, 16)

        @block.vector
        def _(dve):
            link = chained(dve, chain)
            dve.wait_ge(normed, NT)
            ln_stats(nc, dve, link, var_ok, rooted, 0, lambda t: tile_of(m.ln, t), m.mv, stats, stat, m.rstd)
            dve.wait_ge(w_in, 32)

            for e in range(NEX):
                last = nc.vector.memset(last_first[:, :, e:e + 1], float(NEX - e))
            link(last)

            def add_bias(k, b):
                t = 2 * k + b
                dve.wait_ge(mul, t + 1)
                nc.vector.tensor_tensor(tile_of(logit, t), p_l[b][:, 0:NEX], bias[:, :], ALU.add).then_inc(found, 1)
            pipelined(dve, NT, [(0, add_bias)])
            dve.wait_ge(found, NT)
            for i in range(2):
                expert = m.expert[:, i * NT:(i + 1) * NT]
                link(nc.vector.tensor_reduce(top[:, i, :], logit[:, :, :], AX_X, ALU.max))
                link(nc.vector.tensor_tensor(same[:, :, :], logit[:, :, :],
                                             top[:, i, :].unsqueeze(2).to_broadcast([T, NT, NEX]), ALU.is_equal))
                link(nc.vector.tensor_tensor(same[:, :, :], same[:, :, :], last_first[:, :, :], ALU.mult))
                link(nc.vector.tensor_reduce(expert, same[:, :, :], AX_X, ALU.max))
                if i == 0:
                    link(nc.vector.tensor_tensor(same[:, :, :], last_first[:, :, :],
                                                 expert.unsqueeze(2).to_broadcast([T, NT, NEX]), ALU.is_equal))
                    link(nc.vector.scalar_tensor_tensor(out=logit[:, :, :], in0=same[:, :, :], scalar=-BIG,
                                                        in1=logit[:, :, :], op0=ALU.mult, op1=ALU.add))
            link(nc.vector.tensor_scalar(m.expert[:, :], m.expert[:, :], -1.0, float(NEX), ALU.mult, ALU.add))
            nc.vector.tensor_tensor(gap[:, :], top[:, 1, :], top[:, 0, :], ALU.subtract).then_inc(gap_ok, 1)
            dve.wait_ge(exp_ok, 1)
            link(nc.vector.tensor_scalar(den[:, :], gap[:, :], 1.0, None, ALU.add))
            link(nc.vector.reciprocal(m.weight[:, 0:NT], den[:, :]))
            link(nc.vector.tensor_tensor(m.weight[:, NT:2 * NT], gap[:, :], m.weight[:, 0:NT], ALU.mult))

        @block.scalar
        def _(act):
            ln_root(nc, act, var_ok, rooted, 0, m.rstd)

            def stage(k, b):
                t = 2 * k + b
                act.wait_ge(normed, t + 1)
                after(act, turned, t - 1)
                nc.scalar.copy(ln[b][:, :], tile_of(m.ln, t)).then_inc(staged, 1)

            def copy(k, b):
                t = 2 * k + b
                act.wait_ge(turned, t + 1)
                after(act, mul, t - 1)
                nc.scalar.copy(lnT[b][:, :, :].rearrange("p k n -> p (k n)"), p_t[b][:, 0:2 * T]).then_inc(copied, 1)
            pipelined(act, NT, [(0, stage), (1, copy)])
            act.wait_ge(gap_ok, 1)
            nc.scalar.activation(gap[:, :], gap[:, :], ACT.Exp).then_inc(exp_ok, 1)

        @block.tensor
        def _(pe):
            pe.wait_ge(w_in, 32)

            def turn(k, b):
                t = 2 * k + b
                pe.wait_ge(staged, t + 1)
                after(pe, copied, t - 1)
                for j in range(2):
                    last = nc.tensor.transpose(p_t[b][:, j * T:(j + 1) * T], ln[b][:, j * B:(j + 1) * B],
                                               m.ident[0:T, 0:T])
                last.then_inc(turned, 1)

            def multiply(k, b):
                t = 2 * k + b
                pe.wait_ge(copied, t + 1)
                after(pe, found, t - 1)
                for j in range(2):
                    last = nc.tensor.matmul(p_l[b][:, 0:NEX], lnT[b][:, j, :], w[:, j, :], start=(j == 0), stop=(j == 1))
                last.then_inc(mul, 1)
            pipelined(pe, NT, [(2, multiply), (0, turn)])


def fill_tokens(nc, m, tokens, shared=None):
    per = MB * B // B
    some = 8
    with phase(nc, shared) as a:
        blank = a.sb("t_blank", [B, some, D])
        cleared, filled = a.sem("t_cleared"), a.sem("t_filled")
        block = a.block()
        view = tokens.rearrange("(p r) c -> p r c", p=B)

        @block.gpsimd
        def _(pool):
            nc.gpsimd.memset(blank[:, :, :], 0.0).then_inc(cleared, 1)

        @block.sync
        def _(sp):
            sp.wait_ge(cleared, 1)
            with sp.Fori(0, per // some) as i:
                sp.dma_start(view[:, bass.ds(i * some, some), :], blank[:, :, :]).then_inc(filled, 16)
            sp.wait_ge(filled, 16 * (per // some))


def send_tokens(nc, m, tokens, shared=None):
    BUF = 5
    with phase(nc, shared) as a:
        xn = [a.sb(f"t_xn{b}", [T, D]) for b in range(BUF)]
        pos = [a.sb(f"t_pos{b}", [T, 2], I32) for b in range(BUF)]
        built = a.sem("t_built")
        sent = m.indirect_sems(BUF)
        block = a.block()

        @block.vector
        def _(dve):
            def build(k, b):
                t = BUF * k + b
                after(dve, sent[b], 32 * k)
                nc.vector.tensor_copy(pos[b][:, 0:1], m.slot[:, bass.ds(t, 1)])
                nc.vector.tensor_copy(pos[b][:, 1:2], m.slot[:, bass.ds(t + NT, 1)])
                nc.vector.tensor_scalar(xn[b][:, :], tile_of(m.ln, t), m.mv[:, bass.ds(t, 1), 0],
                                        m.rstd[:, bass.ds(t, 1)], ALU.subtract, ALU.mult).then_inc(built, 1)
            pipelined(dve, NT, [(0, build)], BUF)

        @block.gpsimd
        def _(pool):
            def scatter(k, b):
                pool.wait_ge(built, BUF * k + b + 1)
                pool.sem_inc(m.tick, 1)
                for g in range(2):
                    nc.gpsimd.indirect_dma_start(
                        out=tokens, out_offset=bass.IndirectOffsetOnAxis(ap=pos[b][:, g:g + 1].bitcast(U32), axis=0),
                        in_=xn[b][:, :], in_offset=None).then_inc(sent[b], 16)
            pipelined(pool, NT, [(0, scatter)], BUF)
            for b in range(BUF):
                pool.wait_ge(sent[b], 32 * (NT // BUF))


def shift_biases(nc, m, ln_b, b1, shared=None):
    with phase(nc, shared) as a:
        shift = a.sb("b_shift", [B, NEX * 2])
        p_b = a.ps("b_pb", [B, 512])
        small_in, shifted = a.sem("b_small"), a.sem("b_shifted")
        block = a.block()

        @block.sync
        def _(sp):
            sp.dma_start(shift[:, :], ln_b).then_inc(small_in, 16)
            sp.dma_start(m.b1s[:, :], b1).then_inc(small_in, 16)

        @block.tensor
        def _(pe):
            pe.wait_ge(small_in, 32)
            pe.wait_ge(m.weights_in, 32 * NEX)
            for e in range(NEX):
                for j in range(8):
                    for k in range(2):
                        last = nc.tensor.matmul(p_b[:, 8 * e + j:8 * e + j + 1], m.w1s[:, 2 * e + k, j * B:(j + 1) * B],
                                                shift[:, 2 * e + k:2 * e + k + 1], start=(k == 0), stop=(k == 1))
            last.then_inc(shifted, 1)

        @block.vector
        def _(dve):
            dve.wait_ge(small_in, 32)
            dve.wait_ge(shifted, 1)
            nc.vector.tensor_tensor(m.b1s[:, :], p_b[:, 0:8 * NEX], m.b1s[:, :], ALU.add)


def expert_phase(nc, m, tokens, answers, ln_g, b2, shared=None):
    with phase(nc, shared) as a:
        w1s, w2s = m.w1s, m.w2s
        gain = a.sb("e_gain", [B, NEX * 2])
        b1s = m.b1s
        b2s = a.sb("e_b2", [B, NEX, D])
        tok = [a.sb(f"e_tok{b}", [B, D]) for b in range(2)]
        tokT = [a.sb(f"e_tokT{b}", [B, 2, B]) for b in range(2)]
        wg = [a.sb(f"e_wg{b}", [B, 2, HID]) for b in range(2)]
        hid = [a.sb(f"e_hid{b}", [B, 8, B]) for b in range(2)]
        ans = [a.sb(f"e_ans{b}", [B, D]) for b in range(2)]
        p_t = a.ps("e_pt", [B, 512])
        p_h = [[a.ps(f"e_ph{b}{i}", [B, 512]) for i in range(2)] for b in range(2)]
        p_y = [a.ps(f"e_py{b}", [B, 512]) for b in range(2)]
        small_in = a.sem("e_small")
        tok_in = [a.sem(f"e_tok_in{b}") for b in range(2)]
        stored = [a.sem(f"e_stored{b}") for b in range(2)]
        turned, copied, weighted, up, act_ok, down, answered = (
            a.sem("e_" + s) for s in ("turned", "copied", "weighted", "up", "act_ok", "down", "answered"))
        block = a.block()

        @block.sync
        def _(sp):
            sp.dma_start(gain[:, :], ln_g).then_inc(small_in, 16)
            sp.dma_start(b2s[:, :, :].rearrange("p e d -> p (e d)"), row_to_all(b2, B)).then_inc(small_in, 16)

            def load(k, b):
                q = 2 * k + b
                after(sp, turned, q - 1)
                sp.sem_inc(m.tick, 1)
                sp.dma_start(tok[b][:, :], tokens[bass.ds(q * B, B), :]).then_inc(tok_in[b], 16)

            def store(k, b):
                q = 2 * k + b
                sp.wait_ge(answered, q + 1)
                sp.sem_inc(m.tick, 1)
                sp.dma_start(answers[bass.ds(q * B, B), :], ans[b][:, :]).then_inc(stored[b], 16)
            pipelined(sp, MB, [(4, in_twos(store)), (0, in_twos(load))], 4)
            for b in range(2):
                sp.wait_ge(stored[b], 16 * (MB // 2))

        @block.tensor
        def _(pe):
            pe.wait_ge(m.weights_in, 32 * NEX)

            def turn(k, b):
                q = 2 * k + b
                pe.wait_ge(tok_in[b], 16 * (k + 1))
                after(pe, copied, q)
                for j in range(2):
                    last = nc.tensor.transpose(p_t[:, j * B:(j + 1) * B], tok[b][:, j * B:(j + 1) * B], m.ident[:, :])
                last.then_inc(turned, 1)

            def rise(k, b):
                q = 2 * k + b
                pe.wait_ge(copied, q + 1)
                pe.wait_ge(weighted, q + 1)
                after(pe, act_ok, q - 1)
                for j in range(8):
                    for i in range(2):
                        last = nc.tensor.matmul(p_h[b][j // 4][:, (j % 4) * B:(j % 4 + 1) * B],
                                                wg[b][:, i, j * B:(j + 1) * B], tokT[b][:, i, :],
                                                start=(i == 0), stop=(i == 1))
                last.then_inc(up, 1)

            def fall(k, b, e):
                q = 2 * k + b
                pe.wait_ge(act_ok, q + 1)
                after(pe, answered, q - 1)
                for j in range(8):
                    last = nc.tensor.matmul(p_y[b][:, 0:D], hid[b][:, j, :], tile_of(w2s, e * 8 + j),
                                            start=(j == 0), stop=(j == 7))
                last.then_inc(down, 1)
            pipelined(pe, MB, [(1, in_twos(rise)), (0, in_twos(turn)), (2, in_twos(fall), NEX - 1)], 4,
                      m.block_expert)

        @block.scalar
        def _(act):
            def copy(k, b):
                q = 2 * k + b
                act.wait_ge(turned, q + 1)
                after(act, up, q - 1)
                nc.scalar.copy(tokT[b][:, :, :].rearrange("p k n -> p (k n)"), p_t[:, 0:2 * B]).then_inc(copied, 1)

            def gelu(k, b, e):
                q = 2 * k + b
                act.wait_ge(up, q + 1)
                after(act, down, q - 1)
                for j in range(8):
                    last = nc.scalar.activation(hid[b][:, j, :], p_h[b][j // 4][:, (j % 4) * B:(j % 4 + 1) * B],
                                                ACT.Gelu, bias=b1s[:, bass.ds(e * 8 + j, 1)])
                last.then_inc(act_ok, 1)
            pipelined(act, MB, [(1, in_twos(gelu), NEX - 1), (0, in_twos(copy))], 4, m.block_expert)

        @block.vector
        def _(dve):
            dve.wait_ge(small_in, 32)
            dve.wait_ge(m.weights_in, 32 * NEX)

            def weigh(k, b, e):
                q = 2 * k + b
                after(dve, up, q - 1)
                for i in range(2):
                    last = nc.vector.tensor_scalar(wg[b][:, i, :], tile_of(w1s, e * 2 + i),
                                                   gain[:, bass.ds(e * 2 + i, 1)], None, ALU.mult)
                last.then_inc(weighted, 1)

            def answer(k, b, e):
                q = 2 * k + b
                dve.wait_ge(down, q + 1)
                after(dve, stored[b], 16 * k)
                nc.vector.tensor_tensor(ans[b][:, :], p_y[b][:, 0:D], tile_of(b2s, e), ALU.add).then_inc(answered, 1)
            pipelined(dve, MB, [(3, in_twos(answer), NEX - 1), (0, in_twos(weigh), NEX - 1)], 4, m.block_expert)


def combine_phase(nc, m, answers, shared=None):
    BUF = 5
    with phase(nc, shared) as a:
        pos = [a.sb(f"c_pos{b}", [T, 2], I32) for b in range(BUF)]
        got = [[a.sb(f"c_got{b}{g}", [T, D]) for g in range(2)] for b in range(BUF)]
        built, added, chain = (a.sem("c_" + s) for s in ("built", "added", "chain"))
        got_in = m.indirect_sems(BUF)
        block = a.block()

        @block.gpsimd
        def _(pool):
            def gather(k, b):
                pool.wait_ge(built, BUF * k + b + 1)
                pool.sem_inc(m.tick, 1)
                for g in range(2):
                    nc.gpsimd.indirect_dma_start(
                        out=got[b][g][:, :], out_offset=None, in_=answers,
                        in_offset=bass.IndirectOffsetOnAxis(ap=pos[b][:, g:g + 1].bitcast(U32), axis=0)
                    ).then_inc(got_in[b], 16)
            pipelined(pool, NT, [(0, gather)], BUF)

        @block.vector
        def _(dve):
            def build(k, b):
                t = BUF * k + b
                after(dve, added, t - BUF + 1)
                nc.vector.tensor_copy(pos[b][:, 0:1], m.slot[:, bass.ds(t, 1)])
                nc.vector.tensor_copy(pos[b][:, 1:2], m.slot[:, bass.ds(t + NT, 1)]).then_inc(built, 1)

            def add(k, b):
                t = BUF * k + b
                step = steps(dve, chain, 2 * t)
                dve.wait_ge(got_in[b], 32 * (k + 1))
                step(nc.vector.scalar_tensor_tensor(out=tile_of(m.x, t), in0=got[b][0][:, :],
                                                    scalar=m.weight[:, bass.ds(t, 1)], in1=tile_of(m.x, t),
                                                    op0=ALU.mult, op1=ALU.add))
                step(nc.vector.scalar_tensor_tensor(out=tile_of(m.x, t), in0=got[b][1][:, :],
                                                    scalar=m.weight[:, bass.ds(t + NT, 1)], in1=tile_of(m.x, t),
                                                    op0=ALU.mult, op1=ALU.add))
                nc.vector.bn_stats(tile_of(m.stats, t), tile_of(m.x, t)).then_inc(added, 1)
            pipelined(dve, NT, [(3, add), (0, build)], BUF)


def attention_rows(nc, m, wg, a_src, a_dst, table, normed, shared=None):
    with phase(nc, shared) as a:
        w = a.sb("h_w", [B, 2, D])
        a_s = a.sb("h_as", [T, D])
        a_d = a.sb("h_ad", [T, D])
        ln = [a.sb(f"h_ln{b}", [T, D]) for b in range(2)]
        lnT = [a.sb(f"h_lnT{b}", [B, 2, T]) for b in range(2)]
        row = [a.sb(f"h_row{b}", [T, HC]) for b in range(4)]
        junk = a.sb("h_junk", [T, 2, D])
        to = [a.sb(f"h_to{b}", [T, 1]) for b in range(4)]
        p_t = [a.ps(f"h_pt{b}", [B, 512]) for b in range(2)]
        p_h = [a.ps(f"h_ph{b}", [T, 512]) for b in range(2)]
        w_in, staged, turned, copied, mul, made, kept, one, chain, chain_p = (
            a.sem("h_" + s) for s in ("w", "staged", "turned", "copied", "mul", "made", "kept", "one", "chain", "chain_p"))
        stored = [a.sem(f"h_stored{b}") for b in range(4)]
        block = a.block()

        @block.sync
        def _(sp):
            sp.dma_start(w[:, :, :], wg.rearrange("(k p) n -> p k n", p=B)).then_inc(w_in, 16)
            sp.dma_start(a_s[:, :], row_to_all(a_src, T)).then_inc(w_in, 16)
            sp.dma_start(a_d[:, :], row_to_all(a_dst, T)).then_inc(w_in, 16)

            def store(k, b):
                t = 4 * k + b
                sp.wait_ge(made, t + 1)
                sp.sem_inc(m.tick, 1)
                sp.dma_start(table[bass.ds(t * T, T), :], row[b][:, :]).then_inc(stored[b], 16)
            pipelined(sp, NT, [(0, store)], 4)
            for b in range(4):
                sp.wait_ge(stored[b], 16 * ((NT + 3 - b) // 4))

        @block.gpsimd
        def _(pool):
            pool.wait_ge(normed, NT)
            with pool.Fori(0, NT // 5) as k:
                for t in (k * 5 + i for i in range(5)):
                    nc.gpsimd.tensor_tensor(tile_of(m.x, t), tile_of(m.x, t), tile_of(m.ln, t), ALU.add)

        @block.scalar
        def _(act):
            def stage(k, b):
                t = 2 * k + b
                act.wait_ge(normed, t + 1)
                after(act, turned, t - 1)
                nc.scalar.copy(ln[b][:, :], tile_of(m.ln, t)).then_inc(staged, 1)

            def keep(k, b):
                t = 4 * k + b
                act.wait_ge(made, t + 1)
                nc.scalar.copy(tile_of(m.acc, t), row[b][:, :]).then_inc(kept, 1)

            def copy(k, b):
                t = 2 * k + b
                act.wait_ge(turned, t + 1)
                after(act, mul, t - 1)
                nc.scalar.copy(lnT[b][:, :, :].rearrange("p k n -> p (k n)"), p_t[b][:, 0:2 * T]).then_inc(copied, 1)
            pipelined(act, NT, [(4, keep), (0, in_twos(stage)), (1, in_twos(copy))], 4)

        @block.tensor
        def _(pe):
            pe.wait_ge(w_in, 48)

            def turn(k, b):
                t = 2 * k + b
                pe.wait_ge(staged, t + 1)
                after(pe, copied, t - 1)
                for j in range(2):
                    last = nc.tensor.transpose(p_t[b][:, j * T:(j + 1) * T], ln[b][:, j * B:(j + 1) * B],
                                               m.ident[0:T, 0:T])
                last.then_inc(turned, 1)

            def multiply(k, b):
                t = 2 * k + b
                pe.wait_ge(copied, t + 1)
                after(pe, made, t - 1)
                for j in range(2):
                    last = nc.tensor.matmul(p_h[b][:, 0:D], lnT[b][:, j, :], w[:, j, :], start=(j == 0), stop=(j == 1))
                last.then_inc(mul, 1)
            pipelined(pe, NT, [(2, multiply), (0, turn)])

        @block.vector
        def _(dve):
            for b in range(4):
                last = nc.vector.memset(row[b][:, D + 1:D + 2], 1.0)
            last.then_inc(one, 1)
            dve.wait_ge(one, 1)
            dve.wait_ge(w_in, 48)

            def make(k, b):
                t = 4 * k + b
                step = steps(dve, chain, 2 * t)
                dve.wait_ge(mul, t + 1)
                after(dve, stored[b], 16 * k)
                after(dve, kept, t - 3)
                step(nc.vector.tensor_copy(row[b][:, 0:D], p_h[b % 2][:, 0:D]))
                nc.vector.tensor_tensor_reduce(out=junk[:, 0, :], in0=row[b][:, 0:D], in1=a_s[:, :], scale=1.0,
                                               scalar=0.0, op0=ALU.mult, op1=ALU.add,
                                               accum_out=row[b][:, D:D + 1])
                step(nc.vector.tensor_tensor_reduce(out=junk[:, 1, :], in0=row[b][:, 0:D], in1=a_d[:, :], scale=1.0,
                                                    scalar=0.0, op0=ALU.mult, op1=ALU.add, accum_out=to[b][:, :]))
                nc.vector.tensor_copy(m.to[:, bass.ds(t, 1)], to[b][:, :]).then_inc(made, 1)
            pipelined(dve, NT, [(0, make)], 4)
            dve.wait_ge(made, NT)
            dve.wait_ge(kept, NT)
            link = chained(dve, chain_p)
            link(nc.vector.tensor_tensor(m.peak[:, :], m.acc[:, :, D], m.to[:, :], ALU.add))
            link(nc.vector.scalar_tensor_tensor(out=m.peak[:, :], in0=m.peak[:, :], scalar=0.2, in1=m.peak[:, :],
                                                op0=ALU.mult, op1=ALU.max))


def attention_phase(nc, m, recs, table, bias, shared=None):
    with phase(nc, shared) as a:
        peak = m.peak
        rec = [a.sb(f"a_rec{b}", [B, 2, 2]) for b in range(UP)]
        got = [a.sb(f"a_got{b}", [B, 2, HC]) for b in range(UP)]
        mark = [a.sb(f"a_mark{b}", [B, 2, T]) for b in range(4)]
        top = [a.sb(f"a_top{b}", [T, 4]) for b in range(4)]
        shrink = [a.sb(f"a_shrink{b}", [T, 1]) for b in range(UP)]
        score = [a.sb(f"a_score{b}", [T, 2 * B]) for b in range(4)]
        probT = [a.sb(f"a_probT{b}", [B, 2 * T]) for b in range(4)]
        bias_s = a.sb("a_bias", [T, D])
        den = a.sb("a_den", [T, NT])
        out = [a.sb(f"a_out{b}", [T, D]) for b in range(5)]
        p_m = [a.ps(f"a_pm{b}", [T, 512]) for b in range(2)]
        p_p = [a.ps(f"a_pp{b}", [B, 512]) for b in range(2)]
        p_o = [a.ps(f"a_po{b}", [T, 512]) for b in range(2)]
        rec_in = [a.sem(f"a_rec_in{b}") for b in range(UP)]
        got_in = m.indirect_sems(UP)
        (w_in, placed, marked, turned, shifted, leaked, found, grown, compared, scored, prob, prob_turned, prob_copied,
         summed, shrunk, taken, chain, divided, finished) = (
            a.sem("a_" + s) for s in ("w", "placed", "marked", "turned", "shifted", "leaked", "found", "grown", "compared",
                                      "scored", "prob", "prob_turned", "prob_copied", "summed", "shrunk", "taken",
                                      "chain", "divided", "finished"))
        block = a.block()

        @block.sync
        def _(sp):
            sp.dma_start(bias_s[:, :], row_to_all(bias, T)).then_inc(w_in, 16)

            def load(k, b):
                q = UP * k + b
                after(sp, got_in[b], 32 * k)
                sp.sem_inc(m.tick, 1)
                after(sp, marked, q - UP + 1)
                sp.sem_inc(m.tick, 1)
                sp.dma_start(rec[b][:, :, :], recs[bass.ds(q * 2 * B, 2 * B), :].rearrange("(p h) c -> p h c", h=2)
                             ).then_inc(rec_in[b], 16)
            pipelined(sp, PB, [(0, load)], UP)

        @block.gpsimd
        def _(pool):
            def gather(k, b):
                q = UP * k + b
                pool.wait_ge(rec_in[b], 16 * (k + 1))
                after(pool, summed, q - UP + 1)
                pool.sem_inc(m.tick, 1)
                for h in range(2):
                    nc.gpsimd.indirect_dma_start(
                        out=got[b][:, h, :], out_offset=None, in_=table,
                        in_offset=bass.IndirectOffsetOnAxis(ap=rec[b][:, h, 1:2].bitcast(U32), axis=0)
                    ).then_inc(got_in[b], 16)
            pipelined(pool, PB, [(0, gather)], UP)

        @block.vector
        def _(dve):
            link = chained(dve, chain)

            def select_a(k, b):
                q = UP * k + b
                dve.wait_ge(rec_in[b], 16 * (k + 1))
                after(dve, turned, q - 3)
                for h in range(2):
                    last = nc.vector.tensor_scalar(mark[b % 4][:, h, :], m.ramp[:, 0:T], rec[b][:, h, 0:1], BIG,
                                                   ALU.is_equal, ALU.mult)
                last.then_inc(placed, 1)

            def select_b(k, b):
                q = UP * k + b
                dve.wait_ge(got_in[b], 32 * (k + 1))
                dve.wait_ge(placed, q + 1)
                for h in range(2):
                    last = nc.vector.tensor_scalar(mark[b % 4][:, h, :], mark[b % 4][:, h, :], BIG,
                                                   got[b][:, h, D:D + 1], ALU.subtract, ALU.add)
                last.then_inc(marked, 1)

            def leak(k, b):
                c = b % 4
                dve.wait_ge(shifted, UP * k + b + 1)
                nc.vector.scalar_tensor_tensor(out=score[c][:, :], in0=score[c][:, :], scalar=0.2,
                                               in1=score[c][:, :], op0=ALU.mult, op1=ALU.max).then_inc(leaked, 1)

            def peak_a(k, b):
                q = UP * k + b
                dve.wait_ge(leaked, q + 1)
                after(dve, shrunk, q - 3)
                nc.vector.tensor_reduce(top[b % 4][:, 1:2], score[b % 4][:, :], AX_X, ALU.max).then_inc(found, 1)

            def peak_b(k, b, t):
                q = UP * k + b
                dve.wait_ge(found, q + 1)
                after(dve, scored, q)
                nc.vector.tensor_scalar(top[b % 4][:, 2:3], top[b % 4][:, 1:2], peak[:, bass.ds(t, 1)], -1.0,
                                        ALU.max, ALU.mult).then_inc(grown, 1)

            def peak_c(k, b, t):
                q = UP * k + b
                dve.wait_ge(grown, q + 1)
                nc.vector.tensor_tensor(top[b % 4][:, 3:4], top[b % 4][:, 2:3], peak[:, bass.ds(t, 1)],
                                        ALU.add).then_inc(compared, 1)

            def peak_d(k, b, t):
                dve.wait_ge(compared, UP * k + b + 1)
                nc.vector.tensor_scalar(peak[:, bass.ds(t, 1)], top[b % 4][:, 2:3], -1.0, None,
                                        ALU.mult).then_inc(scored, 1)

            def take(k, b, t):
                q = UP * k + b
                dve.wait_ge(summed, q + 1)
                dve.wait_ge(shrunk, q + 1)
                after(dve, taken, q)
                nc.vector.scalar_tensor_tensor(out=tile_of(m.acc, t), in0=tile_of(m.acc, t),
                                               scalar=shrink[b][:, :], in1=p_o[b % 2][:, 0:HC],
                                               op0=ALU.mult, op1=ALU.add).then_inc(taken, 1)

            pipelined(dve, PB, [(3, leak), (4, peak_d, NT - 1), (0, select_a), (3, peak_a), (8, take, NT - 1),
                                (3, peak_b, NT - 1), (0, select_b), (3, peak_c, NT - 1)], UP, m.dst_tile)
            dve.wait_ge(taken, PB)
            dve.wait_ge(w_in, 16)
            link(nc.vector.reciprocal(den[:, :], m.acc[:, :, D + 1]))

            def divide(k, b):
                t = 5 * k + b
                after(dve, finished, t - 4)
                nc.vector.scalar_tensor_tensor(out=out[b][:, :], in0=tile_of(m.acc, t)[:, 0:D],
                                               scalar=den[:, bass.ds(t, 1)], in1=bias_s[:, :],
                                               op0=ALU.mult, op1=ALU.add).then_inc(divided, 1)

            def finish(k, b):
                t = 5 * k + b
                dve.wait_ge(divided, t + 1)
                nc.vector.scalar_tensor_tensor(out=tile_of(m.x, t), in0=out[b][:, :], scalar=0.0, in1=tile_of(m.x, t),
                                               op0=ALU.max, op1=ALU.add).then_inc(finished, 1)

            def measure(k, b):
                dve.wait_ge(finished, 5 * k + b + 1)
                nc.vector.bn_stats(tile_of(m.stats, 5 * k + b), tile_of(m.x, 5 * k + b))
            pipelined(dve, NT, [(0, divide), (1, finish), (2, measure)], 5)

        @block.scalar
        def _(act):
            def shift(k, b, t):
                q = UP * k + b
                act.wait_ge(turned, q + 1)
                after(act, prob_turned, q - 3)
                nc.scalar.activation(score[b % 4][:, :], p_m[b % 2][:, 0:2 * B], ACT.Identity,
                                     bias=m.to[:, bass.ds(t, 1)]).then_inc(shifted, 1)

            def weigh(k, b):
                q = UP * k + b
                c = b % 4
                act.wait_ge(leaked, q + 1)
                act.wait_ge(scored, q + 1)
                after(act, taken, q - UP + 1)
                nc.scalar.activation(score[c][:, :], score[c][:, :], ACT.Exp, bias=top[c][:, 2:3]).then_inc(prob, 1)
                nc.scalar.activation(shrink[b][:, :], top[c][:, 3:4], ACT.Exp).then_inc(shrunk, 1)

            def copy(k, b):
                q = UP * k + b
                act.wait_ge(prob_turned, q + 1)
                after(act, summed, q - 3)
                nc.scalar.copy(probT[b % 4][:, :], p_p[b % 2][:, 0:2 * T]).then_inc(prob_copied, 1)
            pipelined(act, PB, [(6, copy), (4, weigh), (2, shift, NT - 1)], UP, m.dst_tile)

        @block.tensor
        def _(pe):
            def turn(k, b):
                q = UP * k + b
                pe.wait_ge(marked, q + 1)
                after(pe, shifted, q - 1)
                for h in range(2):
                    last = nc.tensor.transpose(p_m[b % 2][0:T, h * B:(h + 1) * B], mark[b % 4][:, h, :], m.ident[:, :])
                last.then_inc(turned, 1)

            def turn_prob(k, b):
                q = UP * k + b
                pe.wait_ge(prob, q + 1)
                after(pe, prob_copied, q - 1)
                for h in range(2):
                    last = nc.tensor.transpose(p_p[b % 2][:, h * T:(h + 1) * T], score[b % 4][:, h * B:(h + 1) * B],
                                               m.ident[0:T, 0:T])
                last.then_inc(prob_turned, 1)

            def gather_sum(k, b):
                q = UP * k + b
                pe.wait_ge(prob_copied, q + 1)
                after(pe, taken, q - 1)
                pe.wait_ge(got_in[b], 32 * (k + 1))
                for h in range(2):
                    last = nc.tensor.matmul(p_o[b % 2][:, 0:HC], probT[b % 4][:, h * T:(h + 1) * T], got[b][:, h, :],
                                            start=(h == 0), stop=(h == 1))
                last.then_inc(summed, 1)
            pipelined(pe, PB, [(7, gather_sum), (5, turn_prob), (1, turn)], UP)


H1, H2 = 256, 128
X1, X2, NX = 128, 64, 4
MLP_LOADS = 14


def load_mlp(nc, m, io, shared=None):
    with phase(nc, shared) as a:
        gw, gb, sw1, sb1, sw2, sb2, sw3, sb3, ew1, eb1, ew2, eb2, ew3 = m.mlp
        loads = ((gw[:, :, :], io["L1_ffn_gW"].rearrange("(k p) n -> p k n", p=B)),
                 (gb[:, :], row_to_all(io["L1_ffn_gb"], T)),
                 (sw1[:, :, :], io["L1_ffn_sW1"].rearrange("(k p) n -> p k n", p=B)),
                 (sb1[:, :], io["sb1_cols"]),
                 (sw2[:, :, :], io["L1_ffn_sW2"].rearrange("(k p) n -> p k n", p=B)),
                 (sb2[:, :], io["sb2_cols"]),
                 (sw3[:, :], io["L1_ffn_sW3"]),
                 (sb3[:, :], row_to_all(io["L1_ffn_sb3"], T)),
                 (ew1[:, :, :], io["L1_ffn_eW1"].rearrange("e (k p) n -> p (e k) n", p=B)),
                 (eb1[:, :], io["eb1_cols"]),
                 (ew2[:, :, :], io["L1_ffn_eW2"].rearrange("e p n -> p e n")),
                 (eb2[:, :], io["eb2_cols"]),
                 (ew3[0:X2, :, :], io["L1_ffn_eW3"].rearrange("e p n -> p e n")),
                 (ew3[X2:X2 + 1, :, :], io["L1_ffn_eb3"].rearrange("(a e) n -> a e n", a=1)))
        assert len(loads) == MLP_LOADS
        block = a.block()

        @block.sync
        def _(sp):
            for dst, src in loads:
                sp.dma_start(dst, src).then_inc(m.mlp_in, 16)


def mlp_phase(nc, m, io, normed, shared=None):
    with phase(nc, shared) as a:
        gw, gb, sw1, sb1, sw2, sb2, sw3, sb3, ew1, eb1, ew2, eb2, ew3 = m.mlp
        ln = [a.sb(f"f_ln{b}", [T, D]) for b in range(2)]
        lnT = [a.sb(f"f_lnT{b}", [B, 2, T]) for b in range(2)]
        gates = [a.sb(f"f_gates{b}", [T, 8]) for b in range(2)]
        top = [a.sb(f"f_top{b}", [T, 8]) for b in range(2)]
        at = [a.sb(f"f_at{b}", [T, 8], U32) for b in range(2)]
        atf = [a.sb(f"f_atf{b}", [T, 2]) for b in range(2)]
        small = [a.sb(f"f_small{b}", [T, 8]) for b in range(2)]
        share = [a.sb(f"f_share{b}", [T, 2 * NX]) for b in range(2)]
        s1 = [a.sb(f"f_s1{b}", [B, 2, T]) for b in range(2)]
        s2 = [a.sb(f"f_s2{b}", [H2, T]) for b in range(2)]
        e1 = [a.sb(f"f_e1{b}", [X1, NX, T]) for b in range(2)]
        e2 = [a.sb(f"f_e2{b}", [X2 + 1, NX, T]) for b in range(2)]
        p_t = a.ps("f_pt", [B, 512])
        p_s1 = a.ps("f_ps1", [B, 512])
        p_s2 = a.ps("f_ps2", [H2, 512])
        p_e1 = a.ps("f_pe1", [B, 512])
        p_e2 = a.ps("f_pe2", [X2, 512])
        p_s3 = a.ps("f_ps3", [T, 512])
        p_e3 = [a.ps(f"f_pe3{i}", [T, 512]) for i in range(2)]
        (staged, turned, copied, gated, gate_read, e1_mul, e1_ok, s1_mul, s1_ok, s2_mul, s2_ok, e2_mul, e2_ok,
         out_mul, added, chain_g, chain_d, chain_a, top_ok, exp_ok, gap_ok, gap_exp, ready, stored) = (
            a.sem("f_" + s) for s in (
                "staged", "turned", "copied", "gated", "gate_read", "e1_mul", "e1_ok", "s1_mul", "s1_ok",
                "s2_mul", "s2_ok", "e2_mul", "e2_ok", "out_mul", "added", "chain_g", "chain_d", "chain_a", "top_ok", "exp_ok",
                "gap_ok", "gap_exp", "ready", "stored"))
        block = a.block()

        @block.sync
        def _(sp):
            out = io["out"].rearrange("(t p) d -> p t d", p=T)
            for i in range(0, NT, 5):
                sp.wait_ge(added, i + 5)
                sp.dma_start(out[:, i:i + 5, :], m.x[:, i:i + 5, :]).then_inc(stored, 16)
            sp.wait_ge(stored, 16 * (NT // 5))

        @block.gpsimd
        def _(pool):
            link = chained(pool, ready)
            for b in range(2):
                link(nc.gpsimd.memset(gates[b][:, :], -1.0))
                link(nc.gpsimd.memset(e2[b][X2:X2 + 1, :, :], 1.0))

            def stage(k, b):
                t = 2 * k + b
                pool.wait_ge(normed, t + 1)
                after(pool, turned, t - 1)
                nc.gpsimd.tensor_copy(ln[b][:, :], tile_of(m.ln, t)).then_inc(staged, 1)
            pipelined(pool, NT, [(0, stage)])

        @block.tensor
        def _(pe):
            pe.wait_ge(m.mlp_in, 16 * MLP_LOADS)
            pe.wait_ge(ready, 4)

            def turn(k, b):
                t = 2 * k + b
                pe.wait_ge(staged, t + 1)
                after(pe, gate_read, t)
                for j in range(2):
                    last = nc.tensor.transpose(p_t[:, j * T:(j + 1) * T], ln[b][:, j * B:(j + 1) * B],
                                               m.ident[0:T, 0:T])
                last.then_inc(turned, 1)

            def gate(k, b):
                t = 2 * k + b
                pe.wait_ge(copied, t + 1)
                for j in range(2):
                    last = nc.tensor.matmul(p_t[0:T, 256:256 + NX], lnT[b][:, j, :], gw[:, j, :],
                                            start=(j == 0), stop=(j == 1))
                last.then_inc(gated, 1)

            def first(k, b):
                t = 2 * k + b
                after(pe, s1_ok, t)
                for i in range(2):
                    for j in range(2):
                        last = nc.tensor.matmul(p_s1[:, i * T:(i + 1) * T], sw1[:, j, i * B:(i + 1) * B],
                                                lnT[b][:, j, :], start=(j == 0), stop=(j == 1))
                last.then_inc(s1_mul, 1)
                after(pe, e1_ok, t)
                for e in range(NX):
                    for j in range(2):
                        last = nc.tensor.matmul(p_e1[:, e * T:(e + 1) * T], ew1[:, 2 * e + j, :], lnT[b][:, j, :],
                                                start=(j == 0), stop=(j == 1))
                last.then_inc(e1_mul, 1)

            def second(k, b):
                t = 2 * k + b
                pe.wait_ge(s1_ok, t + 1)
                after(pe, s2_ok, t)
                for j in range(2):
                    last = nc.tensor.matmul(p_s2[:, 0:T], sw2[:, j, :], s1[b][:, j, :],
                                            start=(j == 0), stop=(j == 1))
                last.then_inc(s2_mul, 1)
                pe.wait_ge(e1_ok, t + 1)
                after(pe, e2_ok, t)
                for e in range(NX):
                    last = nc.tensor.matmul(p_e2[:, e * T:(e + 1) * T], ew2[:, e, :], e1[b][:, e, :],
                                            start=True, stop=True)
                last.then_inc(e2_mul, 1)

            def third(k, b):
                t = 2 * k + b
                pe.wait_ge(s2_ok, t + 1)
                pe.wait_ge(e2_ok, t + 1)
                after(pe, added, t)
                nc.tensor.matmul(p_s3[:, 0:D], s2[b][:, :], sw3[:, :], start=True, stop=True)
                for e in range(NX):
                    last = nc.tensor.matmul(p_e3[e // 2][:, (e % 2) * D:(e % 2 + 1) * D], e2[b][:, e, :],
                                            ew3[:, e, :], start=True, stop=True)
                last.then_inc(out_mul, 1)
            pipelined(pe, NT, [(1, gate), (3, third), (2, second), (0, turn), (1, first)])

        @block.scalar
        def _(act):
            act.wait_ge(m.mlp_in, 16 * MLP_LOADS)

            def copy(k, b):
                t = 2 * k + b
                act.wait_ge(turned, t + 1)
                after(act, e1_mul, t - 1)
                nc.scalar.copy(lnT[b][:, :, :].rearrange("p k n -> p (k n)"), p_t[:, 0:2 * T]).then_inc(copied, 1)

            def first(k, b):
                t = 2 * k + b
                act.wait_ge(s1_mul, t + 1)
                after(act, s2_mul, t - 1)
                for i in range(2):
                    last = nc.scalar.activation(s1[b][:, i, :], p_s1[:, i * T:(i + 1) * T], ACT.Relu, bias=sb1[:, i:i + 1])
                last.then_inc(s1_ok, 1)
                act.wait_ge(e1_mul, t + 1)
                after(act, e2_mul, t - 1)
                for e in range(NX):
                    last = nc.scalar.activation(e1[b][:, e, :], p_e1[:, e * T:(e + 1) * T], ACT.Relu,
                                                bias=eb1[:, e:e + 1])
                last.then_inc(e1_ok, 1)

            def second(k, b):
                t = 2 * k + b
                act.wait_ge(s2_mul, t + 1)
                after(act, out_mul, t - 1)
                nc.scalar.activation(s2[b][:, :], p_s2[:, 0:T], ACT.Relu, bias=sb2[:, 0:1]).then_inc(s2_ok, 1)
                act.wait_ge(e2_mul, t + 1)
                for e in range(NX):
                    last = nc.scalar.activation(e2[b][0:X2, e, :], p_e2[:, e * T:(e + 1) * T], ACT.Relu,
                                                bias=eb2[:, e:e + 1])
                last.then_inc(e2_ok, 1)

            def gate_exp(k, b):
                t = 2 * k + b
                act.wait_ge(top_ok, t + 1)
                nc.scalar.activation(gates[b][:, 0:NX], gates[b][:, 0:NX], ACT.Exp, bias=small[b][:, 0:1]).then_inc(exp_ok, 1)

            def gap_exp_(k, b):
                act.wait_ge(gap_ok, 2 * k + b + 1)
                nc.scalar.activation(small[b][:, 3:4], small[b][:, 3:4], ACT.Exp).then_inc(gap_exp, 1)
            pipelined(act, NT, [(1, gate_exp), (2, second), (0, copy), (1, first), (1, gap_exp_)])

        @block.vector
        def _(dve):
            dve.wait_ge(ready, 4)
            dve.wait_ge(m.mlp_in, 16 * MLP_LOADS)

            def gate(k, b):
                t = 2 * k + b
                g, s = gates[b], small[b]
                step = steps(dve, chain_g, 7 * t)
                dve.wait_ge(gated, t + 1)
                nc.vector.tensor_tensor(g[:, 0:NX], p_t[0:T, 256:256 + NX], gb[:, :], ALU.add).then_inc(gate_read, 1)
                dve.wait_ge(gate_read, t + 1)
                step(nc.vector.tensor_reduce(s[:, 0:1], g[:, 0:NX], AX_X, ALU.max))
                nc.vector.tensor_scalar(s[:, 0:1], s[:, 0:1], -1.0, None, ALU.mult).then_inc(top_ok, 1)

            def choose(k, b):
                t = 2 * k + b
                g, s = gates[b], small[b]
                step = steps(dve, chain_g, 7 * t + 1)
                dve.wait_ge(exp_ok, t + 1)
                step(nc.vector.tensor_reduce(s[:, 1:2], g[:, 0:NX], AX_X, ALU.add))
                step(nc.vector.reciprocal(s[:, 2:3], s[:, 1:2]))
                step(nc.vector.tensor_scalar(g[:, 0:NX], g[:, 0:NX], s[:, 2:3], None, ALU.mult))
                dve.sem_inc(m.tick, 1)
                step(nc.vector.max(top[b][:, :], g[:, :]))
                dve.sem_inc(m.tick, 1)
                step(nc.vector.max_index(at[b][:, :], top[b][:, :], g[:, :]))
                step(nc.vector.tensor_copy(atf[b][:, :], at[b][:, 0:2]))
                nc.vector.tensor_tensor(s[:, 3:4], top[b][:, 1:2], top[b][:, 0:1], ALU.subtract).then_inc(gap_ok, 1)

            def divide(k, b):
                t = 2 * k + b
                s = small[b]
                step = steps(dve, chain_d, 6 * t)
                dve.wait_ge(gap_exp, t + 1)
                step(nc.vector.tensor_scalar(s[:, 4:5], s[:, 3:4], 1.0, None, ALU.add))
                step(nc.vector.reciprocal(s[:, 5:6], s[:, 4:5]))
                step(nc.vector.tensor_tensor(s[:, 6:7], s[:, 3:4], s[:, 5:6], ALU.mult))
                step(nc.vector.tensor_scalar(share[b][:, 0:NX], m.ramp[0:T, 0:NX], atf[b][:, 0:1], s[:, 5:6],
                                             ALU.is_equal, ALU.mult))
                step(nc.vector.tensor_scalar(share[b][:, NX:2 * NX], m.ramp[0:T, 0:NX], atf[b][:, 1:2], s[:, 6:7],
                                             ALU.is_equal, ALU.mult))
                step(nc.vector.tensor_tensor(share[b][:, 0:NX], share[b][:, 0:NX], share[b][:, NX:2 * NX], ALU.add))

            def add(k, b):
                t = 2 * k + b
                step = steps(dve, chain_a, (1 + NX) * t)
                dve.wait_ge(out_mul, t + 1)
                step(nc.vector.tensor_tensor(tile_of(m.x, t), tile_of(m.x, t), sb3[:, :], ALU.add))
                step(nc.vector.tensor_tensor(tile_of(m.x, t), tile_of(m.x, t), p_s3[:, 0:D], ALU.add))
                for e in range(NX):
                    ins = nc.vector.scalar_tensor_tensor(
                        out=tile_of(m.x, t), in0=p_e3[e // 2][:, (e % 2) * D:(e % 2 + 1) * D],
                        scalar=share[b][:, e:e + 1], in1=tile_of(m.x, t), op0=ALU.mult, op1=ALU.add)
                    if e < NX - 1:
                        step(ins)
                ins.then_inc(added, 1)
            pipelined(dve, NT, [(2, divide), (1, gate), (3, add), (1, choose)])


class Mem:

    def indirect_sems(self, n):
        first = len(self.kept.sems)
        return [self.kept.sem(f"indirect{first + b}") for b in range(n)]


def build(nc, io):
    m = Mem()
    with ExitStack() as ctx:
        a = Pool_(nc, ctx)
        m.ramp = a.sb("ramp", [B, B])
        m.part = a.sb("part", [B, 4])
        m.stats = a.sb("stats", [T, NT, 6])
        m.ident = a.sb("ident", [B, B])
        m.ident_b = a.sb("ident_b", [B, B], BF16)
        m.upper = a.sb("upper", [B, B])
        m.ones = a.sb("ones", [B, B])
        m.x = a.sb("x", [T, NT, D])
        m.src_tile = a.sb("src_tile", [1, EB], I32)
        m.dst_tile = a.sb("dst_tile", [1, PB], I32)
        m.tick = a.sem("tick")
        m.weights_in = a.sem("weights_in")
        m.gru_in = a.sem("gru_in")
        m.mlp_in = a.sem("mlp_in")
        m.kept = a
        setup_phase(nc, m)
        m.src_i = a.sb("src_i", [T, EC], I32)
        m.dst_pos = a.sb("dst_pos", [T, EC], I32)
        m.dst_local = a.sb("dst_local", [T, EC])
        with ExitStack() as first:
            c = Pool_(nc, first)
            m.hn = c.sb("hn", [T, NT, D])
            m.a = c.sb("a", [T, NT, 3 * D], BF16)
            with ExitStack() as edges:
                d = Pool_(nc, edges)
                m.dst_i = d.sb("dst_i", [T, EC], I32)
                m.src_f = d.sb("src_f", [T, EC])
                m.dst_f = d.sb("dst_f", [T, EC])
                m.src_pos = d.sb("src_pos", [T, EC], I32)
                m.src_local = d.sb("src_local", [T, EC])
                load_keys(nc, m, io["src"], io["dst"])
                with phase(nc) as side:
                    fill_records(nc, m, "fs_", io["recs"], REC, EA, nc.sync, side)
                    fill_records(nc, m, "fd_", io["recs2"], 2, 0, nc.scalar, side)
                    dispatch(nc, m, "ds_", m.src_f[:, :], EC, NT, T, EB, m.src_pos[:, :], m.src_local[:, :],
                             io["src_tile_dram"], m.src_tile[:, :], B, side)
                with phase(nc) as side:
                    node_phase(nc, m, io["x"], io["w1ab"], io["L0_gnn_b1"], io["b_table"], side)
                    scatter_records(nc, m, "ss_", io["recs"], m.src_pos, m.src_local, m.dst_i, io["edge_attr_64"],
                                    side)
                    dispatch(nc, m, "dd_", m.dst_f[:, :], EC, NT, T, PB, m.dst_pos[:, :], m.dst_local[:, :],
                             io["dst_tile_dram"], m.dst_tile[:, :], 2 * B, side)
            m.acc = c.sb("acc", [T, NT, D + 1])
            m.gru = [c.sb("gru_" + name, shape) for name, shape in (
                ("w2", [B, 2, D]), ("w_ih", [B, 2, 3 * D]), ("w_hh", [B, 2, 3 * D]),
                ("b2", [T, D]), ("b_ih", [T, 3 * D]), ("b_hh", [T, 3 * D]))]
            with phase(nc) as side:
                message_phase(nc, m, io["recs"], io["b_table"], io["w1c"], side)
                load_gru(nc, m, io["gnn_w2"], io["L0_gnn_b2"], io["w_ih"], io["L0_gnn_b_ih"], io["w_hh"],
                         io["L0_gnn_b_hh"], side)
            with phase(nc) as side:
                gru_phase(nc, m, side)
                fill_tokens(nc, m, io["tokens"], side)
                scatter_records(nc, m, "sg_", io["recs2"], m.dst_pos, m.dst_local, m.src_i, None, side, 0, EARLY)
        with ExitStack() as moe:
            c = Pool_(nc, moe)
            m.expert = c.sb("expert", [T, 2 * NT])
            m.weight = c.sb("weight", [T, 2 * NT])
            m.slot = c.sb("slot", [T, 2 * NT], I32)
            m.block_expert = c.sb("block_expert", [1, MB], I32)
            m.b1s = c.sb("b1s", [B, NEX * 8])
            m.w1s = c.sb("w1s", [B, NEX * 2, HID])
            m.w2s = c.sb("w2s", [B, NEX * 8, D])
            with ExitStack() as inner:
                d = Pool_(nc, inner)
                m.ln = d.sb("ln", [T, NT, D])
                m.mv = d.sb("mv", [T, NT, 2])
                m.rstd = d.sb("rstd", [T, NT])
                with phase(nc) as side:
                    normed = normalize(nc, m, "l1_", m.ln, side)
                    router_phase(nc, m, io["L0_ffn_Wr"], io["L0_ffn_br"], normed, side)
                    load_experts(nc, m, io["L0_ffn_W1"], io["L0_ffn_W2"], side)
                dispatch(nc, m, "dm_", m.expert[:, :], 2 * NT, NEX, 1, MB, m.slot[:, :], None,
                         io["expert_dram"], m.block_expert[:, :], B)
                with phase(nc) as side:
                    send_tokens(nc, m, io["tokens"], side)
                    shift_biases(nc, m, io["ln_b_cols"], io["b1_cols"], side)
            with phase(nc) as side:
                expert_phase(nc, m, io["tokens"], io["answers"], io["ln_g_cols"], io["b2_row"], side)
                scatter_records(nc, m, "sd_", io["recs2"], m.dst_pos, m.dst_local, m.src_i, None, side, EARLY)
            combine_phase(nc, m, io["answers"])
        m.ln = a.sb("ln2", [T, NT, D])
        m.mlp = [a.sb(name, shape) for name, shape in (
            ("f_gw", [B, 2, NX]),
            ("f_gb", [T, NX]),
            ("f_sw1", [B, 2, H1]),
            ("f_sb1", [B, 2]),
            ("f_sw2", [B, 2, H2]),
            ("f_sb2", [H2, 1]),
            ("f_sw3", [H2, D]),
            ("f_sb3", [T, D]),
            ("f_ew1", [B, NX * 2, X1]),
            ("f_eb1", [X1, NX]),
            ("f_ew2", [X1, NX, X2]),
            ("f_eb2", [X2, NX]),
            ("f_ew3", [X2 + 1, NX, D]))]
        with ExitStack() as gat:
            c = Pool_(nc, gat)
            m.to = c.sb("to", [T, NT])
            m.peak = c.sb("peak", [T, NT])
            m.acc = c.sb("acc2", [T, NT, HC])
            with phase(nc) as side:
                normed = normalize(nc, m, "l2_", m.ln, side)
                attention_rows(nc, m, io["wg"], io["L1_gnn_a_src"], io["L1_gnn_a_dst"], io["table"], normed, side)
            with phase(nc) as side:
                attention_phase(nc, m, io["recs2"], io["table"], io["L1_gnn_bias"], side)
                load_mlp(nc, m, io, side)
        with phase(nc) as side:
            normed = normalize(nc, m, "l3_", m.ln, side)
            mlp_phase(nc, m, io, normed, side)


_AS_GIVEN = ["x", "src", "dst", "edge_attr_64", "L0_gnn_b1", "L0_gnn_b2", "L0_gnn_b_ih", "L0_gnn_b_hh", "L0_ffn_Wr",
             "L0_ffn_br", "L0_ffn_W1", "L0_ffn_W2", "L1_gnn_a_src", "L1_gnn_a_dst", "L1_gnn_bias", "L1_ffn_sW1",
             "L1_ffn_sW2", "L1_ffn_sW3", "L1_ffn_sb3", "L1_ffn_eW1", "L1_ffn_eW2", "L1_ffn_eW3", "L1_ffn_eb3",
             "L1_ffn_gW", "L1_ffn_gb"]
_SCRATCH = [("recs", (EB * B, REC), F32), ("recs2", (PB * 2 * B, 2), F32), ("b_table", (N, D), F32),
            ("src_tile_dram", (4 * B,), I32), ("dst_tile_dram", (4 * B,), I32), ("expert_dram", (4 * B,), I32),
            ("tokens", (MB * B, D), F32), ("answers", (MB * B, D), F32), ("table", (N, HC), F32)]


def kernel(**inputs):
    import numpy as _np
    import concourse.bacc as _bacc
    from concourse import mybir as _mybir
    from concourse.bass_utils import run_bass_kernel_spmd as _run

    nc = _bacc.Bacc("TRN2", target_bir_lowering=False, num_devices=1)
    given = {k: _np.asarray(v) for k, v in inputs.items()}
    arrays = {k: given[k] for k in _AS_GIVEN}
    w1 = given["L0_gnn_W1"]
    arrays["w1ab"] = _np.concatenate([w1[:, :D].T, w1[:, D:2 * D].T], axis=1)
    arrays["w1c"] = w1[:, 2 * D:].T
    arrays["gnn_w2"] = given["L0_gnn_W2"].T
    arrays["w_ih"] = given["L0_gnn_W_ih"].T
    arrays["w_hh"] = given["L0_gnn_W_hh"].T
    arrays["wg"] = given["L1_gnn_W"].T
    arrays["ln_g_cols"] = given["L0_ffn_ln_g"].reshape(NEX * 2, B).T
    arrays["ln_b_cols"] = given["L0_ffn_ln_b"].reshape(NEX * 2, B).T
    arrays["b1_cols"] = given["L0_ffn_b1"].reshape(NEX * 8, B).T
    arrays["b2_row"] = given["L0_ffn_b2"].reshape(NEX * D)
    arrays["sb1_cols"] = given["L1_ffn_sb1"].reshape(2, B).T
    arrays["sb2_cols"] = given["L1_ffn_sb2"].reshape(1, H2).T
    arrays["eb1_cols"] = given["L1_ffn_eb1"].T
    arrays["eb2_cols"] = given["L1_ffn_eb2"].T
    arrays = {"in_" + k: _np.ascontiguousarray(v) for k, v in arrays.items()}
    io = {k[3:]: nc.dram_tensor(k, v.shape, _mybir.dt.from_np(v.dtype), kind="ExternalInput").ap()
          for k, v in arrays.items()}
    for name, shape, dt in _SCRATCH:
        io[name] = nc.dram_tensor("scratch_" + name, shape, dt, kind="Internal").ap()
    io["out"] = nc.dram_tensor("out", (N, D), F32, kind="ExternalOutput").ap()
    build(nc, io)
    r = _run(nc, [arrays], core_ids=[0])
    return r.results[0]["out"]
```
